# Optimizing a Trainium2 kernel written in Bass

```python
import numpy as np
import jax
import jax.numpy as jnp

def _softmax(x, axis=-1):
    return jax.nn.softmax(x, axis=axis)

def _gelu(x):
    return jax.nn.gelu(x, approximate=True)

def _silu(x):
    return jax.nn.silu(x)

def _sigmoid(x):
    return jax.nn.sigmoid(x)

def _layernorm(x, axis=-1, eps=1e-05):
    m = jnp.mean(x, axis=axis, keepdims=True)
    v = jnp.var(x, axis=axis, keepdims=True)
    return (x - m) / jnp.sqrt(v + eps)

def _scatter_add(tgt, idx, src, axis=0):
    return tgt.at[idx].add(src)

def _segment_sum(src, seg, n):
    return jax.ops.segment_sum(src, seg, n)
kernel_name = 'mk_gnn_resnorm_d4_gnn_r8_8ff3f9'

def setup_inputs(seed: int=0):
    np.random.seed(seed)
    _w = jnp.asarray

    def _rec_inputs():
        import jax
        import jax.numpy as jnp
        _gk = jax.random.key(seed)
        x = -0.000202 + 1 * jax.random.normal(jax.random.fold_in(_gk, 1), (12500, 64), jnp.float32)
        _s = jax.random.randint(jax.random.fold_in(_gk, 2), (100000,), 0, 12500, jnp.int32)
        _d = jax.random.randint(jax.random.fold_in(_gk, 3), (100000,), 0, 12500, jnp.int32)
        _loop = jnp.arange(12500, dtype=jnp.int32)
        src = jnp.concatenate([_s, _d, _loop])
        dst = jnp.concatenate([_d, _s, _loop])
        _o = jnp.argsort(dst, stable=True)
        src = src[_o]
        dst = dst[_o]
        edge_attr_16 = 0.000196303 + 1.00016 * jax.random.normal(jax.random.fold_in(_gk, 13), (212500, 16), jnp.float32)
        edge_attr_64 = 0.000103221 + 1.00003 * jax.random.normal(jax.random.fold_in(_gk, 14), (212500, 64), jnp.float32)
        edge_weight1 = 0.00107675 + 0.999702 * jax.random.normal(jax.random.fold_in(_gk, 16), (212500, 1), jnp.float32)
        node_vec1 = jax.random.uniform(jax.random.fold_in(_gk, 17), (12500, 1), jnp.float32, 0.0, 1)
        return (x, src, dst, edge_attr_16, edge_attr_64, edge_weight1, node_vec1)
    x, src, dst, edge_attr_16, edge_attr_64, edge_weight1, node_vec1 = _rec_inputs()

    def _L0_gnn_setup():
        import jax, jax.numpy as jnp
        import numpy as np
        N_NODES = 12500
        N_EDGES = 150000
        D_FEAT = 64
        key = jax.random.key(seed)
        k1, k2, k3 = jax.random.split(key, 3)
        h = jax.random.normal(k1, (N_NODES, D_FEAT), dtype=jnp.float32)
        edge_src = jax.random.randint(k2, (N_EDGES,), 0, N_NODES, dtype=jnp.int32)
        edge_dst = jax.random.randint(k3, (N_EDGES,), 0, N_NODES, dtype=jnp.int32)
        return {'h': h, 'edge_src': edge_src, 'edge_dst': edge_dst}
    _L0_gnn_all = _L0_gnn_setup()
    _L0_gnn_in = {k: v for k, v in _L0_gnn_all.items() if k in ()}
    del _L0_gnn_all

    def _L1_gnn_setup():
        import jax, jax.numpy as jnp
        import numpy as np
        N, E = (12500, 200000)
        IN_DIM, OUT_DIM, EDGE_DIM, H = (64, 64, 16, 4)
        HD = OUT_DIM // H
        NEG_SLOPE = 0.2
        EPS_SOFTMAX = 1e-08
        EPS_LN = 1e-05
        key = jax.random.key(seed)
        ks = jax.random.split(key, 8)
        return {'x': jax.random.normal(ks[0], (N, IN_DIM), jnp.float32), 'edge_index': jax.random.randint(ks[1], (2, E), 0, N, jnp.int64 if jax.config.jax_enable_x64 else jnp.int32), 'edge_attr': jax.random.normal(ks[2], (E, EDGE_DIM), jnp.float32), 'W_node': jax.random.normal(ks[3], (IN_DIM, OUT_DIM), jnp.float32) / np.sqrt(IN_DIM), 'W_edge': jax.random.normal(ks[4], (EDGE_DIM, H), jnp.float32) / np.sqrt(EDGE_DIM), 'attn_src': jax.random.normal(ks[5], (H, HD), jnp.float32), 'attn_dst': jax.random.normal(ks[6], (H, HD), jnp.float32), 'ln_gamma': jnp.ones((OUT_DIM,), jnp.float32), 'ln_beta': jnp.zeros((OUT_DIM,), jnp.float32)}
    _L1_gnn_all = _L1_gnn_setup()
    _L1_gnn_in = {k: v for k, v in _L1_gnn_all.items() if k in ('W_node', 'W_edge', 'attn_src', 'attn_dst', 'ln_gamma', 'ln_beta')}
    del _L1_gnn_all

    def _L2_gnn_setup():
        import jax, jax.numpy as jnp
        import numpy as np
        N_NODES = 12500
        N_EDGES = 200000
        D_IN = 64
        D_HID = 64
        BN_EPS = 1e-05
        key = jax.random.key(seed)
        k1, k2, k3, k4 = jax.random.split(key, 4)
        x = jax.random.normal(k1, (N_NODES, D_IN), dtype=jnp.float32)
        edge_index = jax.random.randint(k2, (2, N_EDGES), 0, N_NODES, dtype=jnp.int64)
        W = jax.random.normal(k3, (D_IN, D_HID), dtype=jnp.float32) * (1.0 / np.sqrt(D_IN))
        b = jax.random.normal(k4, (D_HID,), dtype=jnp.float32) * 0.01
        gamma = jnp.ones((D_HID,), dtype=jnp.float32)
        beta = jnp.zeros((D_HID,), dtype=jnp.float32)
        return {'x': x, 'edge_index': edge_index, 'W': W, 'b': b, 'gamma': gamma, 'beta': beta}
    _L2_gnn_all = _L2_gnn_setup()
    _L2_gnn_in = {k: v for k, v in _L2_gnn_all.items() if k in ('W', 'b', 'gamma', 'beta')}
    del _L2_gnn_all

    def _L3_gnn_setup():
        import jax, jax.numpy as jnp
        import numpy as np
        N_NODES = 6250
        N_EDGES = 100000
        C_IN = 64
        N_HEADS = 4
        HEAD_DIM = 16
        FC = 64
        key = jax.random.key(seed)
        ks = jax.random.split(key, 20)
        d = {}
        d['node_input'] = jax.random.normal(ks[0], (N_NODES, C_IN), jnp.float32)
        d['node_attr'] = jnp.ones((N_NODES, 1), jnp.float32)
        d['edge_src'] = jax.random.randint(ks[1], (N_EDGES,), 0, N_NODES)
        d['edge_dst'] = jax.random.randint(ks[2], (N_EDGES,), 0, N_NODES)
        d['edge_attr'] = jax.random.normal(ks[3], (N_EDGES, 1), jnp.float32)
        d['edge_scalars'] = jax.random.normal(ks[4], (N_EDGES, FC), jnp.float32)
        d['batch'] = jnp.zeros((N_NODES,), jnp.int32)
        s = 1.0 / np.sqrt(C_IN)
        AD = N_HEADS * HEAD_DIM
        d['Wq'] = jax.random.normal(ks[5], (C_IN, AD), jnp.float32) * s
        d['bq'] = jnp.zeros((AD,), jnp.float32)
        d['W_src'] = jax.random.normal(ks[6], (C_IN, C_IN), jnp.float32) * s
        d['b_src'] = jnp.zeros((C_IN,), jnp.float32)
        d['W_dst'] = jax.random.normal(ks[7], (C_IN, C_IN), jnp.float32) * s
        d['W_fc1'] = jax.random.normal(ks[8], (FC, FC), jnp.float32) * (1.0 / np.sqrt(FC))
        d['b_fc1'] = jnp.zeros((FC,), jnp.float32)
        d['W_fc2'] = jax.random.normal(ks[9], (FC, FC), jnp.float32) * (1.0 / np.sqrt(FC))
        d['b_fc2'] = jnp.zeros((FC,), jnp.float32)
        d['W_fc3'] = jax.random.normal(ks[10], (FC, C_IN), jnp.float32) * (1.0 / np.sqrt(FC))
        d['b_fc3'] = jnp.zeros((C_IN,), jnp.float32)
        d['W_kv'] = jax.random.normal(ks[11], (C_IN, 2 * AD), jnp.float32) * s
        d['b_kv'] = jnp.zeros((2 * AD,), jnp.float32)
        d['W_proj'] = jax.random.normal(ks[12], (AD, C_IN), jnp.float32) * (1.0 / np.sqrt(AD))
        d['b_proj'] = jnp.zeros((C_IN,), jnp.float32)
        return d
    _L3_gnn_all = _L3_gnn_setup()
    _L3_gnn_in = {k: v for k, v in _L3_gnn_all.items() if k in ('Wq', 'bq', 'W_src', 'b_src', 'W_dst', 'W_fc1', 'b_fc1', 'W_fc2', 'b_fc2', 'W_fc3', 'b_fc3', 'W_kv', 'b_kv', 'W_proj', 'b_proj')}
    del _L3_gnn_all
    return {'x': x, 'src': src, 'dst': dst, 'edge_attr_16': edge_attr_16, 'edge_attr_64': edge_attr_64, 'edge_weight1': edge_weight1, 'node_vec1': node_vec1, 'L1_gnn_W_node': _L1_gnn_in['W_node'], 'L1_gnn_W_edge': _L1_gnn_in['W_edge'], 'L1_gnn_attn_src': _L1_gnn_in['attn_src'], 'L1_gnn_attn_dst': _L1_gnn_in['attn_dst'], 'L1_gnn_ln_gamma': _L1_gnn_in['ln_gamma'], 'L1_gnn_ln_beta': _L1_gnn_in['ln_beta'], 'L2_gnn_W': _L2_gnn_in['W'], 'L2_gnn_b': _L2_gnn_in['b'], 'L2_gnn_gamma': _L2_gnn_in['gamma'], 'L2_gnn_beta': _L2_gnn_in['beta'], 'L3_gnn_Wq': _L3_gnn_in['Wq'], 'L3_gnn_bq': _L3_gnn_in['bq'], 'L3_gnn_W_src': _L3_gnn_in['W_src'], 'L3_gnn_b_src': _L3_gnn_in['b_src'], 'L3_gnn_W_dst': _L3_gnn_in['W_dst'], 'L3_gnn_W_fc1': _L3_gnn_in['W_fc1'], 'L3_gnn_b_fc1': _L3_gnn_in['b_fc1'], 'L3_gnn_W_fc2': _L3_gnn_in['W_fc2'], 'L3_gnn_b_fc2': _L3_gnn_in['b_fc2'], 'L3_gnn_W_fc3': _L3_gnn_in['W_fc3'], 'L3_gnn_b_fc3': _L3_gnn_in['b_fc3'], 'L3_gnn_W_kv': _L3_gnn_in['W_kv'], 'L3_gnn_b_kv': _L3_gnn_in['b_kv'], 'L3_gnn_W_proj': _L3_gnn_in['W_proj'], 'L3_gnn_b_proj': _L3_gnn_in['b_proj']}

def reference(x, src, dst, edge_attr_16, edge_attr_64, edge_weight1, node_vec1, L1_gnn_W_node, L1_gnn_W_edge, L1_gnn_attn_src, L1_gnn_attn_dst, L1_gnn_ln_gamma, L1_gnn_ln_beta, L2_gnn_W, L2_gnn_b, L2_gnn_gamma, L2_gnn_beta, L3_gnn_Wq, L3_gnn_bq, L3_gnn_W_src, L3_gnn_b_src, L3_gnn_W_dst, L3_gnn_W_fc1, L3_gnn_b_fc1, L3_gnn_W_fc2, L3_gnn_b_fc2, L3_gnn_W_fc3, L3_gnn_b_fc3, L3_gnn_W_kv, L3_gnn_b_kv, L3_gnn_W_proj, L3_gnn_b_proj):
    import jax
    import jax.numpy as jnp

    def _L0_gnn_ref(h, edge_src, edge_dst):
        import jax, jax.numpy as jnp
        import numpy as np
        N_NODES = 12500
        N_EDGES = 150000
        D_FEAT = 64
        'LightGCN propagation: h_out[v] = sum_{(u,v) in E} h[u] / sqrt(deg_out(u)*deg_in(v)).'
        n = h.shape[0]
        ones = jnp.ones(edge_src.shape[0], dtype=h.dtype)
        deg_out = jnp.maximum(jax.ops.segment_sum(ones, edge_src, num_segments=n), 1.0)
        deg_in = jnp.maximum(jax.ops.segment_sum(ones, edge_dst, num_segments=n), 1.0)
        inv_sqrt_out = jax.lax.rsqrt(deg_out)
        inv_sqrt_in = jax.lax.rsqrt(deg_in)
        w = inv_sqrt_out[edge_src] * inv_sqrt_in[edge_dst]
        m = h[edge_src] * w[:, None]
        h_out = jax.ops.segment_sum(m, edge_dst, num_segments=n)
        return h_out

    def _L1_gnn_ref(x, edge_index, edge_attr, W_node, W_edge, attn_src, attn_dst, ln_gamma, ln_beta):
        import jax, jax.numpy as jnp
        import numpy as np
        N, E = (12500, 200000)
        IN_DIM, OUT_DIM, EDGE_DIM, H = (64, 64, 16, 4)
        HD = OUT_DIM // H
        NEG_SLOPE = 0.2
        EPS_SOFTMAX = 1e-08
        EPS_LN = 1e-05
        n = x.shape[0]
        src, dst = (edge_index[0], edge_index[1])
        h = (x @ W_node).reshape(n, H, HD)
        a_src_node = jnp.einsum('nhd,hd->nh', h, attn_src)
        a_dst_node = jnp.einsum('nhd,hd->nh', h, attn_dst)
        e_score = edge_attr @ W_edge
        attn = a_src_node[src] + a_dst_node[dst] + e_score
        attn = jnp.where(attn >= 0, attn, NEG_SLOPE * attn)
        attn_max = jnp.zeros((n, H), attn.dtype).at[dst].max(attn)
        attn = jnp.exp(attn - attn_max[dst])
        attn_sum = jnp.zeros((n, H), attn.dtype).at[dst].add(attn)
        attn = attn / (attn_sum[dst] + EPS_SOFTMAX)
        msg = h[src] * attn[:, :, None]
        out = jnp.zeros((n, H, HD), h.dtype).at[dst].add(msg).reshape(n, OUT_DIM)
        y = out + h.reshape(n, OUT_DIM)
        mu = jnp.mean(y, axis=-1, keepdims=True)
        var = jnp.mean((y - mu) ** 2, axis=-1, keepdims=True)
        return (y - mu) * jax.lax.rsqrt(var + EPS_LN) * ln_gamma + ln_beta

    def _L2_gnn_ref(x, edge_index, W, b, gamma, beta):
        import jax, jax.numpy as jnp
        import numpy as np
        N_NODES = 12500
        N_EDGES = 200000
        D_IN = 64
        D_HID = 64
        BN_EPS = 1e-05
        src = edge_index[0]
        dst = edge_index[1]
        agg = jax.ops.segment_sum(x[src], dst, num_segments=x.shape[0])
        h = (x + agg) @ W + b
        mu = jnp.mean(h, axis=0)
        var = jnp.var(h, axis=0)
        h = gamma * (h - mu) * jax.lax.rsqrt(var + BN_EPS) + beta
        return jax.nn.relu(h)

    def _L3_gnn_ref(node_input, node_attr, edge_src, edge_dst, edge_attr, edge_scalars, batch, Wq, bq, W_src, b_src, W_dst, W_fc1, b_fc1, W_fc2, b_fc2, W_fc3, b_fc3, W_kv, b_kv, W_proj, b_proj):
        import jax, jax.numpy as jnp
        import numpy as np
        N_NODES = 6250
        N_EDGES = 100000
        C_IN = 64
        N_HEADS = 4
        HEAD_DIM = 16
        FC = 64
        N = node_input.shape[0]
        q = (node_input @ Wq + bq).reshape(N, N_HEADS, HEAD_DIM)
        q = q * (1.0 / jnp.sqrt(jnp.float32(HEAD_DIM)))
        msg_src = node_input @ W_src + b_src
        msg_dst = node_input @ W_dst
        kv = msg_src[edge_src] + msg_dst[edge_dst]
        h = jax.nn.silu(edge_scalars @ W_fc1 + b_fc1)
        h = jax.nn.silu(h @ W_fc2 + b_fc2)
        w = h @ W_fc3 + b_fc3
        tp = kv * edge_attr * w
        kv2 = (tp @ W_kv + b_kv).reshape(-1, 2 * N_HEADS, HEAD_DIM)
        k = kv2[:, :N_HEADS]
        v = kv2[:, N_HEADS:]
        alpha = jnp.einsum('ehd,ehd->eh', q[edge_dst], k)
        seg_max = jax.ops.segment_max(alpha, edge_dst, num_segments=N)
        seg_max = jnp.where(jnp.isfinite(seg_max), seg_max, 0.0)
        ex = jnp.exp(alpha - seg_max[edge_dst])
        denom = jax.ops.segment_sum(ex, edge_dst, num_segments=N)
        alpha = ex / (denom[edge_dst] + 1e-16)
        attn = jax.ops.segment_sum(v * alpha[..., None], edge_dst, num_segments=N)
        attn = attn.reshape(N, N_HEADS * HEAD_DIM)
        return attn @ W_proj + b_proj
    edge_index = jnp.stack([src, dst])
    batch0 = jnp.zeros((12500,), jnp.int32)
    x = _layernorm(x + _L0_gnn_ref(x, src, dst), axis=-1)
    x = _layernorm(x + _L1_gnn_ref(x, edge_index, edge_attr_16, L1_gnn_W_node, L1_gnn_W_edge, L1_gnn_attn_src, L1_gnn_attn_dst, L1_gnn_ln_gamma, L1_gnn_ln_beta), axis=-1)
    x = _layernorm(x + _L2_gnn_ref(x, edge_index, L2_gnn_W, L2_gnn_b, L2_gnn_gamma, L2_gnn_beta), axis=-1)
    x = _layernorm(x + _L3_gnn_ref(x, node_vec1, src, dst, edge_weight1, edge_attr_64, batch0, L3_gnn_Wq, L3_gnn_bq, L3_gnn_W_src, L3_gnn_b_src, L3_gnn_W_dst, L3_gnn_W_fc1, L3_gnn_b_fc1, L3_gnn_W_fc2, L3_gnn_b_fc2, L3_gnn_W_fc3, L3_gnn_b_fc3, L3_gnn_W_kv, L3_gnn_b_kv, L3_gnn_W_proj, L3_gnn_b_proj), axis=-1)
    return x

_drawn_inputs = setup_inputs


def setup_inputs(seed=0):
    import zlib

    import numpy as np

    out = dict(_drawn_inputs(seed))
    spreads = {'L1_gnn_ln_gamma': (1.0, 0.2),
     'L1_gnn_ln_beta': (0.0, 0.1),
     'L2_gnn_gamma': (1.0, 0.2),
     'L2_gnn_beta': (0.0, 0.1),
     'L3_gnn_bq': (0.0, 0.481),
     'L3_gnn_b_src': (0.0, 0.5),
     'L3_gnn_b_fc1': (0.0, 0.39),
     'L3_gnn_b_fc2': (0.0, 0.1),
     'L3_gnn_b_fc3': (0.0, 0.1),
     'L3_gnn_b_kv': (0.0, 0.1),
     'L3_gnn_b_proj': (0.0, 0.1)}
    factors = {'L2_gnn_b': 8.0}
    for name, (base, spread) in spreads.items():
        noise = np.random.default_rng([zlib.crc32(name.encode()), seed]).standard_normal(out[name].shape)
        drawn = base * np.exp(spread * noise) if base else spread * noise
        out[name] = jnp.asarray(drawn.astype(out[name].dtype))
    for name, factor in factors.items():
        out[name] = (out[name] * factor).astype(out[name].dtype)
    return out
```

```python
from contextlib import ExitStack

import numpy as np

import concourse.bass as bass
from concourse import mybir

F32 = mybir.dt.float32
BF16 = mybir.dt.bfloat16
I32 = mybir.dt.int32
U32 = mybir.dt.uint32
ALU = mybir.AluOpType
ACT = mybir.ActivationFunctionType
AX = mybir.AxisListType

P = 128
NODES, EDGES, FEAT, HEADS, EDIM = 12500, 212500, 64, 4, 16
HDIM = FEAT // HEADS
BLKS = -(-NODES // P)
NPAD = BLKS * P
STEP = 64
COLS = -(-EDGES // (P * 2 * STEP)) * 2 * STEP
EPAD = COLS * P
CHUNKS = COLS // STEP
PAIRS = BLKS // 2
SROW = FEAT + 2 * HEADS
SUMS = FEAT + HEADS
QROW = 2 * FEAT + HEADS
GRP = 32
GPC = STEP // GRP
HI = NPAD // P
BIG = 1.0e30
LN_EPS = 1e-5
ds = bass.ds


class Memory:

    def __init__(self, nc, stack, tag):
        self.nc, self.stack, self.tag, self.sems = nc, stack, tag, []
        stack.callback(self.clear)

    def clear(self):
        if self.sems:
            self.nc.clear_and_free_semaphores(self.sems)
            self.nc.all_engine_barrier(sem_only=True)

    def sb(self, name, shape, dtype=F32):
        return self.stack.enter_context(self.nc.sbuf_tensor(f"{self.tag}_{name}", shape, dtype))

    def ps(self, name, shape, dtype=F32):
        return self.stack.enter_context(self.nc.psum_tensor(f"{self.tag}_{name}", shape, dtype))

    def sem(self, name):
        self.sems.append(self.nc.alloc_semaphore(f"{self.tag}_{name}"))
        return self.sems[-1]


def stepper(eng, sem, base=0):
    count = [0]

    def step(ins):
        count[0] += 1
        ins.then_inc(sem, 1)
        eng.wait_ge(sem, base + count[0])

    step.count = count
    return step


def bc(ap, n):
    return ap.unsqueeze(len(ap.shape)).to_broadcast([*ap.shape, n])



def onehot_rows(dve, nc, ch, k, hist, made, used):
    s = k % 2
    dve.wait_ge(used, ch * GPC + k + 1)
    cols = ds(ch * STEP + k * GRP, GRP)
    nc.vector.tensor_tensor(hist["oh_hi"][:, s, :, :], hist["iota"][:, 0:HI, :],
                            hist["hi"][:, cols].unsqueeze(1).to_broadcast([P, HI, GRP]), ALU.is_equal)
    nc.vector.tensor_tensor(hist["oh_lo"][:, s, :, :], hist["iota"][:, :, :],
                            hist["lo"][:, cols].unsqueeze(1).to_broadcast([P, P, GRP]), ALU.is_equal).then_inc(made, 1)


def onehot_products(pe, nc, ch, k, hist, made, used):
    s = k % 2
    pe.wait_ge(made, ch * GPC + k + 1)
    for u in range(GRP):
        last = nc.tensor.matmul(hist["count"][0:HI, 0:P], hist["oh_hi"][:, s, :, u], hist["oh_lo"][:, s, :, u],
                                start=False, stop=False, skip_group_check=True)
    last.then_inc(used, 1)


def split_number(step, nc, number, part, hist):
    step(nc.vector.tensor_single_scalar(part[:, :], number, 7, ALU.logical_shift_right))
    step(nc.vector.tensor_copy(hist["hi"][:, :], part[:, :]))
    step(nc.vector.tensor_single_scalar(part[:, :], number, P - 1, ALU.bitwise_and))
    step(nc.vector.tensor_copy(hist["lo"][:, :], part[:, :]))



def setup_phase(nc, io, g, dram):
    with ExitStack() as stack:
        m = Memory(nc, stack, "setup")
        hist = dict(oh_hi=m.sb("oh_hi", [P, 2, HI, GRP], BF16), oh_lo=m.sb("oh_lo", [P, 2, P, GRP], BF16),
                    iota=g["iota"], hi=m.sb("hi", [P, COLS], BF16), lo=m.sb("lo", [P, COLS], BF16),
                    count=m.ps("count", [P, 512]))
        src = m.sb("src", [P, COLS], U32)
        dst = m.sb("dst", [P, COLS], I32)
        before = m.sb("before", [P, 1], I32)
        beforef = m.sb("beforef", [P, 1])
        part = m.sb("part", [P, COLS], U32)
        dstf = m.sb("dstf", [P, COLS])
        first = m.sb("first", [P, COLS])
        number = m.sb("number", [P, 1])
        zero = m.sb("zero", [P, P], BF16)
        counts = m.sb("counts", [P, P])
        deg = m.sb("deg", [P, BLKS])
        root = m.sb("root", [P, BLKS])
        x = m.sb("x", [P, BLKS, FEAT])
        s_src, s_dst, s_x = m.sem("src_in"), m.sem("dst_in"), m.sem("x_in")
        s_const, s_zero, s_dve = m.sem("constants"), m.sem("zeros"), m.sem("dve")
        s_made, s_used, s_open = m.sem("onehots_made"), m.sem("onehots_used"), m.sem("count_open")
        s_all, s_counts, s_deg_out, s_deg_in = m.sem("count_done"), m.sem("counts"), m.sem("deg_out"), m.sem("deg_in")
        s_max, s_root, s_table, s_store = m.sem("deg_max"), m.sem("root"), m.sem("table"), m.sem("stored")
        block = stack.enter_context(nc.Block())

        @block.sync
        def _(sp):
            sp.dma_start(src[:, :], io["src"][:, 0:COLS]).then_inc(s_src, 16)
            sp.dma_start(x[:, :, :], io["x"].rearrange("(p b) f -> p b f", p=P)).then_inc(s_x, 16)
            sp.wait_ge(s_zero, 1)
            sp.dma_start(before[1:P, :], io["dst"][0:P - 1, COLS - 1:COLS],
                         allow_slow_non_contiguous=True).then_inc(s_dst, 16)
            sp.dma_start(dst[:, :], io["dst"]).then_inc(s_dst, 16)
            sp.wait_ge(s_counts, 1)
            sp.dma_start(dram["count_src"].rearrange("(h l) -> h l", l=P), counts[0:HI, :]).then_inc(s_deg_out, 16)
            sp.wait_ge(s_deg_out, 16)
            sp.dma_start(deg[:, :], dram["count_src"].rearrange("(p b) -> p b", p=P)).then_inc(s_deg_in, 16)
            sp.wait_ge(s_table, 1)
            sp.dma_start(dram["table0"].rearrange("(p b) f -> p b f", p=P), x[:, :, :]).then_inc(s_store, 16)
            sp.wait_ge(s_store, 16)

        @block.gpsimd
        def _(pool):
            pool.iota(g["iota"][:, :, :], [[1, P], [0, GRP]], base=0, channel_multiplier=0,
                      allow_small_or_imprecise_dtypes=True).then_inc(s_const, 1)
            pool.iota(g["rownum"][:, :], [[1, P]], base=0, channel_multiplier=0,
                      allow_small_or_imprecise_dtypes=True).then_inc(s_const, 1)
            pool.iota(g["nodenum"][:, :], [[1, BLKS]], base=0, channel_multiplier=BLKS,
                      allow_small_or_imprecise_dtypes=True).then_inc(s_const, 1)
            pool.iota(g["edge0"][:, :], [[1, 1]], base=-1, channel_multiplier=COLS,
                      allow_small_or_imprecise_dtypes=True).then_inc(s_const, 1)
            pool.iota(number[:, :], [[1, 1]], base=0, channel_multiplier=1,
                      allow_small_or_imprecise_dtypes=True).then_inc(s_const, 1)

        @block.vector
        def _(dve):
            step = stepper(dve, s_dve)
            dve.sem_inc(s_used, 2)
            nc.vector.memset(zero[:, :], 0.0)
            nc.vector.memset(before[:, :], -1).then_inc(s_zero, 1)
            nc.vector.memset(g["eps"][:, :], LN_EPS)
            step(nc.vector.memset(g["ones"][:, :], 1.0))
            dve.wait_ge(s_const, 5)
            step(nc.vector.tensor_scalar(g["ident"][:, :], g["rownum"][:, :], number[:, :], None, ALU.is_equal))
            step(nc.vector.tensor_scalar(g["below"][:, :], g["rownum"][:, :], number[:, :], None, ALU.is_gt))
            dve.wait_ge(s_src, 16)
            split_number(step, nc, src[:, :], part, hist)
            with dve.Fori(0, CHUNKS) as ch:
                for k in range(GPC):
                    onehot_rows(dve, nc, ch, k, hist, s_made, s_used)
            dve.wait_ge(s_dst, 32)
            step(nc.vector.tensor_copy(dstf[:, :], dst[:, :]))
            step(nc.vector.tensor_copy(beforef[:, :], before[:, :]))
            step(nc.vector.tensor_tensor(g["keep"][:, 1:COLS], dstf[:, 1:COLS], dstf[:, 0:COLS - 1], ALU.is_equal))
            step(nc.vector.tensor_tensor(g["keep"][:, 0:1], dstf[:, 0:1], beforef[:, :], ALU.is_equal))
            step(nc.vector.tensor_scalar(first[:, :], dstf[:, :], dstf[:, 0:1], None, ALU.is_equal))
            step(nc.vector.reduce_sum(beforef[:, :], first[:, :], axis=AX.X))
            step(nc.vector.tensor_scalar(g["through"][:, :], beforef[:, :], float(COLS), None, ALU.is_equal))
            step(nc.vector.tensor_tensor(g["through"][:, :], g["through"][:, :], g["keep"][:, 0:1], ALU.mult))
            step(nc.vector.tensor_tensor(beforef[:, :], beforef[:, :], g["edge0"][:, :], ALU.add))
            step(nc.vector.tensor_copy(g["fixrow"][:, :], beforef[:, :]))
            step(nc.vector.tensor_copy(g["dst0"][:, :], dstf[:, 0:1]))
            dve.wait_ge(s_all, 1)
            nc.vector.tensor_copy(counts[0:HI, :], hist["count"][0:HI, 0:P]).then_inc(s_counts, 1)
            dve.wait_ge(s_deg_in, 16)
            nc.vector.tensor_scalar(deg[:, :], deg[:, :], 1.0, None, ALU.max).then_inc(s_max, 1)
            dve.wait_ge(s_root, 1)
            step(nc.vector.reciprocal(root[:, :], root[:, :]))
            dve.wait_ge(s_x, 16)
            nc.vector.tensor_tensor(x[:, :, :], x[:, :, :], bc(root[:, :], FEAT), ALU.mult).then_inc(s_table, 1)

        @block.scalar
        def _(act):
            act.wait_ge(s_max, 1)
            nc.scalar.activation(root[:, :], deg[:, :], ACT.Sqrt).then_inc(s_root, 1)

        @block.tensor
        def _(pe):
            pe.wait_ge(s_zero, 1)
            nc.tensor.matmul(hist["count"][0:HI, 0:P], zero[:, 0:HI], zero[:, :], start=True, stop=False,
                             skip_group_check=True)
            with pe.Fori(0, CHUNKS) as ch:
                for k in range(GPC):
                    onehot_products(pe, nc, ch, k, hist, s_made, s_used)
            nc.tensor.matmul(hist["count"][0:HI, 0:P], zero[:, 0:HI], zero[:, :], start=False, stop=True,
                             skip_group_check=True).then_inc(s_all, 1)



def gather_chunk(pool, nc, slot, table, idx, rows, width, sem):
    for u in range(STEP):
        pool.indirect_dma_start(out=rows[:, slot, u, 0:width], out_offset=None, in_=table,
                                in_offset=bass.IndirectOffsetOnAxis(ap=idx[:, slot, u:u + 1], axis=0)
                                ).then_inc(sem, 16)


def sum_phase(nc, io, g, dram, tag, table, extra):
    with ExitStack() as stack:
        m = Memory(nc, stack, tag)
        idx = m.sb("idx", [P, 2, STEP], U32)
        rows = m.sb("rows", [P, 2, STEP, FEAT])
        run = m.sb("run", [P, 2, STEP + 1, FEAT])
        s_idx = [m.sem(f"idx{h}") for h in range(2)]
        s_rows = [m.sem(f"rows{h}") for h in range(2)]
        s_out = [m.sem(f"out{h}") for h in range(2)]
        s_scan, s_carry, s_pass = m.sem("scanned"), m.sem("carried"), m.sem("passed")
        work = extra(nc, m, io, g, dram)
        block = stack.enter_context(nc.Block())
        store = dram["run_sum"].rearrange("(p j) f -> p j f", p=P)
        SC = FEAT // 8

        @block.sync
        def _(sp):
            for h in range(2):
                sp.sem_inc(s_out[h], 16)
                sp.dma_start(idx[:, h, :], io["src"][:, h * STEP:(h + 1) * STEP]).then_inc(s_idx[h], 16)
            with sp.Fori(0, CHUNKS // 2) as c:
                for h in range(2):
                    ch = 2 * c + h
                    sp.wait_ge(s_scan, (ch + 3) * SC)
                    sp.dma_start(store[:, ds(ch * STEP, STEP), :], run[:, h, 1:STEP + 1, :]).then_inc(s_out[h], 16)
                    sp.dma_start(idx[:, h, :], io["src"][:, ds((ch + 2) * STEP, STEP)]).then_inc(s_idx[h], 16)
            for h in range(2):
                sp.wait_ge(s_out[h], 16 + 16 * (CHUNKS // 2))
                sp.wait_ge(s_idx[h], 16 + 16 * (CHUNKS // 2))

        @block.gpsimd
        def _(pool):
            with pool.Fori(0, CHUNKS // 2) as c:
                for h in range(2):
                    pool.wait_ge(s_idx[h], (c + 1) * 16)
                    pool.sem_inc(s_pass, 1)
                    pool.wait_ge(s_scan, (2 * c + h + 1) * SC)
                    pool.sem_inc(s_pass, 1)
                    gather_chunk(pool, nc, h, table, idx, rows, FEAT, s_rows[h])

        @block.vector
        def _(dve):
            dve.sem_inc(s_scan, 2 * SC)
            nc.vector.memset(run[:, 1, STEP, :], 0.0).then_inc(s_carry, 1)
            work["dve_first"](dve)
            with dve.Fori(0, CHUNKS // 2) as c:
                for h in range(2):
                    ch = 2 * c + h
                    work["dve"](dve, ch)
                    dve.wait_ge(s_out[h], (c + 1) * 16)
                    dve.wait_ge(s_scan, (ch + 2) * SC)
                    dve.wait_ge(s_carry, ch + 1)
                    nc.vector.tensor_copy(run[:, h, 0, :], run[:, 1 - h, STEP, :]).then_inc(s_carry, 1)
                    dve.wait_ge(s_carry, ch + 2)
                    dve.wait_ge(s_rows[h], (c + 1) * 16 * STEP)
                    dve.sem_inc(s_pass, 1)
                    with dve.Fori(0, SC) as k:
                        for u in range(8):
                            f = k * 8 + u
                            last = scan(nc, run[:, h, :, :], rows[:, h, :, :], g["keep"][:, ds(ch * STEP, STEP)],
                                        f, FEAT, FEAT, ALU.mult, ALU.add)
                        last.then_inc(s_scan, 1)
            work["dve_last"](dve)

        @block.scalar
        def _(act):
            work["act"](act)

        @block.tensor
        def _(pe):
            work["pe"](pe)


def scan(nc, run, data, keep, f, rw, dw, op0, op1, df=None):
    flat = run.rearrange("p j f -> p (j f)")
    dflat = data.rearrange("p j f -> p (j f)")
    df = f if df is None else df
    return nc.vector.tensor_tensor_scan(out=flat[:, ds(f + rw, STEP, rw)], data0=keep,
                                        data1=dflat[:, ds(df, STEP, dw)], initial=flat[:, ds(f, 1)],
                                        op0=op0, op1=op1)


def no_extra(nc, m, io, g, dram):
    return dict(dve_first=lambda dve: None, dve=lambda dve, ch: None, dve_last=lambda dve: None,
                act=lambda act: None, pe=lambda pe: None)


def first_extra(nc, m, io, g, dram):
    hist = dict(oh_hi=m.sb("oh_hi", [P, 2, HI, GRP], BF16), oh_lo=m.sb("oh_lo", [P, 2, P, GRP], BF16),
                iota=g["iota"], hi=m.sb("hi", [P, COLS], BF16), lo=m.sb("lo", [P, COLS], BF16), count=m.ps("count", [P, 512]))
    dst = m.sb("dst", [P, COLS], I32)
    part = m.sb("part", [P, COLS], I32)
    zero = m.sb("zero", [P, P], BF16)
    zeros = m.sb("zeros", [P, STEP, QROW])
    counts = m.sb("counts", [P, P])
    s_dst, s_dve, s_zero, s_zeros = m.sem("dst_in"), m.sem("dve"), m.sem("zero"), m.sem("zeroed")
    s_made, s_used, s_all, s_counts = m.sem("onehots_made"), m.sem("onehots_used"), m.sem("count_done"), m.sem("counts")
    s_store = m.sem("counts_out")

    def dve_first(dve):
        step = stepper(dve, s_dve)
        dve.sem_inc(s_used, 2)
        nc.vector.memset(zero[:, :], 0.0).then_inc(s_zero, 1)
        nc.vector.memset(zeros[:, :, :], 0.0).then_inc(s_zero, 1)
        dve.wait_ge(s_dst, 16)
        split_number(step, nc, dst[:, :], part, hist)

    def dve_chunk(dve, ch):
        for k in range(GPC):
            onehot_rows(dve, nc, ch, k, hist, s_made, s_used)

    def dve_last(dve):
        dve.wait_ge(s_all, 1)
        nc.vector.tensor_copy(counts[0:HI, :], hist["count"][0:HI, 0:P]).then_inc(s_counts, 1)

    def act(act):
        act.dma_start(dst[:, :], io["dst"]).then_inc(s_dst, 16)
        act.wait_ge(s_zero, 2)
        zero_row = zeros[:, :, :].rearrange("p j f -> p (j f)").unsqueeze(1)
        act.dma_start(dram["at_dst1"][0:EPAD, :].rearrange("(p c j) f -> p c (j f)", p=P, j=STEP),
                      zero_row[:, :, 0:STEP * HEADS].to_broadcast([P, CHUNKS, STEP * HEADS])
                      ).then_inc(s_zeros, 16)
        with act.Fori(0, CHUNKS) as ch:
            act.wait_ge(s_used, (ch + 1) * GPC + 2)
            act.dma_start(dram["at_dst3"][0:EPAD, :].rearrange("(p j) f -> p j f", p=P)[:, ds(ch * STEP, STEP), :],
                          zeros[:, :, :]).then_inc(s_zeros, 16)
        act.wait_ge(s_counts, 1)
        act.dma_start(dram["count_dst"].rearrange("(h l) -> h l", l=P), counts[0:HI, :]).then_inc(s_store, 16)
        act.wait_ge(s_store, 16)
        act.wait_ge(s_zeros, 16 * (CHUNKS + 1))

    def pe(pe):
        pe.wait_ge(s_zero, 1)
        nc.tensor.matmul(hist["count"][0:HI, 0:P], zero[:, 0:HI], zero[:, :], start=True, stop=False,
                         skip_group_check=True)
        with pe.Fori(0, CHUNKS) as ch:
            for k in range(GPC):
                onehot_products(pe, nc, ch, k, hist, s_made, s_used)
        nc.tensor.matmul(hist["count"][0:HI, 0:P], zero[:, 0:HI], zero[:, :], start=False, stop=True,
                         skip_group_check=True).then_inc(s_all, 1)

    return dict(dve_first=dve_first, dve=dve_chunk, dve_last=dve_last, act=act, pe=pe)



def segments_phase(nc, io, g, dram):
    with ExitStack() as stack:
        m = Memory(nc, stack, "segments")
        deg = m.sb("deg", [P, BLKS])
        upto = m.sb("upto", [P, BLKS])
        total = m.ps("total", [P, 512])
        one = m.sb("one", [P, BLKS])
        t = m.sb("t", [P, BLKS])
        s_deg, s_dve, s_pe, s_act = m.sem("deg_in"), m.sem("dve"), m.sem("pe"), m.sem("act")
        block = stack.enter_context(nc.Block())

        @block.sync
        def _(sp):
            sp.dma_start(deg[:, :], dram["count_dst"].rearrange("(p b) -> p b", p=P)).then_inc(s_deg, 16)

        @block.gpsimd
        def _(pool):
            pass

        @block.vector
        def _(dve):
            step = stepper(dve, s_dve)
            step(nc.vector.memset(one[:, :], 1.0))
            dve.wait_ge(s_deg, 16)
            step(nc.vector.tensor_tensor_scan(out=upto[:, :], data0=one[:, :], data1=deg[:, :], initial=0.0,
                                              op0=ALU.mult, op1=ALU.add))
            dve.wait_ge(s_pe, 1)
            step(nc.vector.tensor_tensor(upto[:, :], upto[:, :], total[:, 0:1].to_broadcast([P, BLKS]), ALU.add))
            step(nc.vector.tensor_scalar(t[:, :], upto[:, :], -1.0, 0.0, ALU.add, ALU.max))
            step(nc.vector.tensor_copy(g["lastrow"][:, :], t[:, :]))
            step(nc.vector.tensor_scalar(g["has"][:, :], deg[:, :], 1.0, None, ALU.min))
            step(nc.vector.tensor_tensor(upto[:, :], upto[:, :], deg[:, :], ALU.subtract))
            step(nc.vector.tensor_tensor(upto[:, :], upto[:, :], g["has"][:, :], ALU.mult))
            step(nc.vector.tensor_scalar(t[:, :], g["nodenum"][:, :], float(EPAD), None, ALU.add))
            step(nc.vector.tensor_scalar(one[:, :], g["has"][:, :], -1.0, 1.0, ALU.mult, ALU.add))
            step(nc.vector.tensor_tensor(t[:, :], t[:, :], one[:, :], ALU.mult))
            step(nc.vector.tensor_tensor(t[:, :], t[:, :], upto[:, :], ALU.add))
            step(nc.vector.tensor_copy(g["firstrow"][:, :], t[:, :]))
            step(nc.vector.tensor_scalar(deg[:, :], deg[:, :], 1.0, None, ALU.max))
            dve.wait_ge(s_act, 1)
            step(nc.vector.reciprocal(g["root_in"][:, :], g["root_in"][:, :]))
            step(nc.vector.tensor_tensor(g["root_in"][:, :], g["root_in"][:, :], g["has"][:, :], ALU.mult))

        @block.scalar
        def _(act):
            act.wait_ge(s_dve, 14)
            nc.scalar.activation(g["root_in"][:, :], deg[:, :], ACT.Sqrt).then_inc(s_act, 1)

        @block.tensor
        def _(pe):
            pe.wait_ge(s_dve, 2)
            nc.tensor.matmul(total[:, 0:1], g["below"][:, :], upto[:, BLKS - 1:BLKS],
                             start=True, stop=True).then_inc(s_pe, 1)



def carry_phase(nc, g, dram, tag, softmax):
    table = dram["run_softmax" if softmax else "run_sum"]
    width = SROW if softmax else FEAT
    sums = SUMS if softmax else FEAT
    with ExitStack() as stack:
        m = Memory(nc, stack, tag)
        end = m.sb("end", [P, width])
        row = m.sb("row", [P, width])
        both = m.sb("both", [P, 3, sums])
        flip = m.sb("flip", [sums, 3, P])
        state = m.sb("state", [sums, P + 1])
        peak = m.sb("peak", [sums, P + 1])
        fac = m.sb("fac", [sums, 2, P])
        back = m.sb("back", [P, 2, sums])
        rpk = m.sb("rpk", [P, sums])
        efac = m.sb("efac", [P, 2, sums])
        ps = m.ps("ps", [P, 512])
        s_end, s_row, s_dve, s_pe, s_act, s_fixed = (m.sem("end_in"), m.sem("row_in"), m.sem("dve"), m.sem("pe"),
                                                     m.sem("act"), m.sem("fixed"))
        s_turned, s_ready, s_exp, s_mend = m.sem("turned"), m.sem("ready"), m.sem("exp"), m.sem("mend")
        block = stack.enter_context(nc.Block())
        np_ = 3 if softmax else 2
        planes = [0, 1, 2] if softmax else [0, 2]

        def widen(step, out, maxima):
            step(nc.vector.tensor_copy(out[:, 0:FEAT].rearrange("p (h d) -> p h d", d=HDIM), bc(maxima, HDIM)))
            step(nc.vector.tensor_copy(out[:, FEAT:SUMS], maxima))

        @block.sync
        def _(sp):
            sp.dma_start(end[:, :], table.rearrange("(p j) f -> p j f", p=P)[:, COLS - 1, :]).then_inc(s_end, 16)

        @block.gpsimd
        def _(pool):
            pool.indirect_dma_start(out=row[:, :], out_offset=None, in_=table[:, :],
                                    in_offset=bass.IndirectOffsetOnAxis(ap=g["fixrow"][:, :], axis=0)
                                    ).then_inc(s_row, 16)
            pool.wait_ge(s_mend, 1)
            pool.indirect_dma_start(out=table[:, :], out_offset=bass.IndirectOffsetOnAxis(ap=g["fixrow"][:, :], axis=0),
                                    in_=row[:, :], in_offset=None).then_inc(s_fixed, 16)
            pool.wait_ge(s_fixed, 16)

        @block.vector
        def _(dve):
            step = stepper(dve, s_dve)
            step(nc.vector.memset(state[:, :], 0.0))
            step(nc.vector.memset(peak[:, :], 0.0))
            step(nc.vector.tensor_copy(both[:, 2, :], g["through"][:, :].to_broadcast([P, sums])))
            dve.wait_ge(s_end, 16)
            step(nc.vector.tensor_copy(both[:, 0, :], end[:, 0:sums]))
            if softmax:
                widen(step, both[:, 1, :], end[:, SUMS:SROW])
            nc.vector.tensor_copy(rpk[:, 0:1], both[:, 0, 0:1]).then_inc(s_ready, 1)
            dve.wait_ge(s_turned, 1)
            step(nc.vector.tensor_copy(flip[:, 0:np_, :], ps[0:sums, 0:np_ * P].rearrange("f (n p) -> f n p", n=np_)))
            through = flip[:, np_ - 1, :]
            if softmax:
                step(nc.vector.tensor_scalar(fac[:, 0, :], through, BIG, -BIG, ALU.mult, ALU.add))
                step(nc.vector.tensor_tensor_scan(out=peak[:, 1:P + 1], data0=fac[:, 0, :], data1=flip[:, 1, :],
                                                  initial=0.0, op0=ALU.add, op1=ALU.max))
                step(nc.vector.tensor_tensor(fac[:, 0, :], peak[:, 0:P], peak[:, 1:P + 1], ALU.subtract))
                step(nc.vector.tensor_scalar(fac[:, 0, :], fac[:, 0, :], 0.0, None, ALU.min))
                step(nc.vector.tensor_tensor(fac[:, 1, :], flip[:, 1, :], peak[:, 1:P + 1], ALU.subtract))
                nc.vector.tensor_scalar(fac[:, 1, :], fac[:, 1, :], 0.0, None, ALU.min).then_inc(s_exp, 1)
                dve.wait_ge(s_act, 1)
                step(nc.vector.tensor_tensor(fac[:, 0, :], fac[:, 0, :], through, ALU.mult))
                step(nc.vector.tensor_tensor(fac[:, 1, :], fac[:, 1, :], flip[:, 0, :], ALU.mult))
                step(nc.vector.tensor_tensor_scan(out=state[:, 1:P + 1], data0=fac[:, 0, :], data1=fac[:, 1, :],
                                                  initial=0.0, op0=ALU.mult, op1=ALU.add))
            else:
                step(nc.vector.tensor_tensor_scan(out=state[:, 1:P + 1], data0=through, data1=flip[:, 0, :],
                                                  initial=0.0, op0=ALU.mult, op1=ALU.add))
            nc.vector.tensor_copy(rpk[:, 0:1], both[:, 0, 0:1]).then_inc(s_ready, 1)
            dve.wait_ge(s_turned, 2)
            dve.wait_ge(s_row, 16)
            if softmax:
                step(nc.vector.tensor_copy(back[:, :, :], ps[:, 0:2 * sums].rearrange("p (n f) -> p n f", n=2)))
                widen(step, rpk, row[:, SUMS:SROW])
                step(nc.vector.tensor_scalar(end[:, 0:1], g["keep"][:, 0:1], BIG, -BIG, ALU.mult, ALU.add))
                step(nc.vector.tensor_scalar(back[:, 1, :], back[:, 1, :], end[:, 0:1], None, ALU.add))
                step(nc.vector.tensor_tensor(efac[:, 1, :], back[:, 1, :], rpk[:, :], ALU.max))
                step(nc.vector.tensor_tensor(efac[:, 0, :], rpk[:, :], efac[:, 1, :], ALU.subtract))
                nc.vector.tensor_tensor(efac[:, 1, :], back[:, 1, :], efac[:, 1, :], ALU.subtract).then_inc(s_exp, 1)
                dve.wait_ge(s_act, 2)
                step(nc.vector.tensor_tensor(row[:, 0:sums], row[:, 0:sums], efac[:, 0, :], ALU.mult))
                step(nc.vector.tensor_tensor(back[:, 0, :], back[:, 0, :], efac[:, 1, :], ALU.mult))
                nc.vector.tensor_tensor(row[:, 0:sums], row[:, 0:sums], back[:, 0, :], ALU.add).then_inc(s_mend, 1)
            else:
                nc.vector.scalar_tensor_tensor(out=row[:, :], in0=ps[:, 0:FEAT], scalar=g["keep"][:, 0:1],
                                               in1=row[:, :], op0=ALU.mult, op1=ALU.add).then_inc(s_mend, 1)

        @block.scalar
        def _(act):
            if softmax:
                act.wait_ge(s_exp, 1)
                nc.scalar.activation(fac[:, :, :], fac[:, :, :], ACT.Exp).then_inc(s_act, 1)
                act.wait_ge(s_exp, 2)
                nc.scalar.activation(efac[:, :, :], efac[:, :, :], ACT.Exp).then_inc(s_act, 1)

        @block.tensor
        def _(pe):
            pe.wait_ge(s_ready, 1)
            for n, plane in enumerate(planes):
                last = nc.tensor.transpose(ps[0:sums, n * P:(n + 1) * P], both[:, plane, :], g["ident"][:, :])
            last.then_inc(s_turned, 1)
            pe.wait_ge(s_ready, 2)
            for n, what in enumerate([state, peak] if softmax else [state]):
                last = nc.tensor.transpose(ps[:, n * sums:(n + 1) * sums], what[:, 0:P], g["ident"][0:sums, 0:sums])
            last.then_inc(s_turned, 1)



def gather_nodes(pool, g, table, acc, sem):
    for b in range(BLKS):
        pool.indirect_dma_start(out=acc[:, b, :], out_offset=None, in_=table[:, :],
                                in_offset=bass.IndirectOffsetOnAxis(ap=g["lastrow"][:, b:b + 1], axis=0)
                                ).then_inc(sem, 16)


def scatter_nodes(pool, g, table, rows, sem):
    for b in range(BLKS):
        pool.indirect_dma_start(out=table[:, :], out_offset=bass.IndirectOffsetOnAxis(ap=g["firstrow"][:, b:b + 1], axis=0),
                                in_=rows[:, b, :], in_offset=None).then_inc(sem, 16)


def norm_dve(dve, nc, step, x, sq, stat, s_var, s_std, turn):
    mean, var = stat[:, 0, :], stat[:, 1, :]
    step(nc.vector.reduce_sum(mean, x, axis=AX.X))
    step(nc.vector.tensor_scalar(mean, mean, 1.0 / FEAT, None, ALU.mult))
    step(nc.vector.tensor_tensor(x, x, bc(mean, FEAT), ALU.subtract))
    step(nc.vector.tensor_tensor(sq, x, x, ALU.mult))
    nc.vector.reduce_sum(var, sq, axis=AX.X).then_inc(s_var, 1)
    dve.wait_ge(s_std, turn)
    step(nc.vector.reciprocal(var, var))
    step(nc.vector.tensor_tensor(x, x, bc(var, FEAT), ALU.mult))


def norm_act(act, nc, g, stat, s_var, s_std, turn):
    act.wait_ge(s_var, turn)
    nc.scalar.activation(stat[:, 1, :], stat[:, 1, :], ACT.Sqrt, scale=1.0 / FEAT, bias=g["eps"][:, :]).then_inc(s_std, 1)


class NodeProduct:

    def __init__(self, nc, m, g, x, w, width, finish):
        self.nc, self.g, self.x, self.w, self.width, self.finish = nc, g, x, w, width, finish
        self.turned = m.ps("turned", [P, 2, 512])
        self.xt = m.sb("xt", [P, 2, 4, P])
        self.out = m.ps("out", [P, 4, 512])
        self.s_turn, self.s_xt, self.s_mm, self.s_done = (m.sem("turn"), m.sem("xt"), m.sem("mm"), m.sem("done"))
        self.groups = [(k, min(4, PAIRS - k)) for k in range(0, PAIRS, 4)]

    def turn(self, pe, n):
        k0, count = self.groups[n]
        if n >= 2:
            pe.wait_ge(self.s_xt, n - 1)
        for k in range(count):
            last = self.nc.tensor.transpose(self.turned[:, n % 2, k * P:(k + 1) * P],
                                            self.x[:, 2 * (k0 + k):2 * (k0 + k) + 2, :].rearrange("p b f -> p (b f)"),
                                            self.g["ident"][:, :])
        last.then_inc(self.s_turn, 1)

    def pe(self, pe):
        self.turn(pe, 0)
        for n, (k0, count) in enumerate(self.groups):
            if n + 1 < len(self.groups):
                self.turn(pe, n + 1)
            pe.wait_ge(self.s_xt, n + 1)
            for k in range(count):
                pair = k0 + k
                if pair >= 4:
                    pe.wait_ge(self.s_done, pair - 3)
                self.nc.tensor.matmul(self.out[:, pair % 4, 0:2 * self.width], self.xt[:, n % 2, k, :],
                                      self.w[:, :], start=True, stop=True).then_inc(self.s_mm, 1)

    def act(self, act):
        for n, (k0, count) in enumerate(self.groups):
            act.wait_ge(self.s_turn, n + 1)
            if n >= 2:
                act.wait_ge(self.s_mm, self.groups[n - 1][0])
            self.nc.scalar.activation(self.xt[:, n % 2, 0:count, :],
                                      self.turned[:, n % 2, 0:count * P].rearrange("p (k n) -> p k n", k=count),
                                      ACT.Copy).then_inc(self.s_xt, 1)

    def dve(self, dve):
        for pair in range(PAIRS):
            dve.wait_ge(self.s_mm, pair + 1)
            self.finish(pair, self.out[:, pair % 4, 0:2 * self.width].rearrange("p (b f) -> p b f", b=2)
                        ).then_inc(self.s_done, 1)


def node_view(ap):
    return ap.rearrange("(p b) f -> p b f", p=P)



ATT = FEAT + 2 * HEADS


def first_nodes_phase(nc, io, g, dram):
    with ExitStack() as stack:
        m = Memory(nc, stack, "nodes1")
        x = m.sb("x", [P, BLKS, FEAT])
        acc = m.sb("acc", [P, BLKS, FEAT])
        stat = m.sb("stat", [P, 2, BLKS])
        tab = m.sb("tab", [P, BLKS, ATT])
        at = m.sb("at", [P, BLKS, HEADS])
        w = m.sb("w", [P, 2 * ATT])
        wt = m.sb("wt", [FEAT, P])
        attn = m.sb("attn", [FEAT, 2 * HEADS])
        small = m.ps("small", [P, 512])
        s_w, s_x, s_acc, s_dve, s_var, s_std = (m.sem("w_in"), m.sem("x_in"), m.sem("acc_in"), m.sem("dve"),
                                                m.sem("var"), m.sem("std"))
        s_small, s_ready, s_tab, s_at, s_out, s_spread = (m.sem("small"), m.sem("ready"), m.sem("tab"), m.sem("at"),
                                                          m.sem("out"), m.sem("spread"))
        prod = NodeProduct(nc, m, g, x, w, ATT,
                           lambda k, ps: nc.vector.tensor_copy(tab[:, 2 * k:2 * k + 2, :], ps))
        block = stack.enter_context(nc.Block())

        @block.sync
        def _(sp):
            sp.dma_start(w[:, :], io["w_node"]).then_inc(s_w, 16)
            sp.dma_start(wt[:, :], io["w_node_t"]).then_inc(s_w, 16)
            sp.dma_start(attn[:, :], io["attn"]).then_inc(s_w, 16)
            sp.dma_start(x[:, :, :], node_view(io["x"])).then_inc(s_x, 16)
            sp.wait_ge(s_ready, 1)
            sp.dma_start(node_view(dram["x1"]), x[:, :, :]).then_inc(s_out, 16)
            sp.wait_ge(s_tab, 1)
            sp.dma_start(node_view(dram["table1"]), tab[:, :, :]).then_inc(s_out, 16)
            sp.wait_ge(s_out, 32)

        @block.gpsimd
        def _(pool):
            gather_nodes(pool, g, dram["run_sum"], acc, s_acc)
            pool.wait_ge(s_at, 1)
            scatter_nodes(pool, g, dram["at_dst1"], at, s_spread)
            pool.wait_ge(s_spread, 16 * BLKS)

        @block.vector
        def _(dve):
            step = stepper(dve, s_dve)
            dve.wait_ge(s_w, 48)
            dve.wait_ge(s_small, 1)
            step(nc.vector.tensor_copy(w[0:FEAT, FEAT:ATT], small[0:FEAT, 0:2 * HEADS]))
            step(nc.vector.tensor_copy(w[FEAT:P, ATT + FEAT:2 * ATT], small[FEAT:P, 0:2 * HEADS]))
            dve.wait_ge(s_x, 16)
            dve.wait_ge(s_acc, 16 * BLKS)
            step(nc.vector.tensor_tensor(acc[:, :, :], acc[:, :, :], bc(g["root_in"][:, :], FEAT), ALU.mult))
            step(nc.vector.tensor_tensor(x[:, :, :], x[:, :, :], acc[:, :, :], ALU.add))
            norm_dve(dve, nc, step, x[:, :, :], acc[:, :, :], stat, s_var, s_std, 1)
            nc.vector.tensor_copy(stat[:, 0, 0:1], stat[:, 1, 0:1]).then_inc(s_ready, 1)
            prod.dve(dve)
            dve.wait_ge(prod.s_done, PAIRS)
            nc.vector.tensor_copy(at[:, :, :], tab[:, :, FEAT + HEADS:ATT]).then_inc(s_at, 1)
            nc.vector.tensor_copy(stat[:, 0, 0:1], stat[:, 1, 0:1]).then_inc(s_tab, 1)

        @block.scalar
        def _(act):
            norm_act(act, nc, g, stat, s_var, s_std, 1)
            prod.act(act)

        @block.tensor
        def _(pe):
            pe.wait_ge(s_w, 48)
            nc.tensor.matmul(small[:, 0:2 * HEADS], wt[:, :], attn[:, :], start=True, stop=True).then_inc(s_small, 1)
            pe.wait_ge(s_ready, 1)
            prod.pe(pe)



def every_chunk(eng, body):
    with eng.Fori(0, CHUNKS // 2 - 1) as c:
        for h in range(2):
            body(c, h, False)
    for h in range(2):
        body(CHUNKS // 2 - 1, h, True)


def softmax_scans(dve, nc, run, fall, grow, data, s_scan):
    for head in range(HEADS):
        factor = fall.rearrange("p j h -> p (j h)")[:, ds(head, STEP, HEADS)]
        with dve.Fori(0, 2) as k:
            for u in range(HDIM // 2):
                scan(nc, run, data, factor, head * HDIM + k * (HDIM // 2) + u, SROW, data.shape[2],
                     ALU.mult, ALU.add)
        last = scan(nc, run, grow, factor, FEAT + head, SROW, HEADS, ALU.mult, ALU.add, df=head)
    last.then_inc(s_scan, 1)


def attention_phase(nc, io, g, dram):
    with ExitStack() as stack:
        m = Memory(nc, stack, "edges2")
        idx = m.sb("idx", [P, 2, STEP], U32)
        rows = m.sb("rows", [P, 2, STEP, ATT])
        run = m.sb("run", [P, 2, STEP + 1, SROW])
        at = m.sb("at", [P, 2, STEP + 1, HEADS])
        start = m.sb("start", [P, ATT])
        attr = m.sb("attr", [P, 2, STEP // 8, P])
        w_edge = m.sb("w_edge", [P, 8 * HEADS])
        delta = m.sb("delta", [P, 2, STEP, HEADS])
        score = m.ps("score", [P, 2, 512])
        s_idx, s_rows, s_out, s_attr, s_at = ([m.sem(f"{n}{h}") for h in range(2)]
                                              for n in ("idx", "rows", "out", "attr", "at"))
        s_start, s_w, s_scan, s_dve, s_pass = m.sem("start"), m.sem("w"), m.sem("scanned"), m.sem("dve"), m.sem("passed")
        s_score, s_read, s_exp, s_expd = m.sem("score"), m.sem("score_read"), m.sem("to_exp"), m.sem("exp_done")
        block = stack.enter_context(nc.Block())
        store = dram["run_softmax"].rearrange("(p j) f -> p j f", p=P)
        spread = dram["at_dst1"][0:EPAD, :].rearrange("(p j) f -> p j f", p=P)
        STEPS = 11

        @block.sync
        def _(sp):
            sp.dma_start(w_edge[:, :], io["w_edge"]).then_inc(s_w, 16)
            for h in range(2):
                sp.sem_inc(s_out[h], 16)
                sp.dma_start(idx[:, h, :], io["src"][:, h * STEP:(h + 1) * STEP]).then_inc(s_idx[h], 16)
                sp.dma_start(attr[:, h, :, :], io["e16"][:, h * 8:(h + 1) * 8, :]).then_inc(s_attr[h], 16)

            def chunk(c, h, last):
                ch = 2 * c + h
                sp.wait_ge(s_scan, ch + 3)
                sp.dma_start(store[:, ds(ch * STEP, STEP), :], run[:, h, 1:STEP + 1, :]).then_inc(s_out[h], 16)
                if not last:
                    sp.dma_start(idx[:, h, :], io["src"][:, ds((ch + 2) * STEP, STEP)]).then_inc(s_idx[h], 16)
                    sp.dma_start(attr[:, h, :, :], io["e16"][:, ds((ch + 2) * 8, 8), :]).then_inc(s_attr[h], 16)

            every_chunk(sp, chunk)
            for h in range(2):
                sp.wait_ge(s_out[h], 16 + 16 * (CHUNKS // 2))

        @block.gpsimd
        def _(pool):
            pool.indirect_dma_start(out=start[:, :], out_offset=None, in_=dram["table1"],
                                    in_offset=bass.IndirectOffsetOnAxis(ap=g["dst0"][:, :], axis=0)
                                    ).then_inc(s_start, 16)
            with pool.Fori(0, CHUNKS // 2) as c:
                for h in range(2):
                    pool.wait_ge(s_idx[h], (c + 1) * 16)
                    pool.sem_inc(s_pass, 1)
                    pool.wait_ge(s_scan, 2 * c + h + 1)
                    pool.sem_inc(s_pass, 1)
                    gather_chunk(pool, nc, h, dram["table1"], idx, rows, ATT, s_rows[h])

        @block.vector
        def _(dve):
            dve.sem_inc(s_scan, 2)
            dve.sem_inc(s_read, 2)
            head = stepper(dve, s_dve)
            head(nc.vector.memset(run[:, 1, STEP, :], 0.0))
            dve.wait_ge(s_start, 16)
            head(nc.vector.tensor_copy(at[:, 1, STEP, :], start[:, FEAT + HEADS:ATT]))

            def chunk(c, h):
                ch = 2 * c + h
                step = stepper(dve, s_dve, 2 + ch * STEPS)
                keep = g["keep"][:, ds(ch * STEP, STEP)]
                fall, grow = delta[:, 0, :, :], delta[:, 1, :, :]
                dve.wait_ge(s_out[h], (c + 1) * 16)
                dve.wait_ge(s_scan, ch + 2)
                step(nc.vector.tensor_copy(run[:, h, 0, :], run[:, 1 - h, STEP, :]))
                step(nc.vector.tensor_copy(at[:, h, 0, :], at[:, 1 - h, STEP, :]))
                dve.wait_ge(s_at[h], (c + 1) * 16)
                for k in range(HEADS):
                    last = scan(nc, at[:, h, :, :], at[:, h, 1:STEP + 1, :], keep, k, HEADS, HEADS, ALU.mult, ALU.add)
                step(last)
                dve.wait_ge(s_rows[h], (c + 1) * 16 * STEP)
                step(nc.vector.tensor_tensor(fall, rows[:, h, :, FEAT:FEAT + HEADS], at[:, h, 1:STEP + 1, :], ALU.add))
                dve.wait_ge(s_score, ch + 1)
                nc.vector.tensor_tensor(fall, score[:, h, 0:STEP * HEADS].rearrange("p (j h) -> p j h", h=HEADS),
                                        fall, ALU.add).then_inc(s_read, 1)
                dve.wait_ge(s_read, ch + 3)
                step(nc.vector.scalar_tensor_tensor(out=grow, in0=fall, scalar=0.2, in1=fall, op0=ALU.mult, op1=ALU.max))
                step(nc.vector.tensor_scalar(fall, fall, 0.0, None, ALU.max))
                for k in range(HEADS):
                    last = scan(nc, run[:, h, :, :], fall, keep, SUMS + k, SROW, HEADS, ALU.mult, ALU.max, df=k)
                step(last)
                step(nc.vector.tensor_tensor(fall, run[:, h, 0:STEP, SUMS:SROW], run[:, h, 1:STEP + 1, SUMS:SROW],
                                             ALU.subtract))
                step(nc.vector.tensor_scalar(fall, fall, 0.0, None, ALU.min))
                nc.vector.tensor_tensor(grow, grow, run[:, h, 1:STEP + 1, SUMS:SROW], ALU.subtract).then_inc(s_exp, 1)
                dve.wait_ge(s_expd, ch + 1)
                step(nc.vector.tensor_tensor(fall, fall, bc(keep, HEADS), ALU.mult))
                h4 = rows[:, h, :, 0:FEAT].rearrange("p j (h d) -> p j h d", d=HDIM)
                step(nc.vector.tensor_tensor(h4, h4, bc(grow, HDIM), ALU.mult))
                assert step.count[0] == STEPS
                dve.sem_inc(s_pass, 1)
                softmax_scans(dve, nc, run[:, h, :, :], fall, grow, rows[:, h, :, :], s_scan)

            with dve.Fori(0, CHUNKS // 2) as c:
                for h in range(2):
                    chunk(c, h)

        @block.scalar
        def _(act):
            act.dma_start(at[:, 0, 1:STEP + 1, :], spread[:, 0:STEP, :]).then_inc(s_at[0], 16)

            def chunk(c, h, last):
                ch = 2 * c + h
                act.wait_ge(s_exp, ch + 1)
                nc.scalar.activation(delta[:, :, :, :], delta[:, :, :, :], ACT.Exp).then_inc(s_expd, 1)
                if not (last and h == 1):
                    act.dma_start(at[:, 1 - h, 1:STEP + 1, :], spread[:, ds((ch + 1) * STEP, STEP), :]
                                  ).then_inc(s_at[1 - h], 16)

            every_chunk(act, chunk)

        @block.tensor
        def _(pe):
            pe.wait_ge(s_w, 16)
            with pe.Fori(0, CHUNKS // 2) as c:
                for h in range(2):
                    pe.wait_ge(s_attr[h], (c + 1) * 16)
                    pe.wait_ge(s_read, 2 * c + h + 1)
                    for k in range(8):
                        last = nc.tensor.matmul(score[:, h, k * 8 * HEADS:(k + 1) * 8 * HEADS], attr[:, h, k, :],
                                                w_edge[:, :], start=True, stop=True)
                    last.then_inc(s_score, 1)


def attention_nodes_phase(nc, io, g, dram):
    with ExitStack() as stack:
        m = Memory(nc, stack, "nodes2")
        x = m.sb("x", [P, BLKS, FEAT])
        acc = m.sb("acc", [P, BLKS, SROW])
        y = m.sb("y", [P, BLKS, FEAT])
        hn = m.sb("h", [P, BLKS, ATT])
        inv = m.sb("inv", [P, BLKS, HEADS])
        stat = m.sb("stat", [P, 2, BLKS])
        gamma, beta = m.sb("gamma", [P, FEAT]), m.sb("beta", [P, FEAT])
        s_in, s_acc, s_dve, s_var, s_std, s_x, s_out = (m.sem(n) for n in ("in", "acc", "dve", "var", "std", "x", "out"))
        block = stack.enter_context(nc.Block())

        @block.sync
        def _(sp):
            sp.dma_start(x[:, :, :], node_view(dram["x1"])).then_inc(s_in, 16)
            sp.dma_start(hn[:, :, :], node_view(dram["table1"])).then_inc(s_in, 16)
            sp.dma_start(gamma[:, :], io["ln_gamma"]).then_inc(s_in, 16)
            sp.dma_start(beta[:, :], io["ln_beta"]).then_inc(s_in, 16)
            sp.wait_ge(s_x, 1)
            sp.dma_start(node_view(dram["x2"]), x[:, :, :]).then_inc(s_out, 16)
            sp.wait_ge(s_out, 16)

        @block.gpsimd
        def _(pool):
            gather_nodes(pool, g, dram["run_softmax"], acc, s_acc)

        @block.vector
        def _(dve):
            step = stepper(dve, s_dve)
            dve.wait_ge(s_in, 64)
            dve.wait_ge(s_acc, 16 * BLKS)
            step(nc.vector.tensor_scalar(inv[:, :, :], acc[:, :, FEAT:SUMS], 1e-8, None, ALU.add))
            step(nc.vector.reciprocal(inv[:, :, :], inv[:, :, :]))
            step(nc.vector.tensor_tensor(inv[:, :, :], inv[:, :, :], bc(g["has"][:, :], HEADS), ALU.mult))
            step(nc.vector.tensor_tensor(y[:, :, :].rearrange("p b (h d) -> p b h d", d=HDIM),
                                         acc[:, :, 0:FEAT].rearrange("p b (h d) -> p b h d", d=HDIM),
                                         bc(inv[:, :, :], HDIM), ALU.mult))
            step(nc.vector.tensor_tensor(y[:, :, :], y[:, :, :], hn[:, :, 0:FEAT], ALU.add))
            norm_dve(dve, nc, step, y[:, :, :], acc[:, :, 0:FEAT], stat, s_var, s_std, 1)
            step(nc.vector.tensor_tensor(y[:, :, :], y[:, :, :], over_blocks(gamma), ALU.mult))
            step(nc.vector.tensor_tensor(y[:, :, :], y[:, :, :], over_blocks(beta), ALU.add))
            step(nc.vector.tensor_tensor(x[:, :, :], x[:, :, :], y[:, :, :], ALU.add))
            norm_dve(dve, nc, step, x[:, :, :], acc[:, :, 0:FEAT], stat, s_var, s_std, 2)
            nc.vector.tensor_copy(stat[:, 0, 0:1], stat[:, 1, 0:1]).then_inc(s_x, 1)

        @block.scalar
        def _(act):
            norm_act(act, nc, g, stat, s_var, s_std, 1)
            norm_act(act, nc, g, stat, s_var, s_std, 2)


def over_blocks(v, blocks=BLKS):
    return v[:, :].unsqueeze(1).to_broadcast([P, blocks, FEAT])



def network_extra(nc, m, io, g, dram):
    CP = STEP // 2
    PARTS = CP // 4
    attr = m.sb("attr", [P, 2, CP, P])
    out = m.sb("weight", [P, 2, CP, P])
    hid = [m.sb(f"hid{i}", [P, 2, 512]) for i in range(2)]
    w = [m.sb(f"fc{i}", [P, P]) for i in range(3)]
    bias = m.sb("bias", [P, 3])
    pre = [m.ps(f"pre{i}", [P, 2, 512]) for i in range(3)]
    s_w = m.sem("w")
    s_attr, s_out = ([m.sem(f"{n}{h}") for h in range(2)] for n in ("attr_in", "weight_out"))
    s_mm = [m.sem(f"mm{i}") for i in range(3)]
    s_act = [m.sem(f"act{i}") for i in range(3)]

    def act(act):
        for i in range(3):
            act.dma_start(w[i][:, :], io[f"fc{i + 1}"]).then_inc(s_w, 16)
        act.dma_start(bias[:, :], io["bfc"]).then_inc(s_w, 16)
        for h in range(2):
            act.dma_start(attr[:, h, :, :], io["e64"][:, h * CP:(h + 1) * CP, :]).then_inc(s_attr[h], 16)
            act.sem_inc(s_out[h], 16)
        for i in range(3):
            act.sem_inc(s_act[i], 2)
        act.wait_ge(s_w, 64)

        def chunk(c, h, last):
            ch = 2 * c + h
            flat = out[:, h, :, :].rearrange("p k n -> p (k n)")
            for q in range(PARTS + 2):
                if q < PARTS:
                    act.wait_ge(s_mm[0], ch * PARTS + q + 1)
                    act.wait_ge(s_mm[1], ch * PARTS + q + 1)
                    nc.scalar.activation(hid[0][:, q % 2, :], pre[0][:, q % 2, :], ACT.Silu, bias=bias[:, 0:1]
                                         ).then_inc(s_act[0], 1)
                if 1 <= q <= PARTS:
                    r = q - 1
                    act.wait_ge(s_mm[1], ch * PARTS + r + 3)
                    act.wait_ge(s_mm[2], ch * PARTS + r + 1)
                    nc.scalar.activation(hid[1][:, r % 2, :], pre[1][:, r % 2, :], ACT.Silu, bias=bias[:, 1:2]
                                         ).then_inc(s_act[1], 1)
                if q >= 2:
                    r = q - 2
                    if r == 0:
                        act.wait_ge(s_out[h], 16 * (c + 1))
                    act.wait_ge(s_mm[2], ch * PARTS + r + 3)
                    nc.scalar.activation(flat[:, r * 512:(r + 1) * 512], pre[2][:, r % 2, :], ACT.Identity,
                                         bias=bias[:, 2:3]).then_inc(s_act[2], 1)
            act.wait_ge(s_act[2], (ch + 1) * PARTS + 2)
            act.dma_start(dram["weight3"][:, ds(ch * CP, CP), :], out[:, h, :, :]).then_inc(s_out[h], 16)
            if not last:
                act.dma_start(attr[:, h, :, :], io["e64"][:, ds((ch + 2) * CP, CP), :]).then_inc(s_attr[h], 16)

        every_chunk(act, chunk)
        for h in range(2):
            act.wait_ge(s_out[h], 16 + 16 * (CHUNKS // 2))

    def pe(pe):
        for i in (1, 2):
            pe.sem_inc(s_mm[i], 2)
        pe.wait_ge(s_w, 64)
        with pe.Fori(0, CHUNKS // 2) as c:
            for h in range(2):
                ch = 2 * c + h
                pe.wait_ge(s_attr[h], (c + 1) * 16)
                flat = attr[:, h, :, :].rearrange("p k n -> p (k n)")
                for q in range(PARTS + 2):
                    if q < PARTS:
                        pe.wait_ge(s_act[0], ch * PARTS + q + 1)
                        nc.tensor.matmul(pre[0][:, q % 2, :], w[0][:, :], flat[:, q * 512:(q + 1) * 512],
                                         start=True, stop=True).then_inc(s_mm[0], 1)
                    if 1 <= q <= PARTS:
                        r = q - 1
                        pe.wait_ge(s_act[0], ch * PARTS + r + 3)
                        pe.wait_ge(s_act[1], ch * PARTS + r + 1)
                        nc.tensor.matmul(pre[1][:, r % 2, :], w[1][:, :], hid[0][:, r % 2, :],
                                         start=True, stop=True).then_inc(s_mm[1], 1)
                    if q >= 2:
                        r = q - 2
                        pe.wait_ge(s_act[1], ch * PARTS + r + 3)
                        pe.wait_ge(s_act[2], ch * PARTS + r + 1)
                        nc.tensor.matmul(pre[2][:, r % 2, :], w[2][:, :], hid[1][:, r % 2, :],
                                         start=True, stop=True).then_inc(s_mm[2], 1)

    return dict(dve_first=lambda dve: None, dve=lambda dve, ch: None, dve_last=lambda dve: None, act=act, pe=pe)



def batchnorm_phase(nc, io, g, dram):
    with ExitStack() as stack:
        m = Memory(nc, stack, "nodes3")
        x = m.sb("x", [P, BLKS, FEAT])
        acc = m.sb("acc", [P, BLKS, FEAT])
        y = m.sb("y", [P, BLKS, FEAT])
        valid = m.sb("valid", [P, BLKS])
        stat = m.sb("stat", [P, 2, BLKS])
        w, b = m.sb("w", [P, P]), m.sb("b", [P, FEAT])
        gamma, beta, part, mean = (m.sb(n, [P, FEAT]) for n in ("gamma", "beta", "part", "mean"))
        total = m.ps("total", [P, 512])
        s_in, s_acc, s_dve, s_var, s_std, s_x, s_out = (m.sem(n) for n in ("in", "acc", "dve", "var", "std", "x", "out"))
        s_sum, s_part, s_tot, s_bvar, s_bstd = (m.sem(n) for n in ("sum", "part", "total", "bvar", "bstd"))
        prod = NodeProduct(nc, m, g, acc, w, FEAT,
                           lambda k, ps: nc.vector.tensor_tensor(y[:, 2 * k:2 * k + 2, :], ps, over_blocks(b, 2), ALU.add))
        block = stack.enter_context(nc.Block())

        @block.sync
        def _(sp):
            sp.dma_start(x[:, :, :], node_view(dram["x2"])).then_inc(s_in, 16)
            for tile, name in ((w, "w2"), (b, "b2"), (gamma, "gamma2"), (beta, "beta2")):
                sp.dma_start(tile[:, :], io[name]).then_inc(s_in, 16)
            sp.wait_ge(s_x, 1)
            sp.dma_start(node_view(dram["x3"]), x[:, :, :]).then_inc(s_out, 16)
            sp.wait_ge(s_out, 16)

        @block.gpsimd
        def _(pool):
            gather_nodes(pool, g, dram["run_sum"], acc, s_acc)

        @block.vector
        def _(dve):
            step = stepper(dve, s_dve)
            by_feature = y[:, :, :].rearrange("p b f -> p f b")
            step(nc.vector.tensor_scalar(valid[:, :], g["nodenum"][:, :], float(NODES), None, ALU.is_lt))
            dve.wait_ge(s_in, 80)
            dve.wait_ge(s_acc, 16 * BLKS)
            step(nc.vector.tensor_tensor(acc[:, :, :], acc[:, :, :], bc(g["has"][:, :], FEAT), ALU.mult))
            nc.vector.tensor_tensor(acc[:, :, :], acc[:, :, :], x[:, :, :], ALU.add).then_inc(s_sum, 1)
            prod.dve(dve)
            dve.wait_ge(prod.s_done, PAIRS)
            step(nc.vector.tensor_tensor(y[:, :, :], y[:, :, :], bc(valid[:, :], FEAT), ALU.mult))
            nc.vector.reduce_sum(part[:, :], by_feature, axis=AX.X).then_inc(s_part, 1)
            dve.wait_ge(s_tot, 1)
            step(nc.vector.tensor_scalar(mean[:, :], total[:, 0:FEAT], 1.0 / NODES, None, ALU.mult))
            step(nc.vector.tensor_tensor(y[:, :, :], y[:, :, :], over_blocks(mean), ALU.subtract))
            step(nc.vector.tensor_tensor(y[:, :, :], y[:, :, :], bc(valid[:, :], FEAT), ALU.mult))
            step(nc.vector.tensor_tensor(acc[:, :, :], y[:, :, :], y[:, :, :], ALU.mult))
            nc.vector.reduce_sum(part[:, :], acc[:, :, :].rearrange("p b f -> p f b"), axis=AX.X).then_inc(s_part, 1)
            dve.wait_ge(s_bstd, 1)
            step(nc.vector.reciprocal(mean[:, :], mean[:, :]))
            step(nc.vector.tensor_tensor(mean[:, :], mean[:, :], gamma[:, :], ALU.mult))
            step(nc.vector.tensor_tensor(y[:, :, :], y[:, :, :], over_blocks(mean), ALU.mult))
            step(nc.vector.tensor_tensor(y[:, :, :], y[:, :, :], over_blocks(beta), ALU.add))
            step(nc.vector.scalar_tensor_tensor(out=x[:, :, :], in0=y[:, :, :], scalar=0.0, in1=x[:, :, :],
                                                op0=ALU.max, op1=ALU.add))
            norm_dve(dve, nc, step, x[:, :, :], acc[:, :, :], stat, s_var, s_std, 1)
            nc.vector.tensor_copy(stat[:, 0, 0:1], stat[:, 1, 0:1]).then_inc(s_x, 1)

        @block.scalar
        def _(act):
            prod.act(act)
            act.wait_ge(s_tot, 2)
            nc.scalar.activation(mean[:, :], total[:, 0:FEAT], ACT.Sqrt, scale=1.0 / NODES, bias=g["eps"][:, :]
                                 ).then_inc(s_bstd, 1)
            norm_act(act, nc, g, stat, s_var, s_std, 1)

        @block.tensor
        def _(pe):
            pe.wait_ge(s_sum, 1)
            prod.pe(pe)
            for n in range(2):
                pe.wait_ge(s_part, n + 1)
                nc.tensor.matmul(total[:, 0:FEAT], g["ones"][:, :], part[:, :], start=True, stop=True).then_inc(s_tot, 1)


QALL = QROW + FEAT


def queries_phase(nc, io, g, dram):
    with ExitStack() as stack:
        m = Memory(nc, stack, "queries")
        x = m.sb("x", [P, BLKS, FEAT])
        tab = m.sb("tab", [P, BLKS, QALL])
        tmp = m.sb("tmp", [P, BLKS, FEAT])
        w, b, bk = m.sb("w", [P, 6 * FEAT]), m.sb("b", [P, 3 * FEAT]), m.sb("bk", [P, FEAT])
        s_in, s_dve, s_tab, s_out, s_spread = (m.sem(n) for n in ("in", "dve", "tab", "out", "spread"))

        def finish(k, ps):
            bias = b[:, :].unsqueeze(1).to_broadcast([P, 2, 3 * FEAT])
            nc.vector.tensor_tensor(tab[:, 2 * k:2 * k + 2, 0:2 * FEAT], ps[:, :, 0:2 * FEAT], bias[:, :, 0:2 * FEAT], ALU.add)
            return nc.vector.tensor_tensor(tab[:, 2 * k:2 * k + 2, QROW:QALL], ps[:, :, 2 * FEAT:], bias[:, :, 2 * FEAT:], ALU.add)

        prod = NodeProduct(nc, m, g, x, w, 3 * FEAT, finish)
        block = stack.enter_context(nc.Block())

        @block.sync
        def _(sp):
            sp.dma_start(x[:, :, :], node_view(dram["x3"])).then_inc(s_in, 16)
            for tile, name in ((w, "w3"), (b, "b3"), (bk, "bk")):
                sp.dma_start(tile[:, :], io[name]).then_inc(s_in, 16)
            sp.wait_ge(s_tab, 1)
            sp.dma_start(node_view(dram["quer3"]), tab[:, :, 0:QROW]).then_inc(s_out, 16)
            sp.dma_start(node_view(dram["table3"]), tab[:, :, QROW:QALL]).then_inc(s_out, 16)
            sp.wait_ge(s_out, 32)

        @block.gpsimd
        def _(pool):
            pool.wait_ge(s_tab, 1)
            scatter_nodes(pool, g, dram["at_dst3"], tab[:, :, 0:QROW], s_spread)
            pool.wait_ge(s_spread, 16 * BLKS)

        @block.vector
        def _(dve):
            step = stepper(dve, s_dve)
            dve.wait_ge(s_in, 64)
            prod.dve(dve)
            dve.wait_ge(prod.s_done, PAIRS)
            step(nc.vector.tensor_scalar(tab[:, :, 0:FEAT], tab[:, :, 0:FEAT], float(HDIM) ** -0.5, None, ALU.mult))
            step(nc.vector.tensor_tensor(tmp[:, :, :], tab[:, :, 0:FEAT], over_blocks(bk), ALU.mult))
            nc.vector.reduce_sum(tab[:, :, 2 * FEAT:QROW], tmp[:, :, :].rearrange("p b (h d) -> p b h d", d=HDIM),
                                 axis=AX.X).then_inc(s_tab, 1)

        @block.scalar
        def _(act):
            prod.act(act)

        @block.tensor
        def _(pe):
            pe.wait_ge(s_in, 64)
            prod.pe(pe)



def transformer_phase(nc, io, g, dram):
    CP = STEP // 2
    GROUPS = CP // 4
    with ExitStack() as stack:
        m = Memory(nc, stack, "edges4")
        idx = m.sb("idx", [P, 2, STEP], U32)
        rows = m.sb("rows", [P, 2, STEP, FEAT])
        run = m.sb("run", [P, 2, STEP + 1, SROW])
        at = m.sb("at", [P, 2, STEP + 1, QROW])
        start = m.sb("start", [P, QROW])
        weight = m.sb("weight", [P, 2, CP, P])
        ea = m.sb("ea", [P, COLS])
        w_kv = m.sb("w_kv", [P, 4 * FEAT])
        cut = m.sb("cut", [P, STEP])
        delta = m.sb("delta", [P, 2, 2, STEP, HEADS])
        times = m.sb("times", [P, STEP, HEADS])
        turned = m.ps("turned", [P, 2, 512])
        keys = m.ps("keys", [P, 2, 512])
        values = m.ps("values", [P, 2, 512])
        s_idx, s_rows, s_out, s_at, s_wt = ([m.sem(f"{n}{h}") for h in range(2)]
                                            for n in ("idx", "rows", "out", "at", "weight"))
        (s_w, s_start, s_scan, s_dve, s_pass, s_kv, s_turn, s_tp, s_mm, s_k, s_v, s_alpha, s_exp, s_expd) = (
            m.sem(n) for n in ("w", "start", "scanned", "dve", "passed", "kv", "turned", "times", "mm", "k_read",
                               "v_read", "alpha", "to_exp", "exp_done"))
        block = stack.enter_context(nc.Block())
        store = dram["run_softmax"].rearrange("(p j) f -> p j f", p=P)
        spread = dram["at_dst3"][0:EPAD, :].rearrange("(p j) f -> p j f", p=P)
        STEPS = 13

        @block.sync
        def _(sp):
            def load_idx(ch, h):
                sp.dma_start(idx[:, h, :], io["src"][:, ds(ch * STEP, STEP)]).then_inc(s_idx[h], 16)

            def load_weight(ch, h):
                sp.dma_start(weight[:, h, :, :], dram["weight3"][:, ds(ch * CP, CP), :]).then_inc(s_wt[h], 16)

            sp.dma_start(ea[:, :], io["ea"]).then_inc(s_w, 16)
            sp.dma_start(w_kv[:, :], io["w_kv"]).then_inc(s_w, 16)
            for h in range(2):
                sp.sem_inc(s_out[h], 16)
                load_idx(h, h)
                load_weight(h, h)

            def chunk(c, h, last):
                ch = 2 * c + h
                if not last:
                    sp.wait_ge(s_kv, ch + 1)
                    load_idx(ch + 2, h)
                    sp.wait_ge(s_mm, (ch + 1) * GROUPS)
                    load_weight(ch + 2, h)
                sp.wait_ge(s_scan, ch + 2)
                sp.dma_start(store[:, ds(ch * STEP, STEP), :], run[:, h, 1:STEP + 1, :]).then_inc(s_out[h], 16)

            every_chunk(sp, chunk)
            for h in range(2):
                sp.wait_ge(s_out[h], 16 + 16 * (CHUNKS // 2))

        @block.gpsimd
        def _(pool):
            pool.indirect_dma_start(out=start[:, :], out_offset=None, in_=dram["quer3"],
                                    in_offset=bass.IndirectOffsetOnAxis(ap=g["dst0"][:, :], axis=0)
                                    ).then_inc(s_start, 16)
            with pool.Fori(0, CHUNKS // 2) as c:
                for h in range(2):
                    pool.wait_ge(s_idx[h], (c + 1) * 16)
                    pool.sem_inc(s_pass, 1)
                    pool.wait_ge(s_turn, (2 * c + h + 1) * GROUPS)
                    pool.sem_inc(s_pass, 1)
                    gather_chunk(pool, nc, h, dram["table3"], idx, rows, FEAT, s_rows[h])

        @block.vector
        def _(dve):
            dve.sem_inc(s_k, 2)
            dve.sem_inc(s_tp, 2)
            head = stepper(dve, s_dve)
            head(nc.vector.memset(delta[:, :, :, :, :], 0.0))
            head(nc.vector.memset(run[:, :, :, :], 0.0))
            head(nc.vector.memset(run[:, 1, STEP, SUMS:SROW], -BIG))
            dve.wait_ge(s_start, 16)
            dve.wait_ge(s_w, 32)

            def spread_scans(ch, h, first, count):
                for f in range(first, first + count):
                    last = scan(nc, at[:, h, :, :], at[:, h, 1:STEP + 1, :], g["keep"][:, ds(ch * STEP, STEP)],
                                f, QROW, QROW, ALU.mult, ALU.add)
                return last

            def sum_scans(h, head):
                factor = delta[:, h, 0, :, :].rearrange("p j h -> p (j h)")[:, ds(head, STEP, HEADS)]
                data = run[:, h, 1:STEP + 1, :]
                for f in range(head * HDIM, (head + 1) * HDIM):
                    scan(nc, run[:, h, :, :], data, factor, f, SROW, SROW, ALU.mult, ALU.add)
                return scan(nc, run[:, h, :, :], delta[:, h, 1, :, :], factor, FEAT + head, SROW, HEADS,
                            ALU.mult, ALU.add, df=head)

            head(nc.vector.tensor_copy(at[:, 0, 0, :], start[:, :]))
            dve.wait_ge(s_at[0], 16)
            head(spread_scans(0, 0, 0, QROW))

            def chunk(c, h, end):
                ch = 2 * c + h
                step = stepper(dve, s_dve, 5 + ch * STEPS)
                keep = g["keep"][:, ds(ch * STEP, STEP)]
                fall, grow = delta[:, h, 0, :, :], delta[:, h, 1, :, :]
                ea4 = bc(ea[:, ds(ch * STEP, STEP)], HEADS)
                q = at[:, h, 1:STEP + 1, 0:FEAT]
                flat = weight[:, h, :, :].rearrange("p k n -> p (k n)")
                more = not (end and h == 1)
                dve.wait_ge(s_rows[h], (c + 1) * 16 * STEP)
                nc.vector.tensor_tensor(rows[:, h, :, :], rows[:, h, :, :], at[:, h, 1:STEP + 1, FEAT:2 * FEAT],
                                        ALU.add).then_inc(s_kv, 1)
                step(nc.vector.tensor_copy(run[:, 1 - h, 0, 0:SUMS], run[:, h, STEP, 0:SUMS]))
                if more:
                    step(nc.vector.tensor_copy(at[:, 1 - h, 0, :], at[:, h, STEP, :]))
                step(nc.vector.tensor_scalar(cut[:, :], keep, BIG, -BIG, ALU.mult, ALU.add))
                dve.wait_ge(s_wt[h], (c + 1) * 16)
                for n in range(GROUPS + 1):
                    if n < GROUPS:
                        dve.wait_ge(s_turn, (ch + 2) * GROUPS + n + 1)
                        nc.vector.tensor_tensor(flat[:, n * 512:(n + 1) * 512], turned[:, n % 2, :],
                                                flat[:, n * 512:(n + 1) * 512], ALU.mult).then_inc(s_tp, 1)
                    if n < HEADS:
                        last = sum_scans(1 - h, n)
                        if n == HEADS - 1:
                            last.then_inc(s_scan, 1)
                    elif more:
                        if n == HEADS:
                            dve.wait_ge(s_at[1 - h], (c + 1 + h) * 16)
                        rest = -(-QROW // (GROUPS + 1 - HEADS))
                        first = (n - HEADS) * rest
                        last = spread_scans(ch + 1, 1 - h, first, min(rest, QROW - first))
                    if n >= 1:
                        i = n - 1
                        dve.wait_ge(s_mm, ch * GROUPS + i + 1)
                        q8 = at[:, h, 1 + 8 * i:9 + 8 * i, 0:FEAT]
                        nc.vector.tensor_tensor(q8, keys[:, i % 2, :].rearrange("p (j f) -> p j f", j=8), q8,
                                                ALU.mult).then_inc(s_k, 1)
                if more:
                    step(last)
                step(nc.vector.tensor_copy(run[:, h, 0, SUMS:SROW], run[:, 1 - h, STEP, SUMS:SROW]))
                dve.wait_ge(s_k, (ch + 1) * GROUPS + 2)
                step(nc.vector.reduce_sum(fall, q.rearrange("p j (h d) -> p j h d", d=HDIM), axis=AX.X))
                step(nc.vector.tensor_tensor(fall, fall, ea4, ALU.mult))
                nc.vector.tensor_tensor(fall, fall, at[:, h, 1:STEP + 1, 2 * FEAT:QROW], ALU.add).then_inc(s_alpha, 1)
                dve.wait_ge(s_alpha, ch + 1)
                dve.wait_ge(s_out[h], (c + 1) * 16)
                for k in range(HEADS):
                    last = scan(nc, run[:, h, :, :], fall, cut[:, :], SUMS + k, SROW, HEADS, ALU.add, ALU.max, df=k)
                step(last)
                peak, before = run[:, h, 1:STEP + 1, SUMS:SROW], run[:, h, 0:STEP, SUMS:SROW]
                step(nc.vector.tensor_tensor(grow, fall, peak, ALU.subtract))
                step(nc.vector.tensor_tensor(fall, before, peak, ALU.subtract))
                nc.vector.tensor_scalar(fall, fall, 0.0, None, ALU.min).then_inc(s_exp, 1)
                dve.wait_ge(s_expd, ch + 1)
                step(nc.vector.tensor_tensor(fall, fall, bc(keep, HEADS), ALU.mult))
                step(nc.vector.tensor_tensor(times[:, :, :], grow, ea4, ALU.mult))
                dve.wait_ge(s_v, (ch + 1) * GROUPS + 2)
                h4 = run[:, h, 1:STEP + 1, 0:FEAT].rearrange("p j (h d) -> p j h d", d=HDIM)
                step(nc.vector.tensor_tensor(h4, h4, bc(times[:, :, :], HDIM), ALU.mult))
                dve.sem_inc(s_pass, 1)
                assert step.count[0] == STEPS or not more, step.count

            every_chunk(dve, chunk)
            tail = stepper(dve, s_dve, 5 + CHUNKS * STEPS - 2)
            tail(nc.vector.tensor_copy(run[:, 1, 0, 0:SUMS], run[:, 0, STEP, 0:SUMS]))
            for head_ in range(HEADS):
                last = sum_scans(1, head_)
            last.then_inc(s_scan, 1)

        @block.scalar
        def _(act):
            act.sem_inc(s_v, 2)
            for h in range(2):
                act.dma_start(at[:, h, 1:STEP + 1, :], spread[:, h * STEP:(h + 1) * STEP, :]).then_inc(s_at[h], 16)

            def chunk(c, h, last):
                ch = 2 * c + h
                act.wait_ge(s_out[h], (c + 1) * 16)
                for i in range(GROUPS):
                    act.wait_ge(s_mm, ch * GROUPS + i + 1)
                    nc.scalar.activation(run[:, h, 1 + 8 * i:9 + 8 * i, 0:FEAT],
                                         values[:, i % 2, :].rearrange("p (j f) -> p j f", j=8),
                                         ACT.Copy).then_inc(s_v, 1)
                if not last:
                    act.wait_ge(s_alpha, ch + 1)
                    act.dma_start(at[:, h, 1:STEP + 1, :], spread[:, ds((ch + 2) * STEP, STEP), :]).then_inc(s_at[h], 16)
                act.wait_ge(s_exp, ch + 1)
                nc.scalar.activation(delta[:, h, :, :, :], delta[:, h, :, :, :], ACT.Exp).then_inc(s_expd, 1)

            every_chunk(act, chunk)

        @block.tensor
        def _(pe):
            pe.sem_inc(s_turn, 2 * GROUPS)
            pe.wait_ge(s_w, 32)
            with pe.Fori(0, CHUNKS // 2) as c:
                for h in range(2):
                    ch = 2 * c + h
                    pe.wait_ge(s_kv, ch + 1)
                    for n in range(GROUPS + 1):
                        if n < GROUPS:
                            pe.wait_ge(s_tp, ch * GROUPS + n + 1)
                            for k in range(4):
                                j = 2 * (4 * n + k)
                                last = nc.tensor.transpose(turned[:, n % 2, k * P:(k + 1) * P],
                                                           rows[:, h, j:j + 2, :].rearrange("p a f -> p (a f)"),
                                                           g["ident"][:, :])
                            last.then_inc(s_turn, 1)
                        if n >= 1:
                            pe.wait_ge(s_tp, ch * GROUPS + n + 2)
                            i = n - 1
                            pe.wait_ge(s_k, ch * GROUPS + i + 1)
                            pe.wait_ge(s_v, ch * GROUPS + i + 1)
                            for k in range(4):
                                for bank, part in ((keys, 0), (values, 1)):
                                    last = nc.tensor.matmul(bank[:, i % 2, k * P:(k + 1) * P], weight[:, h, 4 * i + k, :],
                                                            w_kv[:, part * P:(part + 1) * P], start=True, stop=True)
                            last.then_inc(s_mm, 1)


def result_phase(nc, io, g, dram, out):
    with ExitStack() as stack:
        m = Memory(nc, stack, "nodes4")
        x = m.sb("x", [P, BLKS, FEAT])
        acc = m.sb("acc", [P, BLKS, SROW])
        y = m.sb("y", [P, BLKS, FEAT])
        tmp = m.sb("tmp", [P, BLKS, FEAT])
        inv = m.sb("inv", [P, BLKS, HEADS])
        stat = m.sb("stat", [P, 2, BLKS])
        w, b, bv = m.sb("w", [P, P]), m.sb("b", [P, FEAT]), m.sb("bv", [P, FEAT])
        s_in, s_acc, s_dve, s_var, s_std, s_x, s_out, s_y = (
            m.sem(n) for n in ("in", "acc", "dve", "var", "std", "x", "out", "y"))
        prod = NodeProduct(nc, m, g, y, w, FEAT,
                           lambda k, ps: nc.vector.tensor_tensor(tmp[:, 2 * k:2 * k + 2, :], ps, over_blocks(b, 2), ALU.add))
        block = stack.enter_context(nc.Block())

        @block.sync
        def _(sp):
            sp.dma_start(x[:, :, :], node_view(dram["x3"])).then_inc(s_in, 16)
            for tile, name in ((w, "w_proj"), (b, "b_proj"), (bv, "bv")):
                sp.dma_start(tile[:, :], io[name]).then_inc(s_in, 16)
            sp.wait_ge(s_x, 1)
            whole = NODES // BLKS
            sp.dma_start(out[0:whole * BLKS, :].rearrange("(p b) f -> p b f", b=BLKS), x[0:whole, :, :]).then_inc(s_out, 16)
            left = NODES - whole * BLKS
            sp.dma_start(out[whole * BLKS:NODES, :].rearrange("(p b) f -> p b f", p=1), x[whole:whole + 1, 0:left, :]
                         ).then_inc(s_out, 16)
            sp.wait_ge(s_out, 32)

        @block.gpsimd
        def _(pool):
            gather_nodes(pool, g, dram["run_softmax"], acc, s_acc)

        @block.vector
        def _(dve):
            step = stepper(dve, s_dve)
            heads = lambda t: t.rearrange("p b (h d) -> p b h d", d=HDIM)
            dve.wait_ge(s_in, 64)
            dve.wait_ge(s_acc, 16 * BLKS)
            den = acc[:, :, FEAT:SUMS]
            step(nc.vector.tensor_scalar(inv[:, :, :], den, 1e-16, None, ALU.add))
            step(nc.vector.reciprocal(inv[:, :, :], inv[:, :, :]))
            step(nc.vector.tensor_tensor(inv[:, :, :], inv[:, :, :], bc(g["has"][:, :], HEADS), ALU.mult))
            step(nc.vector.tensor_tensor(heads(y[:, :, :]), heads(acc[:, :, 0:FEAT]), bc(inv[:, :, :], HDIM), ALU.mult))
            step(nc.vector.tensor_tensor(inv[:, :, :], inv[:, :, :], den, ALU.mult))
            step(nc.vector.tensor_copy(tmp[:, :, :], over_blocks(bv)))
            step(nc.vector.tensor_tensor(heads(tmp[:, :, :]), heads(tmp[:, :, :]), bc(inv[:, :, :], HDIM), ALU.mult))
            nc.vector.tensor_tensor(y[:, :, :], y[:, :, :], tmp[:, :, :], ALU.add).then_inc(s_y, 1)
            prod.dve(dve)
            dve.wait_ge(prod.s_done, PAIRS)
            step(nc.vector.tensor_tensor(x[:, :, :], x[:, :, :], tmp[:, :, :], ALU.add))
            norm_dve(dve, nc, step, x[:, :, :], y[:, :, :], stat, s_var, s_std, 1)
            nc.vector.tensor_copy(stat[:, 0, 0:1], stat[:, 1, 0:1]).then_inc(s_x, 1)

        @block.scalar
        def _(act):
            prod.act(act)
            norm_act(act, nc, g, stat, s_var, s_std, 1)

        @block.tensor
        def _(pe):
            pe.wait_ge(s_y, 1)
            prod.pe(pe)



def program(nc, io, out, upto):
    dram = {}
    for name, shape in dict(table0=(NPAD, FEAT), table1=(NPAD, ATT), table2=(NPAD, FEAT), table3=(NPAD, FEAT),
                            quer3=(NPAD, QROW), x1=(NPAD, FEAT), x2=(NPAD, FEAT), x3=(NPAD, FEAT),
                            run_sum=(EPAD, FEAT), run_softmax=(EPAD, SROW),
                            at_dst1=(EPAD + NPAD, HEADS), at_dst3=(EPAD + NPAD, QROW),
                            weight3=(P, COLS // 2, P), count_src=(NPAD,), count_dst=(NPAD,)).items():
        dram[name] = nc.dram_tensor(name, shape, F32, kind="Internal").ap()
    with ExitStack() as stack:
        m = Memory(nc, stack, "g")
        g = dict(iota=m.sb("iota", [P, P, GRP], BF16), rownum=m.sb("rownum", [P, P]), nodenum=m.sb("nodenum", [P, BLKS]),
                 edge0=m.sb("edge0", [P, 1]), eps=m.sb("eps", [P, 1]), ones=m.sb("ones", [P, P]),
                 ident=m.sb("ident", [P, P]), below=m.sb("below", [P, P]),
                 keep=m.sb("keep", [P, COLS]), through=m.sb("through", [P, 1]),
                 fixrow=m.sb("fixrow", [P, 1], U32), dst0=m.sb("dst0", [P, 1], U32),
                 has=m.sb("has", [P, BLKS]), lastrow=m.sb("lastrow", [P, BLKS], U32),
                 firstrow=m.sb("firstrow", [P, BLKS], U32), root_in=m.sb("root_in", [P, BLKS]))
        setup_phase(nc, io, g, dram)
        sum_phase(nc, io, g, dram, "edges1", dram["table0"], first_extra)
        segments_phase(nc, io, g, dram)
        carry_phase(nc, g, dram, "carry1", False)
        first_nodes_phase(nc, io, g, dram)
        rest(nc, io, g, dram, out, upto)


def store_phase(nc, src, out):
    with ExitStack() as stack:
        m = Memory(nc, stack, "store")
        s = m.sem("out")
        block = stack.enter_context(nc.Block())

        @block.sync
        def _(sp):
            sp.dma_start(out, src[0:NODES, 0:FEAT]).then_inc(s, 16)
            sp.wait_ge(s, 16)


def rest(nc, io, g, dram, out, upto):
    attention_phase(nc, io, g, dram)
    carry_phase(nc, g, dram, "carry2", True)
    attention_nodes_phase(nc, io, g, dram)
    if upto == 2:
        return store_phase(nc, dram["x2"], out)
    sum_phase(nc, io, g, dram, "edges3", dram["x2"], network_extra)
    carry_phase(nc, g, dram, "carry3", False)
    batchnorm_phase(nc, io, g, dram)
    if upto == 3:
        return store_phase(nc, dram["x3"], out)
    queries_phase(nc, io, g, dram)
    transformer_phase(nc, io, g, dram)
    carry_phase(nc, g, dram, "carry4", True)
    result_phase(nc, io, g, dram, out)


def kernel(**inputs):
    import concourse.bacc as bacc
    from concourse.bass_utils import run_bass_kernel_spmd as run

    v = {k: np.asarray(a) for k, a in inputs.items()}

    def edges(a, cols=COLS, fill=0):
        flat = np.full((EPAD,) + a.shape[1:], fill, a.dtype)
        flat[:EDGES] = a
        wide = np.full((P, cols) + a.shape[1:], fill, a.dtype)
        wide[:, :COLS] = flat.reshape((P, COLS) + a.shape[1:])
        return wide

    def diagonal(a, n):
        k, w = a.shape
        d = np.zeros((n * k, n * w), a.dtype)
        for i in range(n):
            d[i * k:(i + 1) * k, i * w:(i + 1) * w] = a
        return d

    def rows(a):
        return np.ascontiguousarray(np.broadcast_to(a.reshape(1, -1), (P, a.size)))

    x = np.zeros((NPAD, FEAT), v["x"].dtype)
    x[:NODES] = v["x"]
    w_node = np.zeros((FEAT, ATT), np.float32)
    w_node[:, :FEAT] = v["L1_gnn_W_node"]
    attn = np.zeros((FEAT, 2 * HEADS), np.float32)
    for h in range(HEADS):
        attn[h * HDIM:(h + 1) * HDIM, h] = v["L1_gnn_attn_src"][h]
        attn[h * HDIM:(h + 1) * HDIM, HEADS + h] = v["L1_gnn_attn_dst"][h]
    w3 = np.zeros((FEAT, 3 * FEAT), np.float32)
    w3[:, :FEAT], w3[:, FEAT:2 * FEAT], w3[:, 2 * FEAT:] = v["L3_gnn_Wq"], v["L3_gnn_W_dst"], v["L3_gnn_W_src"]
    b3 = np.zeros((3 * FEAT,), np.float32)
    b3[:FEAT], b3[2 * FEAT:] = v["L3_gnn_bq"], v["L3_gnn_b_src"]
    e16 = edges(v["edge_attr_16"]).reshape(P, COLS // 8, 8, EDIM).transpose(2, 3, 1, 0).reshape(P, COLS // 8, P)
    e64 = edges(v["edge_attr_64"]).reshape(P, COLS // 2, 2, FEAT).transpose(2, 3, 1, 0).reshape(P, COLS // 2, P)
    arrays = dict(
        x=x, src=edges(v["src"], COLS + 2 * STEP, NPAD - 1), dst=edges(v["dst"], COLS, NPAD - 1),
        e16=e16, e64=e64, ea=edges(v["edge_weight1"][:, 0]),
        w_node=diagonal(w_node, 2), w_node_t=np.concatenate([v["L1_gnn_W_node"].T] * 2, axis=1), attn=attn,
        w_edge=diagonal(v["L1_gnn_W_edge"], 8), ln_gamma=rows(v["L1_gnn_ln_gamma"]), ln_beta=rows(v["L1_gnn_ln_beta"]),
        w2=diagonal(v["L2_gnn_W"], 2), b2=rows(v["L2_gnn_b"]), gamma2=rows(v["L2_gnn_gamma"]), beta2=rows(v["L2_gnn_beta"]),
        w3=diagonal(w3, 2), b3=rows(b3), bk=rows(v["L3_gnn_b_kv"][:FEAT]), bv=rows(v["L3_gnn_b_kv"][FEAT:]),
        fc1=diagonal(v["L3_gnn_W_fc1"], 2), fc2=diagonal(v["L3_gnn_W_fc2"], 2), fc3=diagonal(v["L3_gnn_W_fc3"], 2),
        bfc=np.stack([np.concatenate([v[f"L3_gnn_b_fc{i}"]] * 2) for i in (1, 2, 3)], axis=1),
        w_kv=np.concatenate([diagonal(v["L3_gnn_W_kv"][:, :FEAT], 2), diagonal(v["L3_gnn_W_kv"][:, FEAT:], 2)], axis=1), w_proj=diagonal(v["L3_gnn_W_proj"], 2), b_proj=rows(v["L3_gnn_b_proj"]),
    )
    arrays = {k: np.ascontiguousarray(a) for k, a in arrays.items()}
    nc = bacc.Bacc("TRN2", target_bir_lowering=False, num_devices=1)
    io = {k: nc.dram_tensor(f"in_{k}", a.shape, mybir.dt.from_np(a.dtype), kind="ExternalInput").ap()
          for k, a in arrays.items()}
    io["src"] = io["src"].bitcast(U32)
    out = nc.dram_tensor("out", (NODES, FEAT), F32, kind="ExternalOutput").ap()
    program(nc, io, out, 4)
    r = run(nc, [{f"in_{k}": a for k, a in arrays.items()}], core_ids=[0])
    return r.results[0]["out"]
```

```python
from contextlib import ExitStack

import numpy as np

import concourse.bass as bass
from concourse import mybir

F32 = mybir.dt.float32
BF16 = mybir.dt.bfloat16
I32 = mybir.dt.int32
U32 = mybir.dt.uint32
ALU = mybir.AluOpType
ACT = mybir.ActivationFunctionType
AX = mybir.AxisListType

P = 128
NODES, EDGES, FEAT, HEADS, EDIM = 12500, 212500, 64, 4, 16
HDIM = FEAT // HEADS
BLKS = -(-NODES // P)
NPAD = BLKS * P
STEP = 64
COLS = -(-EDGES // (P * 2 * STEP)) * 2 * STEP
EPAD = COLS * P
CHUNKS = COLS // STEP
PARTS = 7
PBLK = BLKS // PARTS
PPAIR = PBLK // 2
PAIRS = BLKS // 2
REAL = NODES - (P - 1) * BLKS
SROW = FEAT + 2 * HEADS
SUMS = FEAT + HEADS
QROW = 2 * FEAT + HEADS
GRP = 32
GPC = STEP // GRP
HI = NPAD // P
BIG = 1.0e30
LN_EPS = 1e-5
ds = bass.ds


class Memory:

    def __init__(self, nc, stack, tag):
        self.nc, self.stack, self.tag, self.sems = nc, stack, tag, []
        stack.callback(self.clear)

    def clear(self):
        if self.sems:
            self.nc.clear_and_free_semaphores(self.sems)
            self.nc.all_engine_barrier(sem_only=True)

    def sb(self, name, shape, dtype=F32):
        return self.stack.enter_context(self.nc.sbuf_tensor(f"{self.tag}_{name}", shape, dtype))

    def ps(self, name, shape, dtype=F32):
        return self.stack.enter_context(self.nc.psum_tensor(f"{self.tag}_{name}", shape, dtype))

    def sem(self, name):
        self.sems.append(self.nc.alloc_semaphore(f"{self.tag}_{name}"))
        return self.sems[-1]


def stepper(eng, sem, base=0):
    count = [0]

    def step(ins):
        count[0] += 1
        ins.then_inc(sem, 1)
        eng.wait_ge(sem, base + count[0])

    step.count = count
    return step


def bc(ap, n):
    return ap.unsqueeze(len(ap.shape)).to_broadcast([*ap.shape, n])



def onehot_rows(dve, nc, ch, k, hist, made, used):
    s = k % 2
    dve.wait_ge(used, ch * GPC + k + 1)
    cols = ds(ch * STEP + k * GRP, GRP)
    nc.vector.tensor_tensor(hist["oh_hi"][:, s, :, :], hist["iota"][:, 0:HI, :],
                            hist["hi"][:, cols].unsqueeze(1).to_broadcast([P, HI, GRP]), ALU.is_equal)
    nc.vector.tensor_tensor(hist["oh_lo"][:, s, :, :], hist["iota"][:, :, :],
                            hist["lo"][:, cols].unsqueeze(1).to_broadcast([P, P, GRP]), ALU.is_equal).then_inc(made, 1)


def onehot_products(pe, nc, ch, k, hist, made, used):
    s = k % 2
    pe.wait_ge(made, ch * GPC + k + 1)
    for u in range(GRP):
        last = nc.tensor.matmul(hist["count"][0:HI, 0:P], hist["oh_hi"][:, s, :, u], hist["oh_lo"][:, s, :, u],
                                start=False, stop=False, skip_group_check=True)
    last.then_inc(used, 1)


def split_number(step, nc, number, part, hist):
    step(nc.vector.tensor_single_scalar(part[:, :], number, 7, ALU.logical_shift_right))
    step(nc.vector.tensor_copy(hist["hi"][:, :], part[:, :]))
    step(nc.vector.tensor_single_scalar(part[:, :], number, P - 1, ALU.bitwise_and))
    step(nc.vector.tensor_copy(hist["lo"][:, :], part[:, :]))



def setup_phase(nc, io, g, dram):
    with ExitStack() as stack:
        m = Memory(nc, stack, "setup")
        hist = dict(oh_hi=m.sb("oh_hi", [P, 2, HI, GRP], BF16), oh_lo=m.sb("oh_lo", [P, 2, P, GRP], BF16),
                    iota=g["iota"], hi=m.sb("hi", [P, COLS], BF16), lo=m.sb("lo", [P, COLS], BF16),
                    count=m.ps("count", [P, 512]))
        src = m.sb("src", [P, COLS], U32)
        dst = m.sb("dst", [P, COLS], I32)
        before = m.sb("before", [P, 1], I32)
        beforef = m.sb("beforef", [P, 1])
        part = m.sb("part", [P, COLS], U32)
        dstf = m.sb("dstf", [P, COLS])
        first = m.sb("first", [P, COLS])
        number = m.sb("number", [P, 1])
        zero = m.sb("zero", [P, P], BF16)
        counts = m.sb("counts", [P, P])
        deg = m.sb("deg", [P, BLKS])
        root = m.sb("root", [P, BLKS])
        x = m.sb("x", [P, BLKS, FEAT])
        s_src, s_dst, s_x = m.sem("src_in"), m.sem("dst_in"), m.sem("x_in")
        s_const, s_zero, s_dve = m.sem("constants"), m.sem("zeros"), m.sem("dve")
        s_made, s_used, s_open = m.sem("onehots_made"), m.sem("onehots_used"), m.sem("count_open")
        s_all, s_counts, s_deg_out, s_deg_in = m.sem("count_done"), m.sem("counts"), m.sem("deg_out"), m.sem("deg_in")
        s_max, s_root, s_table, s_store = m.sem("deg_max"), m.sem("root"), m.sem("table"), m.sem("stored")
        block = stack.enter_context(nc.Block())

        @block.sync
        def _(sp):
            sp.dma_start(src[:, :], io["src"][:, 0:COLS]).then_inc(s_src, 16)
            sp.dma_start(x[:, :, :], io["x"].rearrange("(p b) f -> p b f", p=P)).then_inc(s_x, 16)
            sp.wait_ge(s_zero, 1)
            sp.dma_start(before[1:P, :], io["dst"][0:P - 1, COLS - 1:COLS],
                         allow_slow_non_contiguous=True).then_inc(s_dst, 16)
            sp.dma_start(dst[:, :], io["dst"]).then_inc(s_dst, 16)
            sp.wait_ge(s_counts, 1)
            sp.dma_start(dram["count_src"].rearrange("(h l) -> h l", l=P), counts[0:HI, :]).then_inc(s_deg_out, 16)
            sp.wait_ge(s_deg_out, 16)
            sp.dma_start(deg[:, :], dram["count_src"].rearrange("(p b) -> p b", p=P)).then_inc(s_deg_in, 16)
            sp.wait_ge(s_table, 1)
            sp.dma_start(dram["table0"].rearrange("(p b) f -> p b f", p=P), x[:, :, :]).then_inc(s_store, 16)
            sp.wait_ge(s_store, 16)

        @block.gpsimd
        def _(pool):
            pool.iota(g["iota"][:, :, :], [[1, P], [0, GRP]], base=0, channel_multiplier=0,
                      allow_small_or_imprecise_dtypes=True).then_inc(s_const, 1)
            pool.iota(g["rownum"][:, :], [[1, P]], base=0, channel_multiplier=0,
                      allow_small_or_imprecise_dtypes=True).then_inc(s_const, 1)
            pool.iota(g["nodenum"][:, :], [[1, BLKS]], base=0, channel_multiplier=BLKS,
                      allow_small_or_imprecise_dtypes=True).then_inc(s_const, 1)
            pool.iota(g["edge0"][:, :], [[1, 1]], base=-1, channel_multiplier=COLS,
                      allow_small_or_imprecise_dtypes=True).then_inc(s_const, 1)
            pool.iota(number[:, :], [[1, 1]], base=0, channel_multiplier=1,
                      allow_small_or_imprecise_dtypes=True).then_inc(s_const, 1)

        @block.vector
        def _(dve):
            step = stepper(dve, s_dve)
            dve.sem_inc(s_used, 2)
            nc.vector.memset(zero[:, :], 0.0)
            nc.vector.memset(before[:, :], -1).then_inc(s_zero, 1)
            nc.vector.memset(g["eps"][:, :], LN_EPS)
            step(nc.vector.memset(g["ones"][:, :], 1.0))
            dve.wait_ge(s_const, 5)
            step(nc.vector.tensor_scalar(g["ident"][:, :], g["rownum"][:, :], number[:, :], None, ALU.is_equal))
            step(nc.vector.tensor_scalar(g["below"][:, :], g["rownum"][:, :], number[:, :], None, ALU.is_gt))
            dve.wait_ge(s_src, 16)
            split_number(step, nc, src[:, :], part, hist)
            with dve.Fori(0, CHUNKS) as ch:
                for k in range(GPC):
                    onehot_rows(dve, nc, ch, k, hist, s_made, s_used)
            dve.wait_ge(s_dst, 32)
            step(nc.vector.tensor_copy(dstf[:, :], dst[:, :]))
            step(nc.vector.tensor_copy(beforef[:, :], before[:, :]))
            step(nc.vector.tensor_tensor(g["keep"][:, 1:COLS], dstf[:, 1:COLS], dstf[:, 0:COLS - 1], ALU.is_equal))
            step(nc.vector.tensor_tensor(g["keep"][:, 0:1], dstf[:, 0:1], beforef[:, :], ALU.is_equal))
            step(nc.vector.tensor_scalar(first[:, :], dstf[:, :], dstf[:, 0:1], None, ALU.is_equal))
            step(nc.vector.reduce_sum(beforef[:, :], first[:, :], axis=AX.X))
            step(nc.vector.tensor_scalar(g["through"][:, :], beforef[:, :], float(COLS), None, ALU.is_equal))
            step(nc.vector.tensor_tensor(g["through"][:, :], g["through"][:, :], g["keep"][:, 0:1], ALU.mult))
            step(nc.vector.tensor_tensor(beforef[:, :], beforef[:, :], g["edge0"][:, :], ALU.add))
            step(nc.vector.tensor_copy(g["fixrow"][:, :], beforef[:, :]))
            step(nc.vector.tensor_copy(g["dst0"][:, :], dstf[:, 0:1]))
            dve.wait_ge(s_all, 1)
            nc.vector.tensor_copy(counts[0:HI, :], hist["count"][0:HI, 0:P]).then_inc(s_counts, 1)
            dve.wait_ge(s_deg_in, 16)
            nc.vector.tensor_scalar(deg[:, :], deg[:, :], 1.0, None, ALU.max).then_inc(s_max, 1)
            dve.wait_ge(s_root, 1)
            step(nc.vector.reciprocal(root[:, :], root[:, :]))
            dve.wait_ge(s_x, 16)
            nc.vector.tensor_tensor(x[:, :, :], x[:, :, :], bc(root[:, :], FEAT), ALU.mult).then_inc(s_table, 1)

        @block.scalar
        def _(act):
            act.wait_ge(s_max, 1)
            nc.scalar.activation(root[:, :], deg[:, :], ACT.Sqrt).then_inc(s_root, 1)

        @block.tensor
        def _(pe):
            pe.wait_ge(s_zero, 1)
            nc.tensor.matmul(hist["count"][0:HI, 0:P], zero[:, 0:HI], zero[:, :], start=True, stop=False,
                             skip_group_check=True)
            with pe.Fori(0, CHUNKS) as ch:
                for k in range(GPC):
                    onehot_products(pe, nc, ch, k, hist, s_made, s_used)
            nc.tensor.matmul(hist["count"][0:HI, 0:P], zero[:, 0:HI], zero[:, :], start=False, stop=True,
                             skip_group_check=True).then_inc(s_all, 1)



def gather_chunk(pool, nc, slot, table, idx, rows, width, sem):
    for u in range(STEP):
        pool.indirect_dma_start(out=rows[:, slot, u, 0:width], out_offset=None, in_=table,
                                in_offset=bass.IndirectOffsetOnAxis(ap=idx[:, slot, u:u + 1], axis=0)
                                ).then_inc(sem, 16)


def sum_phase(nc, io, g, dram, tag, table, extra):
    with ExitStack() as stack:
        m = Memory(nc, stack, tag)
        idx = m.sb("idx", [P, 2, STEP], U32)
        rows = m.sb("rows", [P, 2, STEP, FEAT])
        run = m.sb("run", [P, 2, STEP + 1, FEAT])
        s_idx = [m.sem(f"idx{h}") for h in range(2)]
        s_rows = [m.sem(f"rows{h}") for h in range(2)]
        s_out = [m.sem(f"out{h}") for h in range(2)]
        s_scan, s_carry, s_pass = m.sem("scanned"), m.sem("carried"), m.sem("passed")
        work = extra(nc, m, io, g, dram)
        block = stack.enter_context(nc.Block())
        store = dram["run_sum"].rearrange("(p j) f -> p j f", p=P)
        SC = FEAT // 8

        @block.sync
        def _(sp):
            for h in range(2):
                sp.sem_inc(s_out[h], 16)
                sp.dma_start(idx[:, h, :], io["src"][:, h * STEP:(h + 1) * STEP]).then_inc(s_idx[h], 16)
            with sp.Fori(0, CHUNKS // 2) as c:
                for h in range(2):
                    ch = 2 * c + h
                    sp.wait_ge(s_scan, (ch + 3) * SC)
                    sp.dma_start(store[:, ds(ch * STEP, STEP), :], run[:, h, 1:STEP + 1, :]).then_inc(s_out[h], 16)
                    sp.dma_start(idx[:, h, :], io["src"][:, ds((ch + 2) * STEP, STEP)]).then_inc(s_idx[h], 16)
            for h in range(2):
                sp.wait_ge(s_out[h], 16 + 16 * (CHUNKS // 2))
                sp.wait_ge(s_idx[h], 16 + 16 * (CHUNKS // 2))

        @block.gpsimd
        def _(pool):
            with pool.Fori(0, CHUNKS // 2) as c:
                for h in range(2):
                    pool.wait_ge(s_idx[h], (c + 1) * 16)
                    pool.sem_inc(s_pass, 1)
                    pool.wait_ge(s_scan, (2 * c + h + 1) * SC)
                    pool.sem_inc(s_pass, 1)
                    gather_chunk(pool, nc, h, table, idx, rows, FEAT, s_rows[h])

        @block.vector
        def _(dve):
            dve.sem_inc(s_scan, 2 * SC)
            nc.vector.memset(run[:, 1, STEP, :], 0.0).then_inc(s_carry, 1)
            work["dve_first"](dve)
            with dve.Fori(0, CHUNKS // 2) as c:
                for h in range(2):
                    ch = 2 * c + h
                    work["dve"](dve, ch)
                    dve.wait_ge(s_out[h], (c + 1) * 16)
                    dve.wait_ge(s_scan, (ch + 2) * SC)
                    dve.wait_ge(s_carry, ch + 1)
                    nc.vector.tensor_copy(run[:, h, 0, :], run[:, 1 - h, STEP, :]).then_inc(s_carry, 1)
                    dve.wait_ge(s_carry, ch + 2)
                    dve.wait_ge(s_rows[h], (c + 1) * 16 * STEP)
                    dve.sem_inc(s_pass, 1)
                    with dve.Fori(0, SC) as k:
                        for u in range(8):
                            f = k * 8 + u
                            last = scan(nc, run[:, h, :, :], rows[:, h, :, :], g["keep"][:, ds(ch * STEP, STEP)],
                                        f, FEAT, FEAT, ALU.mult, ALU.add)
                        last.then_inc(s_scan, 1)
            work["dve_last"](dve)

        @block.scalar
        def _(act):
            work["act"](act)

        @block.tensor
        def _(pe):
            work["pe"](pe)


def scan(nc, run, data, keep, f, rw, dw, op0, op1, df=None):
    flat = run.rearrange("p j f -> p (j f)")
    dflat = data.rearrange("p j f -> p (j f)")
    df = f if df is None else df
    return nc.vector.tensor_tensor_scan(out=flat[:, ds(f + rw, STEP, rw)], data0=keep,
                                        data1=dflat[:, ds(df, STEP, dw)], initial=flat[:, ds(f, 1)],
                                        op0=op0, op1=op1)


def no_extra(nc, m, io, g, dram):
    return dict(dve_first=lambda dve: None, dve=lambda dve, ch: None, dve_last=lambda dve: None,
                act=lambda act: None, pe=lambda pe: None)


def first_extra(nc, m, io, g, dram):
    hist = dict(oh_hi=m.sb("oh_hi", [P, 2, HI, GRP], BF16), oh_lo=m.sb("oh_lo", [P, 2, P, GRP], BF16),
                iota=g["iota"], hi=m.sb("hi", [P, COLS], BF16), lo=m.sb("lo", [P, COLS], BF16), count=m.ps("count", [P, 512]))
    dst = m.sb("dst", [P, COLS], I32)
    part = m.sb("part", [P, COLS], I32)
    zero = m.sb("zero", [P, P], BF16)
    zeros = m.sb("zeros", [P, STEP, QROW])
    counts = m.sb("counts", [P, P])
    s_dst, s_dve, s_zero, s_zeros = m.sem("dst_in"), m.sem("dve"), m.sem("zero"), m.sem("zeroed")
    s_made, s_used, s_all, s_counts = m.sem("onehots_made"), m.sem("onehots_used"), m.sem("count_done"), m.sem("counts")
    s_store = m.sem("counts_out")

    def dve_first(dve):
        step = stepper(dve, s_dve)
        dve.sem_inc(s_used, 2)
        nc.vector.memset(zero[:, :], 0.0).then_inc(s_zero, 1)
        nc.vector.memset(zeros[:, :, :], 0.0).then_inc(s_zero, 1)
        dve.wait_ge(s_dst, 16)
        split_number(step, nc, dst[:, :], part, hist)

    def dve_chunk(dve, ch):
        for k in range(GPC):
            onehot_rows(dve, nc, ch, k, hist, s_made, s_used)

    def dve_last(dve):
        dve.wait_ge(s_all, 1)
        nc.vector.tensor_copy(counts[0:HI, :], hist["count"][0:HI, 0:P]).then_inc(s_counts, 1)

    def act(act):
        act.dma_start(dst[:, :], io["dst"]).then_inc(s_dst, 16)
        act.wait_ge(s_zero, 2)
        zero_row = zeros[:, :, :].rearrange("p j f -> p (j f)").unsqueeze(1)
        act.dma_start(dram["at_dst1"][0:EPAD, :].rearrange("(p c j) f -> p c (j f)", p=P, j=STEP),
                      zero_row[:, :, 0:STEP * HEADS].to_broadcast([P, CHUNKS, STEP * HEADS])
                      ).then_inc(s_zeros, 16)
        with act.Fori(0, CHUNKS) as ch:
            act.wait_ge(s_used, (ch + 1) * GPC + 2)
            act.dma_start(dram["at_dst3"][0:EPAD, :].rearrange("(p j) f -> p j f", p=P)[:, ds(ch * STEP, STEP), :],
                          zeros[:, :, :]).then_inc(s_zeros, 16)
        act.wait_ge(s_counts, 1)
        act.dma_start(dram["count_dst"].rearrange("(h l) -> h l", l=P), counts[0:HI, :]).then_inc(s_store, 16)
        act.wait_ge(s_store, 16)
        act.wait_ge(s_zeros, 16 * (CHUNKS + 1))

    def pe(pe):
        pe.wait_ge(s_zero, 1)
        nc.tensor.matmul(hist["count"][0:HI, 0:P], zero[:, 0:HI], zero[:, :], start=True, stop=False,
                         skip_group_check=True)
        with pe.Fori(0, CHUNKS) as ch:
            for k in range(GPC):
                onehot_products(pe, nc, ch, k, hist, s_made, s_used)
        nc.tensor.matmul(hist["count"][0:HI, 0:P], zero[:, 0:HI], zero[:, :], start=False, stop=True,
                         skip_group_check=True).then_inc(s_all, 1)

    return dict(dve_first=dve_first, dve=dve_chunk, dve_last=dve_last, act=act, pe=pe)



def segments_phase(nc, io, g, dram):
    with ExitStack() as stack:
        m = Memory(nc, stack, "segments")
        deg = m.sb("deg", [P, BLKS])
        upto = m.sb("upto", [P, BLKS])
        total = m.ps("total", [P, 512])
        one = m.sb("one", [P, BLKS])
        t = m.sb("t", [P, BLKS])
        s_deg, s_dve, s_pe, s_act = m.sem("deg_in"), m.sem("dve"), m.sem("pe"), m.sem("act")
        block = stack.enter_context(nc.Block())

        @block.sync
        def _(sp):
            sp.dma_start(deg[:, :], dram["count_dst"].rearrange("(p b) -> p b", p=P)).then_inc(s_deg, 16)

        @block.gpsimd
        def _(pool):
            pass

        @block.vector
        def _(dve):
            step = stepper(dve, s_dve)
            step(nc.vector.memset(one[:, :], 1.0))
            dve.wait_ge(s_deg, 16)
            step(nc.vector.tensor_tensor_scan(out=upto[:, :], data0=one[:, :], data1=deg[:, :], initial=0.0,
                                              op0=ALU.mult, op1=ALU.add))
            dve.wait_ge(s_pe, 1)
            step(nc.vector.tensor_tensor(upto[:, :], upto[:, :], total[:, 0:1].to_broadcast([P, BLKS]), ALU.add))
            step(nc.vector.tensor_scalar(t[:, :], upto[:, :], -1.0, 0.0, ALU.add, ALU.max))
            step(nc.vector.tensor_copy(g["lastrow"][:, :], t[:, :]))
            step(nc.vector.tensor_scalar(g["has"][:, :], deg[:, :], 1.0, None, ALU.min))
            step(nc.vector.tensor_tensor(upto[:, :], upto[:, :], deg[:, :], ALU.subtract))
            step(nc.vector.tensor_tensor(upto[:, :], upto[:, :], g["has"][:, :], ALU.mult))
            step(nc.vector.tensor_scalar(t[:, :], g["nodenum"][:, :], float(EPAD), None, ALU.add))
            step(nc.vector.tensor_scalar(one[:, :], g["has"][:, :], -1.0, 1.0, ALU.mult, ALU.add))
            step(nc.vector.tensor_tensor(t[:, :], t[:, :], one[:, :], ALU.mult))
            step(nc.vector.tensor_tensor(t[:, :], t[:, :], upto[:, :], ALU.add))
            step(nc.vector.tensor_copy(g["firstrow"][:, :], t[:, :]))
            step(nc.vector.tensor_scalar(deg[:, :], deg[:, :], 1.0, None, ALU.max))
            dve.wait_ge(s_act, 1)
            step(nc.vector.reciprocal(g["root_in"][:, :], g["root_in"][:, :]))
            step(nc.vector.tensor_tensor(g["root_in"][:, :], g["root_in"][:, :], g["has"][:, :], ALU.mult))

        @block.scalar
        def _(act):
            act.wait_ge(s_dve, 14)
            nc.scalar.activation(g["root_in"][:, :], deg[:, :], ACT.Sqrt).then_inc(s_act, 1)

        @block.tensor
        def _(pe):
            pe.wait_ge(s_dve, 2)
            nc.tensor.matmul(total[:, 0:1], g["below"][:, :], upto[:, BLKS - 1:BLKS],
                             start=True, stop=True).then_inc(s_pe, 1)



def carry_phase(nc, g, dram, tag, softmax):
    table = dram["run_softmax" if softmax else "run_sum"]
    width = SROW if softmax else FEAT
    sums = SUMS if softmax else FEAT
    with ExitStack() as stack:
        m = Memory(nc, stack, tag)
        end = m.sb("end", [P, width])
        row = m.sb("row", [P, width])
        both = m.sb("both", [P, 3, sums])
        flip = m.sb("flip", [sums, 3, P])
        state = m.sb("state", [sums, P + 1])
        peak = m.sb("peak", [sums, P + 1])
        fac = m.sb("fac", [sums, 2, P])
        back = m.sb("back", [P, 2, sums])
        rpk = m.sb("rpk", [P, sums])
        efac = m.sb("efac", [P, 2, sums])
        ps = m.ps("ps", [P, 512])
        s_end, s_row, s_dve, s_pe, s_act, s_fixed = (m.sem("end_in"), m.sem("row_in"), m.sem("dve"), m.sem("pe"),
                                                     m.sem("act"), m.sem("fixed"))
        s_turned, s_ready, s_exp, s_mend = m.sem("turned"), m.sem("ready"), m.sem("exp"), m.sem("mend")
        block = stack.enter_context(nc.Block())
        np_ = 3 if softmax else 2
        planes = [0, 1, 2] if softmax else [0, 2]

        def widen(step, out, maxima):
            step(nc.vector.tensor_copy(out[:, 0:FEAT].rearrange("p (h d) -> p h d", d=HDIM), bc(maxima, HDIM)))
            step(nc.vector.tensor_copy(out[:, FEAT:SUMS], maxima))

        @block.sync
        def _(sp):
            sp.dma_start(end[:, :], table.rearrange("(p j) f -> p j f", p=P)[:, COLS - 1, :]).then_inc(s_end, 16)

        @block.gpsimd
        def _(pool):
            pool.indirect_dma_start(out=row[:, :], out_offset=None, in_=table[:, :],
                                    in_offset=bass.IndirectOffsetOnAxis(ap=g["fixrow"][:, :], axis=0)
                                    ).then_inc(s_row, 16)
            pool.wait_ge(s_mend, 1)
            pool.indirect_dma_start(out=table[:, :], out_offset=bass.IndirectOffsetOnAxis(ap=g["fixrow"][:, :], axis=0),
                                    in_=row[:, :], in_offset=None).then_inc(s_fixed, 16)
            pool.wait_ge(s_fixed, 16)

        @block.vector
        def _(dve):
            step = stepper(dve, s_dve)
            step(nc.vector.memset(state[:, :], 0.0))
            step(nc.vector.memset(peak[:, :], 0.0))
            step(nc.vector.tensor_copy(both[:, 2, :], g["through"][:, :].to_broadcast([P, sums])))
            dve.wait_ge(s_end, 16)
            step(nc.vector.tensor_copy(both[:, 0, :], end[:, 0:sums]))
            if softmax:
                widen(step, both[:, 1, :], end[:, SUMS:SROW])
            nc.vector.tensor_copy(rpk[:, 0:1], both[:, 0, 0:1]).then_inc(s_ready, 1)
            dve.wait_ge(s_turned, 1)
            step(nc.vector.tensor_copy(flip[:, 0:np_, :], ps[0:sums, 0:np_ * P].rearrange("f (n p) -> f n p", n=np_)))
            through = flip[:, np_ - 1, :]
            if softmax:
                step(nc.vector.tensor_scalar(fac[:, 0, :], through, BIG, -BIG, ALU.mult, ALU.add))
                step(nc.vector.tensor_tensor_scan(out=peak[:, 1:P + 1], data0=fac[:, 0, :], data1=flip[:, 1, :],
                                                  initial=0.0, op0=ALU.add, op1=ALU.max))
                step(nc.vector.tensor_tensor(fac[:, 0, :], peak[:, 0:P], peak[:, 1:P + 1], ALU.subtract))
                step(nc.vector.tensor_scalar(fac[:, 0, :], fac[:, 0, :], 0.0, None, ALU.min))
                step(nc.vector.tensor_tensor(fac[:, 1, :], flip[:, 1, :], peak[:, 1:P + 1], ALU.subtract))
                nc.vector.tensor_scalar(fac[:, 1, :], fac[:, 1, :], 0.0, None, ALU.min).then_inc(s_exp, 1)
                dve.wait_ge(s_act, 1)
                step(nc.vector.tensor_tensor(fac[:, 0, :], fac[:, 0, :], through, ALU.mult))
                step(nc.vector.tensor_tensor(fac[:, 1, :], fac[:, 1, :], flip[:, 0, :], ALU.mult))
                step(nc.vector.tensor_tensor_scan(out=state[:, 1:P + 1], data0=fac[:, 0, :], data1=fac[:, 1, :],
                                                  initial=0.0, op0=ALU.mult, op1=ALU.add))
            else:
                step(nc.vector.tensor_tensor_scan(out=state[:, 1:P + 1], data0=through, data1=flip[:, 0, :],
                                                  initial=0.0, op0=ALU.mult, op1=ALU.add))
            nc.vector.tensor_copy(rpk[:, 0:1], both[:, 0, 0:1]).then_inc(s_ready, 1)
            dve.wait_ge(s_turned, 2)
            dve.wait_ge(s_row, 16)
            if softmax:
                step(nc.vector.tensor_copy(back[:, :, :], ps[:, 0:2 * sums].rearrange("p (n f) -> p n f", n=2)))
                widen(step, rpk, row[:, SUMS:SROW])
                step(nc.vector.tensor_scalar(end[:, 0:1], g["keep"][:, 0:1], BIG, -BIG, ALU.mult, ALU.add))
                step(nc.vector.tensor_scalar(back[:, 1, :], back[:, 1, :], end[:, 0:1], None, ALU.add))
                step(nc.vector.tensor_tensor(efac[:, 1, :], back[:, 1, :], rpk[:, :], ALU.max))
                step(nc.vector.tensor_tensor(efac[:, 0, :], rpk[:, :], efac[:, 1, :], ALU.subtract))
                nc.vector.tensor_tensor(efac[:, 1, :], back[:, 1, :], efac[:, 1, :], ALU.subtract).then_inc(s_exp, 1)
                dve.wait_ge(s_act, 2)
                step(nc.vector.tensor_tensor(row[:, 0:sums], row[:, 0:sums], efac[:, 0, :], ALU.mult))
                step(nc.vector.tensor_tensor(back[:, 0, :], back[:, 0, :], efac[:, 1, :], ALU.mult))
                nc.vector.tensor_tensor(row[:, 0:sums], row[:, 0:sums], back[:, 0, :], ALU.add).then_inc(s_mend, 1)
            else:
                nc.vector.scalar_tensor_tensor(out=row[:, :], in0=ps[:, 0:FEAT], scalar=g["keep"][:, 0:1],
                                               in1=row[:, :], op0=ALU.mult, op1=ALU.add).then_inc(s_mend, 1)

        @block.scalar
        def _(act):
            if softmax:
                act.wait_ge(s_exp, 1)
                nc.scalar.activation(fac[:, :, :], fac[:, :, :], ACT.Exp).then_inc(s_act, 1)
                act.wait_ge(s_exp, 2)
                nc.scalar.activation(efac[:, :, :], efac[:, :, :], ACT.Exp).then_inc(s_act, 1)

        @block.tensor
        def _(pe):
            pe.wait_ge(s_ready, 1)
            for n, plane in enumerate(planes):
                last = nc.tensor.transpose(ps[0:sums, n * P:(n + 1) * P], both[:, plane, :], g["ident"][:, :])
            last.then_inc(s_turned, 1)
            pe.wait_ge(s_ready, 2)
            for n, what in enumerate([state, peak] if softmax else [state]):
                last = nc.tensor.transpose(ps[:, n * sums:(n + 1) * sums], what[:, 0:P], g["ident"][0:sums, 0:sums])
            last.then_inc(s_turned, 1)



def blocks_of(part):
    return slice(part * PBLK, (part + 1) * PBLK)


def gather_nodes(pool, g, table, acc, sems):
    for b in range(BLKS):
        pool.indirect_dma_start(out=acc[:, b, :], out_offset=None, in_=table[:, :],
                                in_offset=bass.IndirectOffsetOnAxis(ap=g["lastrow"][:, b:b + 1], axis=0)
                                ).then_inc(sems[b // PBLK], 16)


def scatter_nodes(pool, g, table, rows, ready, sem):
    for b in range(BLKS):
        if b % PBLK == 0:
            pool.wait_ge(ready, b // PBLK + 1)
        pool.indirect_dma_start(out=table[:, :], out_offset=bass.IndirectOffsetOnAxis(ap=g["firstrow"][:, b:b + 1], axis=0),
                                in_=rows[:, b, :], in_offset=None).then_inc(sem, 16)


def norm_dve(dve, nc, step, x, sq, stat, s_var, s_std, turn, ready=None):
    mean, var = stat[:, 0, :], stat[:, 1, :]
    step(nc.vector.reduce_sum(mean, x, axis=AX.X))
    step(nc.vector.tensor_scalar(mean, mean, 1.0 / FEAT, None, ALU.mult))
    step(nc.vector.tensor_tensor(x, x, bc(mean, FEAT), ALU.subtract))
    step(nc.vector.tensor_tensor(sq, x, x, ALU.mult))
    nc.vector.reduce_sum(var, sq, axis=AX.X).then_inc(s_var, 1)
    dve.wait_ge(s_std, turn)
    step(nc.vector.reciprocal(var, var))
    last = nc.vector.tensor_tensor(x, x, bc(var, FEAT), ALU.mult)
    if ready is None:
        step(last)
    else:
        last.then_inc(ready, 1)


def norm_act(act, nc, g, stat, s_var, s_std, turn):
    act.wait_ge(s_var, turn)
    nc.scalar.activation(stat[:, 1, :], stat[:, 1, :], ACT.Sqrt, scale=1.0 / FEAT, bias=g["eps"][:, :]).then_inc(s_std, 1)


class NodeProduct:

    def __init__(self, nc, m, g, name, x, w, width, finish, banks=None):
        self.nc, self.g, self.x, self.w, self.width, self.finish = nc, g, x, w, width, finish
        self.turned, self.out, self.xt = banks or (m.ps("turned", [P, 2, 512]), m.ps("out", [P, 4, 512]),
                                                   m.sb("xt", [P, 2, 4, P]))
        self.s_turn, self.s_xt, self.s_mm, self.s_done = (m.sem(name + n) for n in ("turn", "xt", "mm", "done"))
        self.groups = [(part * PPAIR + k, min(4, PPAIR - k)) for part in range(PARTS) for k in (0, 4)]

    def pe(self, pe, part):
        for n in (2 * part, 2 * part + 1):
            if n >= 2:
                pe.wait_ge(self.s_xt, n - 1)
            k0, count = self.groups[n]
            for k in range(count):
                last = self.nc.tensor.transpose(self.turned[:, n % 2, k * P:(k + 1) * P],
                                                self.x[:, 2 * (k0 + k):2 * (k0 + k) + 2, :].rearrange("p b f -> p (b f)"),
                                                self.g["ident"][:, :])
            last.then_inc(self.s_turn, 1)
        for n in (2 * part, 2 * part + 1):
            pe.wait_ge(self.s_xt, n + 1)
            k0, count = self.groups[n]
            for k in range(count):
                pair = k0 + k
                if pair >= 4:
                    pe.wait_ge(self.s_done, pair - 3)
                self.nc.tensor.matmul(self.out[:, pair % 4, 0:2 * self.width], self.xt[:, n % 2, k, :],
                                      self.w[:, :], start=True, stop=True).then_inc(self.s_mm, 1)

    def act(self, act, part):
        for n in (2 * part, 2 * part + 1):
            k0, count = self.groups[n]
            act.wait_ge(self.s_turn, n + 1)
            if n >= 2:
                act.wait_ge(self.s_mm, self.groups[n - 1][0])
            self.nc.scalar.activation(self.xt[:, n % 2, 0:count, :],
                                      self.turned[:, n % 2, 0:count * P].rearrange("p (k n) -> p k n", k=count),
                                      ACT.Copy).then_inc(self.s_xt, 1)

    def dve(self, dve, part):
        for pair in range(part * PPAIR, (part + 1) * PPAIR):
            dve.wait_ge(self.s_mm, pair + 1)
            self.finish(pair, self.out[:, pair % 4, 0:2 * self.width].rearrange("p (b f) -> p b f", b=2)
                        ).then_inc(self.s_done, 1)
        dve.wait_ge(self.s_done, (part + 1) * PPAIR)


def node_view(ap):
    return ap.rearrange("(p b) f -> p b f", p=P)



ATT = FEAT + 2 * HEADS


def first_nodes_phase(nc, io, g, dram):
    with ExitStack() as stack:
        m = Memory(nc, stack, "nodes1")
        x = m.sb("x", [P, BLKS, FEAT])
        acc = m.sb("acc", [P, BLKS, FEAT])
        stat = m.sb("stat", [P, 2, BLKS])
        tab = m.sb("tab", [P, BLKS, ATT])
        at = m.sb("at", [P, BLKS, HEADS])
        w = m.sb("w", [P, 2 * ATT])
        wt = m.sb("wt", [FEAT, P])
        attn = m.sb("attn", [FEAT, 2 * HEADS])
        small = m.ps("small", [P, 512])
        s_w, s_x, s_dve, s_var, s_std = m.sem("w_in"), m.sem("x_in"), m.sem("dve"), m.sem("var"), m.sem("std")
        s_acc = [m.sem(f"acc_in{k}") for k in range(PARTS)]
        s_small, s_ready, s_at, s_out, s_spread = (m.sem("small"), m.sem("ready"), m.sem("at"), m.sem("out"),
                                                   m.sem("spread"))
        prod = NodeProduct(nc, m, g, "", x, w, ATT,
                           lambda k, ps: nc.vector.tensor_copy(tab[:, 2 * k:2 * k + 2, :], ps))
        block = stack.enter_context(nc.Block())

        @block.sync
        def _(sp):
            sp.dma_start(w[:, :], io["w_node"]).then_inc(s_w, 16)
            sp.dma_start(wt[:, :], io["w_node_t"]).then_inc(s_w, 16)
            sp.dma_start(attn[:, :], io["attn"]).then_inc(s_w, 16)
            sp.dma_start(x[:, :, :], node_view(io["x"])).then_inc(s_x, 16)
            sp.wait_ge(s_ready, PARTS)
            sp.dma_start(node_view(dram["x1"]), x[:, :, :]).then_inc(s_out, 16)
            sp.wait_ge(s_at, PARTS)
            sp.dma_start(node_view(dram["table1"]), tab[:, :, :]).then_inc(s_out, 16)
            sp.wait_ge(s_out, 32)

        @block.gpsimd
        def _(pool):
            gather_nodes(pool, g, dram["run_sum"], acc, s_acc)
            scatter_nodes(pool, g, dram["at_dst1"], at, s_at, s_spread)
            pool.wait_ge(s_spread, 16 * BLKS)

        @block.vector
        def _(dve):
            step = stepper(dve, s_dve)
            dve.wait_ge(s_w, 48)
            dve.wait_ge(s_small, 1)
            step(nc.vector.tensor_copy(w[0:FEAT, FEAT:ATT], small[0:FEAT, 0:2 * HEADS]))
            step(nc.vector.tensor_copy(w[FEAT:P, ATT + FEAT:2 * ATT], small[FEAT:P, 0:2 * HEADS]))
            dve.wait_ge(s_x, 16)
            for part in range(PARTS + 1):
                if part < PARTS:
                    bl = blocks_of(part)
                    xp, ap = x[:, bl, :], acc[:, bl, :]
                    dve.wait_ge(s_acc[part], 16 * PBLK)
                    step(nc.vector.tensor_tensor(ap, ap, bc(g["root_in"][:, bl], FEAT), ALU.mult))
                    step(nc.vector.tensor_tensor(xp, xp, ap, ALU.add))
                    norm_dve(dve, nc, step, xp, ap, stat[:, :, bl], s_var, s_std, part + 1, s_ready)
                if part >= 1:
                    prod.dve(dve, part - 1)
                    bl = blocks_of(part - 1)
                    nc.vector.tensor_copy(at[:, bl, :], tab[:, bl, FEAT + HEADS:ATT]).then_inc(s_at, 1)

        @block.scalar
        def _(act):
            for part in range(PARTS):
                norm_act(act, nc, g, stat[:, :, blocks_of(part)], s_var, s_std, part + 1)
                prod.act(act, part)

        @block.tensor
        def _(pe):
            pe.wait_ge(s_w, 48)
            nc.tensor.matmul(small[:, 0:2 * HEADS], wt[:, :], attn[:, :], start=True, stop=True).then_inc(s_small, 1)
            for part in range(PARTS):
                pe.wait_ge(s_ready, part + 1)
                prod.pe(pe, part)



def every_chunk(eng, body):
    with eng.Fori(0, CHUNKS // 2 - 1) as c:
        for h in range(2):
            body(c, h, False)
    for h in range(2):
        body(CHUNKS // 2 - 1, h, True)


def softmax_scans(dve, nc, run, fall, grow, data, s_scan):
    for head in range(HEADS):
        factor = fall.rearrange("p j h -> p (j h)")[:, ds(head, STEP, HEADS)]
        with dve.Fori(0, 2) as k:
            for u in range(HDIM // 2):
                scan(nc, run, data, factor, head * HDIM + k * (HDIM // 2) + u, SROW, data.shape[2],
                     ALU.mult, ALU.add)
        last = scan(nc, run, grow, factor, FEAT + head, SROW, HEADS, ALU.mult, ALU.add, df=head)
    last.then_inc(s_scan, 1)


def attention_phase(nc, io, g, dram):
    with ExitStack() as stack:
        m = Memory(nc, stack, "edges2")
        idx = m.sb("idx", [P, 2, STEP], U32)
        rows = m.sb("rows", [P, 2, STEP, ATT])
        run = m.sb("run", [P, 2, STEP + 1, SROW])
        at = m.sb("at", [P, 2, STEP + 1, HEADS])
        start = m.sb("start", [P, ATT])
        attr = m.sb("attr", [P, 2, STEP // 8, P])
        w_edge = m.sb("w_edge", [P, 8 * HEADS])
        delta = m.sb("delta", [P, 2, STEP, HEADS])
        score = m.ps("score", [P, 2, 512])
        s_idx, s_rows, s_out, s_attr, s_at = ([m.sem(f"{n}{h}") for h in range(2)]
                                              for n in ("idx", "rows", "out", "attr", "at"))
        s_start, s_w, s_scan, s_dve, s_pass = m.sem("start"), m.sem("w"), m.sem("scanned"), m.sem("dve"), m.sem("passed")
        s_score, s_read, s_exp, s_expd = m.sem("score"), m.sem("score_read"), m.sem("to_exp"), m.sem("exp_done")
        block = stack.enter_context(nc.Block())
        store = dram["run_softmax"].rearrange("(p j) f -> p j f", p=P)
        spread = dram["at_dst1"][0:EPAD, :].rearrange("(p j) f -> p j f", p=P)
        STEPS = 11

        @block.sync
        def _(sp):
            sp.dma_start(w_edge[:, :], io["w_edge"]).then_inc(s_w, 16)
            for h in range(2):
                sp.sem_inc(s_out[h], 16)
                sp.dma_start(idx[:, h, :], io["src"][:, h * STEP:(h + 1) * STEP]).then_inc(s_idx[h], 16)
                sp.dma_start(attr[:, h, :, :], io["e16"][:, h * 8:(h + 1) * 8, :]).then_inc(s_attr[h], 16)

            def chunk(c, h, last):
                ch = 2 * c + h
                sp.wait_ge(s_scan, ch + 3)
                sp.dma_start(store[:, ds(ch * STEP, STEP), :], run[:, h, 1:STEP + 1, :]).then_inc(s_out[h], 16)
                if not last:
                    sp.dma_start(idx[:, h, :], io["src"][:, ds((ch + 2) * STEP, STEP)]).then_inc(s_idx[h], 16)
                    sp.dma_start(attr[:, h, :, :], io["e16"][:, ds((ch + 2) * 8, 8), :]).then_inc(s_attr[h], 16)

            every_chunk(sp, chunk)
            for h in range(2):
                sp.wait_ge(s_out[h], 16 + 16 * (CHUNKS // 2))

        @block.gpsimd
        def _(pool):
            pool.indirect_dma_start(out=start[:, :], out_offset=None, in_=dram["table1"],
                                    in_offset=bass.IndirectOffsetOnAxis(ap=g["dst0"][:, :], axis=0)
                                    ).then_inc(s_start, 16)
            with pool.Fori(0, CHUNKS // 2) as c:
                for h in range(2):
                    pool.wait_ge(s_idx[h], (c + 1) * 16)
                    pool.sem_inc(s_pass, 1)
                    pool.wait_ge(s_scan, 2 * c + h + 1)
                    pool.sem_inc(s_pass, 1)
                    gather_chunk(pool, nc, h, dram["table1"], idx, rows, ATT, s_rows[h])

        @block.vector
        def _(dve):
            dve.sem_inc(s_scan, 2)
            dve.sem_inc(s_read, 2)
            head = stepper(dve, s_dve)
            head(nc.vector.memset(run[:, 1, STEP, :], 0.0))
            dve.wait_ge(s_start, 16)
            head(nc.vector.tensor_copy(at[:, 1, STEP, :], start[:, FEAT + HEADS:ATT]))

            def chunk(c, h):
                ch = 2 * c + h
                step = stepper(dve, s_dve, 2 + ch * STEPS)
                keep = g["keep"][:, ds(ch * STEP, STEP)]
                fall, grow = delta[:, 0, :, :], delta[:, 1, :, :]
                dve.wait_ge(s_out[h], (c + 1) * 16)
                dve.wait_ge(s_scan, ch + 2)
                step(nc.vector.tensor_copy(run[:, h, 0, :], run[:, 1 - h, STEP, :]))
                step(nc.vector.tensor_copy(at[:, h, 0, :], at[:, 1 - h, STEP, :]))
                dve.wait_ge(s_at[h], (c + 1) * 16)
                for k in range(HEADS):
                    last = scan(nc, at[:, h, :, :], at[:, h, 1:STEP + 1, :], keep, k, HEADS, HEADS, ALU.mult, ALU.add)
                step(last)
                dve.wait_ge(s_rows[h], (c + 1) * 16 * STEP)
                step(nc.vector.tensor_tensor(fall, rows[:, h, :, FEAT:FEAT + HEADS], at[:, h, 1:STEP + 1, :], ALU.add))
                dve.wait_ge(s_score, ch + 1)
                nc.vector.tensor_tensor(fall, score[:, h, 0:STEP * HEADS].rearrange("p (j h) -> p j h", h=HEADS),
                                        fall, ALU.add).then_inc(s_read, 1)
                dve.wait_ge(s_read, ch + 3)
                step(nc.vector.scalar_tensor_tensor(out=grow, in0=fall, scalar=0.2, in1=fall, op0=ALU.mult, op1=ALU.max))
                step(nc.vector.tensor_scalar(fall, fall, 0.0, None, ALU.max))
                for k in range(HEADS):
                    last = scan(nc, run[:, h, :, :], fall, keep, SUMS + k, SROW, HEADS, ALU.mult, ALU.max, df=k)
                step(last)
                step(nc.vector.tensor_tensor(fall, run[:, h, 0:STEP, SUMS:SROW], run[:, h, 1:STEP + 1, SUMS:SROW],
                                             ALU.subtract))
                step(nc.vector.tensor_scalar(fall, fall, 0.0, None, ALU.min))
                nc.vector.tensor_tensor(grow, grow, run[:, h, 1:STEP + 1, SUMS:SROW], ALU.subtract).then_inc(s_exp, 1)
                dve.wait_ge(s_expd, ch + 1)
                step(nc.vector.tensor_tensor(fall, fall, bc(keep, HEADS), ALU.mult))
                h4 = rows[:, h, :, 0:FEAT].rearrange("p j (h d) -> p j h d", d=HDIM)
                step(nc.vector.tensor_tensor(h4, h4, bc(grow, HDIM), ALU.mult))
                assert step.count[0] == STEPS
                dve.sem_inc(s_pass, 1)
                softmax_scans(dve, nc, run[:, h, :, :], fall, grow, rows[:, h, :, :], s_scan)

            with dve.Fori(0, CHUNKS // 2) as c:
                for h in range(2):
                    chunk(c, h)

        @block.scalar
        def _(act):
            act.dma_start(at[:, 0, 1:STEP + 1, :], spread[:, 0:STEP, :]).then_inc(s_at[0], 16)

            def chunk(c, h, last):
                ch = 2 * c + h
                act.wait_ge(s_exp, ch + 1)
                nc.scalar.activation(delta[:, :, :, :], delta[:, :, :, :], ACT.Exp).then_inc(s_expd, 1)
                if not (last and h == 1):
                    act.dma_start(at[:, 1 - h, 1:STEP + 1, :], spread[:, ds((ch + 1) * STEP, STEP), :]
                                  ).then_inc(s_at[1 - h], 16)

            every_chunk(act, chunk)

        @block.tensor
        def _(pe):
            pe.wait_ge(s_w, 16)
            with pe.Fori(0, CHUNKS // 2) as c:
                for h in range(2):
                    pe.wait_ge(s_attr[h], (c + 1) * 16)
                    pe.wait_ge(s_read, 2 * c + h + 1)
                    for k in range(8):
                        last = nc.tensor.matmul(score[:, h, k * 8 * HEADS:(k + 1) * 8 * HEADS], attr[:, h, k, :],
                                                w_edge[:, :], start=True, stop=True)
                    last.then_inc(s_score, 1)


def attention_nodes_phase(nc, io, g, dram):
    with ExitStack() as stack:
        m = Memory(nc, stack, "nodes2")
        x = m.sb("x", [P, BLKS, FEAT])
        acc = m.sb("acc", [P, BLKS, SROW])
        y = m.sb("y", [P, BLKS, FEAT])
        hn = m.sb("h", [P, BLKS, ATT])
        inv = m.sb("inv", [P, BLKS, HEADS])
        stat = m.sb("stat", [P, 2, BLKS])
        gamma, beta = m.sb("gamma", [P, FEAT]), m.sb("beta", [P, FEAT])
        s_in, s_dve, s_var, s_std, s_x, s_out = (m.sem(n) for n in ("in", "dve", "var", "std", "x", "out"))
        s_acc = [m.sem(f"acc_in{k}") for k in range(PARTS)]
        block = stack.enter_context(nc.Block())

        @block.sync
        def _(sp):
            sp.dma_start(x[:, :, :], node_view(dram["x1"])).then_inc(s_in, 16)
            sp.dma_start(hn[:, :, :], node_view(dram["table1"])).then_inc(s_in, 16)
            sp.dma_start(gamma[:, :], io["ln_gamma"]).then_inc(s_in, 16)
            sp.dma_start(beta[:, :], io["ln_beta"]).then_inc(s_in, 16)
            for part in range(PARTS):
                sp.wait_ge(s_x, part + 1)
                sp.dma_start(node_view(dram["x2"])[:, blocks_of(part), :], x[:, blocks_of(part), :]).then_inc(s_out, 16)
            sp.wait_ge(s_out, 16 * PARTS)

        @block.gpsimd
        def _(pool):
            gather_nodes(pool, g, dram["run_softmax"], acc, s_acc)

        @block.vector
        def _(dve):
            step = stepper(dve, s_dve)
            dve.wait_ge(s_in, 64)
            for part in range(PARTS):
                bl = blocks_of(part)
                xp, yp, ap, ip = x[:, bl, :], y[:, bl, :], acc[:, bl, :], inv[:, bl, :]
                dve.wait_ge(s_acc[part], 16 * PBLK)
                step(nc.vector.tensor_scalar(ip, ap[:, :, FEAT:SUMS], 1e-8, None, ALU.add))
                step(nc.vector.reciprocal(ip, ip))
                step(nc.vector.tensor_tensor(ip, ip, bc(g["has"][:, bl], HEADS), ALU.mult))
                step(nc.vector.tensor_tensor(yp.rearrange("p b (h d) -> p b h d", d=HDIM),
                                             ap[:, :, 0:FEAT].rearrange("p b (h d) -> p b h d", d=HDIM),
                                             bc(ip, HDIM), ALU.mult))
                step(nc.vector.tensor_tensor(yp, yp, hn[:, bl, 0:FEAT], ALU.add))
                norm_dve(dve, nc, step, yp, ap[:, :, 0:FEAT], stat[:, :, bl], s_var, s_std, 2 * part + 1)
                step(nc.vector.tensor_tensor(yp, yp, over_blocks(gamma, PBLK), ALU.mult))
                step(nc.vector.tensor_tensor(yp, yp, over_blocks(beta, PBLK), ALU.add))
                step(nc.vector.tensor_tensor(xp, xp, yp, ALU.add))
                norm_dve(dve, nc, step, xp, ap[:, :, 0:FEAT], stat[:, :, bl], s_var, s_std, 2 * part + 2, s_x)

        @block.scalar
        def _(act):
            for part in range(PARTS):
                norm_act(act, nc, g, stat[:, :, blocks_of(part)], s_var, s_std, 2 * part + 1)
                norm_act(act, nc, g, stat[:, :, blocks_of(part)], s_var, s_std, 2 * part + 2)


def over_blocks(v, blocks=BLKS):
    return v[:, :].unsqueeze(1).to_broadcast([P, blocks, FEAT])



def network_extra(nc, m, io, g, dram):
    CP = STEP // 2
    SUBS = CP // 4
    attr = m.sb("attr", [P, 2, CP, P])
    out = m.sb("weight", [P, 2, CP, P])
    hid = [m.sb(f"hid{i}", [P, 2, 512]) for i in range(2)]
    w = [m.sb(f"fc{i}", [P, P]) for i in range(3)]
    bias = m.sb("bias", [P, 3])
    pre = [m.ps(f"pre{i}", [P, 2, 512]) for i in range(3)]
    s_w = m.sem("w")
    s_attr, s_out = ([m.sem(f"{n}{h}") for h in range(2)] for n in ("attr_in", "weight_out"))
    s_mm = [m.sem(f"mm{i}") for i in range(3)]
    s_act = [m.sem(f"act{i}") for i in range(3)]

    def act(act):
        for i in range(3):
            act.dma_start(w[i][:, :], io[f"fc{i + 1}"]).then_inc(s_w, 16)
        act.dma_start(bias[:, :], io["bfc"]).then_inc(s_w, 16)
        for h in range(2):
            act.dma_start(attr[:, h, :, :], io["e64"][:, h * CP:(h + 1) * CP, :]).then_inc(s_attr[h], 16)
            act.sem_inc(s_out[h], 16)
        for i in range(3):
            act.sem_inc(s_act[i], 2)
        act.wait_ge(s_w, 64)

        def chunk(c, h, last):
            ch = 2 * c + h
            flat = out[:, h, :, :].rearrange("p k n -> p (k n)")
            for q in range(SUBS + 2):
                if q < SUBS:
                    act.wait_ge(s_mm[0], ch * SUBS + q + 1)
                    act.wait_ge(s_mm[1], ch * SUBS + q + 1)
                    nc.scalar.activation(hid[0][:, q % 2, :], pre[0][:, q % 2, :], ACT.Silu, bias=bias[:, 0:1]
                                         ).then_inc(s_act[0], 1)
                if 1 <= q <= SUBS:
                    r = q - 1
                    act.wait_ge(s_mm[1], ch * SUBS + r + 3)
                    act.wait_ge(s_mm[2], ch * SUBS + r + 1)
                    nc.scalar.activation(hid[1][:, r % 2, :], pre[1][:, r % 2, :], ACT.Silu, bias=bias[:, 1:2]
                                         ).then_inc(s_act[1], 1)
                if q >= 2:
                    r = q - 2
                    if r == 0:
                        act.wait_ge(s_out[h], 16 * (c + 1))
                    act.wait_ge(s_mm[2], ch * SUBS + r + 3)
                    nc.scalar.activation(flat[:, r * 512:(r + 1) * 512], pre[2][:, r % 2, :], ACT.Identity,
                                         bias=bias[:, 2:3]).then_inc(s_act[2], 1)
            act.wait_ge(s_act[2], (ch + 1) * SUBS + 2)
            act.dma_start(dram["weight3"][:, ds(ch * CP, CP), :], out[:, h, :, :]).then_inc(s_out[h], 16)
            if not last:
                act.dma_start(attr[:, h, :, :], io["e64"][:, ds((ch + 2) * CP, CP), :]).then_inc(s_attr[h], 16)

        every_chunk(act, chunk)
        for h in range(2):
            act.wait_ge(s_out[h], 16 + 16 * (CHUNKS // 2))

    def pe(pe):
        for i in (1, 2):
            pe.sem_inc(s_mm[i], 2)
        pe.wait_ge(s_w, 64)
        with pe.Fori(0, CHUNKS // 2) as c:
            for h in range(2):
                ch = 2 * c + h
                pe.wait_ge(s_attr[h], (c + 1) * 16)
                flat = attr[:, h, :, :].rearrange("p k n -> p (k n)")
                for q in range(SUBS + 2):
                    if q < SUBS:
                        pe.wait_ge(s_act[0], ch * SUBS + q + 1)
                        nc.tensor.matmul(pre[0][:, q % 2, :], w[0][:, :], flat[:, q * 512:(q + 1) * 512],
                                         start=True, stop=True).then_inc(s_mm[0], 1)
                    if 1 <= q <= SUBS:
                        r = q - 1
                        pe.wait_ge(s_act[0], ch * SUBS + r + 3)
                        pe.wait_ge(s_act[1], ch * SUBS + r + 1)
                        nc.tensor.matmul(pre[1][:, r % 2, :], w[1][:, :], hid[0][:, r % 2, :],
                                         start=True, stop=True).then_inc(s_mm[1], 1)
                    if q >= 2:
                        r = q - 2
                        pe.wait_ge(s_act[1], ch * SUBS + r + 3)
                        pe.wait_ge(s_act[2], ch * SUBS + r + 1)
                        nc.tensor.matmul(pre[2][:, r % 2, :], w[2][:, :], hid[1][:, r % 2, :],
                                         start=True, stop=True).then_inc(s_mm[2], 1)

    return dict(dve_first=lambda dve: None, dve=lambda dve, ch: None, dve_last=lambda dve: None, act=act, pe=pe)



QALL = QROW + FEAT


def batchnorm_phase(nc, io, g, dram):
    with ExitStack() as stack:
        m = Memory(nc, stack, "nodes3")
        x = m.sb("x", [P, BLKS, FEAT])
        acc = m.sb("acc", [P, BLKS, FEAT])
        y = m.sb("y", [P, BLKS, FEAT])
        tab = m.sb("tab", [P, BLKS, QALL])
        stat = m.sb("stat", [P, 2, BLKS])
        w, b = m.sb("w", [P, P]), m.sb("b", [P, FEAT])
        w3, b3, bk = m.sb("w3", [P, 6 * FEAT]), m.sb("b3", [P, 3 * FEAT]), m.sb("bk", [P, FEAT])
        gamma, beta, mean, std = (m.sb(n, [P, FEAT]) for n in ("gamma", "beta", "mean", "std"))
        real = m.sb("real", [P, P])
        total = m.ps("total", [P, 2, 512])
        s_in, s_dve, s_var, s_std, s_x, s_out = (m.sem(n) for n in ("in", "dve", "var", "std", "x", "out"))
        s_sum, s_y, s_tot, s_mean, s_diff, s_sq, s_bstd, s_tab, s_spread = (
            m.sem(n) for n in ("sum", "y", "total", "mean", "diff", "square", "bstd", "tab", "spread"))
        s_acc = [m.sem(f"acc_in{k}") for k in range(PARTS)]
        prod = NodeProduct(nc, m, g, "y", acc, w, FEAT,
                           lambda k, ps: nc.vector.tensor_tensor(y[:, 2 * k:2 * k + 2, :], ps, over_blocks(b, 2), ALU.add))

        def finish(k, ps):
            bias = b3[:, :].unsqueeze(1).to_broadcast([P, 2, 3 * FEAT])
            nc.vector.tensor_tensor(tab[:, 2 * k:2 * k + 2, 0:2 * FEAT], ps[:, :, 0:2 * FEAT], bias[:, :, 0:2 * FEAT], ALU.add)
            return nc.vector.tensor_tensor(tab[:, 2 * k:2 * k + 2, QROW:QALL], ps[:, :, 2 * FEAT:], bias[:, :, 2 * FEAT:], ALU.add)

        prod3 = NodeProduct(nc, m, g, "q", x, w3, 3 * FEAT, finish, (prod.turned, prod.out, prod.xt))
        starts = sorted(set(range(0, REAL, PPAIR)) | set(range(REAL, BLKS, PPAIR)) | {REAL})
        runs = list(zip(starts, starts[1:] + [BLKS]))
        block = stack.enter_context(nc.Block())

        def total_of(pe, what, ready, half):
            for n, (b0, b1) in enumerate(runs):
                pe.wait_ge(ready, (b1 - 1) // PBLK + 1)
                last = nc.tensor.matmul(total[:, half, 0:(b1 - b0) * FEAT], g["ones"][:, :] if b0 < REAL else real[:, :],
                                        what[:, b0:b1, :].rearrange("p b f -> p (b f)"),
                                        start=n == 0, stop=n == len(runs) - 1, skip_group_check=True)
            last.then_inc(s_tot, 1)

        def by_feature(half):
            return total[:, half, 0:PPAIR * FEAT].rearrange("p (b f) -> p f b", f=FEAT)

        @block.sync
        def _(sp):
            sp.dma_start(x[:, :, :], node_view(dram["x2"])).then_inc(s_in, 16)
            for tile, name in ((w, "w2"), (b, "b2"), (gamma, "gamma2"), (beta, "beta2"), (w3, "w3"), (b3, "b3"), (bk, "bk")):
                sp.dma_start(tile[:, :], io[name]).then_inc(s_in, 16)
            sp.wait_ge(s_x, PARTS)
            sp.dma_start(node_view(dram["x3"]), x[:, :, :]).then_inc(s_out, 16)
            sp.wait_ge(s_tab, PARTS)
            sp.dma_start(node_view(dram["quer3"]), tab[:, :, 0:QROW]).then_inc(s_out, 16)
            sp.dma_start(node_view(dram["table3"]), tab[:, :, QROW:QALL]).then_inc(s_out, 16)
            sp.wait_ge(s_out, 48)

        @block.gpsimd
        def _(pool):
            gather_nodes(pool, g, dram["run_sum"], acc, s_acc)
            scatter_nodes(pool, g, dram["at_dst3"], tab[:, :, 0:QROW], s_tab, s_spread)
            pool.wait_ge(s_spread, 16 * BLKS)

        @block.vector
        def _(dve):
            step = stepper(dve, s_dve)
            step(nc.vector.tensor_scalar(real[:, :], g["ident"][:, P - 1:P].to_broadcast([P, P]), -1.0, 1.0, ALU.mult, ALU.add))
            dve.wait_ge(s_in, 128)
            for part in range(PARTS + 1):
                if part < PARTS:
                    bl = blocks_of(part)
                    dve.wait_ge(s_acc[part], 16 * PBLK)
                    step(nc.vector.tensor_tensor(acc[:, bl, :], acc[:, bl, :], bc(g["has"][:, bl], FEAT), ALU.mult))
                    nc.vector.tensor_tensor(acc[:, bl, :], acc[:, bl, :], x[:, bl, :], ALU.add).then_inc(s_sum, 1)
                if part >= 1:
                    prod.dve(dve, part - 1)
                    dve.sem_inc(s_y, 1)
            dve.wait_ge(s_tot, 1)
            step(nc.vector.reduce_sum(mean[:, :], by_feature(0), axis=AX.X))
            step(nc.vector.tensor_scalar(mean[:, :], mean[:, :], 1.0 / NODES, None, ALU.mult))
            for part in range(PARTS):
                bl = blocks_of(part)
                nc.vector.tensor_tensor(y[:, bl, :], y[:, bl, :], over_blocks(mean, PBLK), ALU.subtract).then_inc(s_diff, 1)
            dve.wait_ge(s_tot, 2)
            nc.vector.reduce_sum(std[:, :], by_feature(1), axis=AX.X).then_inc(s_mean, 1)
            dve.wait_ge(s_bstd, 1)
            step(nc.vector.reciprocal(std[:, :], std[:, :]))
            step(nc.vector.tensor_tensor(std[:, :], std[:, :], gamma[:, :], ALU.mult))
            for part in range(PARTS + 1):
                if part < PARTS:
                    bl = blocks_of(part)
                    xp, yp = x[:, bl, :], y[:, bl, :]
                    step(nc.vector.tensor_tensor(yp, yp, over_blocks(std, PBLK), ALU.mult))
                    step(nc.vector.tensor_tensor(yp, yp, over_blocks(beta, PBLK), ALU.add))
                    step(nc.vector.scalar_tensor_tensor(out=xp, in0=yp, scalar=0.0, in1=xp, op0=ALU.max, op1=ALU.add))
                    norm_dve(dve, nc, step, xp, yp, stat[:, :, bl], s_var, s_std, part + 1, s_x)
                if part >= 1:
                    prod3.dve(dve, part - 1)
                    bl = blocks_of(part - 1)
                    q, tmp = tab[:, bl, 0:FEAT], acc[:, bl, :]
                    step(nc.vector.tensor_scalar(q, q, float(HDIM) ** -0.5, None, ALU.mult))
                    step(nc.vector.tensor_tensor(tmp, q, over_blocks(bk, PBLK), ALU.mult))
                    nc.vector.reduce_sum(tab[:, bl, 2 * FEAT:QROW], tmp.rearrange("p b (h d) -> p b h d", d=HDIM),
                                         axis=AX.X).then_inc(s_tab, 1)

        @block.scalar
        def _(act):
            for part in range(PARTS):
                prod.act(act, part)
            for part in range(PARTS):
                bl = blocks_of(part)
                act.wait_ge(s_diff, part + 1)
                nc.scalar.activation(acc[:, bl, :], y[:, bl, :], ACT.Square).then_inc(s_sq, 1)
            act.wait_ge(s_mean, 1)
            nc.scalar.activation(std[:, :], std[:, :], ACT.Sqrt, scale=1.0 / NODES, bias=g["eps"][:, :]).then_inc(s_bstd, 1)
            for part in range(PARTS):
                norm_act(act, nc, g, stat[:, :, blocks_of(part)], s_var, s_std, part + 1)
                prod3.act(act, part)

        @block.tensor
        def _(pe):
            for part in range(PARTS):
                pe.wait_ge(s_sum, part + 1)
                prod.pe(pe, part)
            total_of(pe, y, s_y, 0)
            total_of(pe, acc, s_sq, 1)
            for part in range(PARTS):
                pe.wait_ge(s_x, part + 1)
                prod3.pe(pe, part)



def transformer_phase(nc, io, g, dram):
    CP = STEP // 2
    GROUPS = CP // 4
    with ExitStack() as stack:
        m = Memory(nc, stack, "edges4")
        idx = m.sb("idx", [P, 2, STEP], U32)
        rows = m.sb("rows", [P, 2, STEP, FEAT])
        run = m.sb("run", [P, 2, STEP + 1, SROW])
        at = m.sb("at", [P, 2, STEP + 1, QROW])
        start = m.sb("start", [P, QROW])
        weight = m.sb("weight", [P, 2, CP, P])
        ea = m.sb("ea", [P, COLS])
        w_kv = m.sb("w_kv", [P, 4 * FEAT])
        cut = m.sb("cut", [P, STEP])
        delta = m.sb("delta", [P, 2, 2, STEP, HEADS])
        times = m.sb("times", [P, STEP, HEADS])
        turned = m.ps("turned", [P, 2, 512])
        keys = m.ps("keys", [P, 2, 512])
        values = m.ps("values", [P, 2, 512])
        s_idx, s_rows, s_out, s_at, s_wt = ([m.sem(f"{n}{h}") for h in range(2)]
                                            for n in ("idx", "rows", "out", "at", "weight"))
        (s_w, s_start, s_scan, s_dve, s_pass, s_kv, s_turn, s_tp, s_mm, s_k, s_v, s_alpha, s_exp, s_expd) = (
            m.sem(n) for n in ("w", "start", "scanned", "dve", "passed", "kv", "turned", "times", "mm", "k_read",
                               "v_read", "alpha", "to_exp", "exp_done"))
        block = stack.enter_context(nc.Block())
        store = dram["run_softmax"].rearrange("(p j) f -> p j f", p=P)
        spread = dram["at_dst3"][0:EPAD, :].rearrange("(p j) f -> p j f", p=P)
        STEPS = 13

        @block.sync
        def _(sp):
            def load_idx(ch, h):
                sp.dma_start(idx[:, h, :], io["src"][:, ds(ch * STEP, STEP)]).then_inc(s_idx[h], 16)

            def load_weight(ch, h):
                sp.dma_start(weight[:, h, :, :], dram["weight3"][:, ds(ch * CP, CP), :]).then_inc(s_wt[h], 16)

            sp.dma_start(ea[:, :], io["ea"]).then_inc(s_w, 16)
            sp.dma_start(w_kv[:, :], io["w_kv"]).then_inc(s_w, 16)
            for h in range(2):
                sp.sem_inc(s_out[h], 16)
                load_idx(h, h)
                load_weight(h, h)

            def chunk(c, h, last):
                ch = 2 * c + h
                if not last:
                    sp.wait_ge(s_kv, ch + 1)
                    load_idx(ch + 2, h)
                    sp.wait_ge(s_mm, (ch + 1) * GROUPS)
                    load_weight(ch + 2, h)
                sp.wait_ge(s_scan, ch + 2)
                sp.dma_start(store[:, ds(ch * STEP, STEP), :], run[:, h, 1:STEP + 1, :]).then_inc(s_out[h], 16)

            every_chunk(sp, chunk)
            for h in range(2):
                sp.wait_ge(s_out[h], 16 + 16 * (CHUNKS // 2))

        @block.gpsimd
        def _(pool):
            pool.indirect_dma_start(out=start[:, :], out_offset=None, in_=dram["quer3"],
                                    in_offset=bass.IndirectOffsetOnAxis(ap=g["dst0"][:, :], axis=0)
                                    ).then_inc(s_start, 16)
            with pool.Fori(0, CHUNKS // 2) as c:
                for h in range(2):
                    pool.wait_ge(s_idx[h], (c + 1) * 16)
                    pool.sem_inc(s_pass, 1)
                    pool.wait_ge(s_turn, (2 * c + h + 1) * GROUPS)
                    pool.sem_inc(s_pass, 1)
                    gather_chunk(pool, nc, h, dram["table3"], idx, rows, FEAT, s_rows[h])

        @block.vector
        def _(dve):
            dve.sem_inc(s_k, 2)
            dve.sem_inc(s_tp, 2)
            head = stepper(dve, s_dve)
            head(nc.vector.memset(delta[:, :, :, :, :], 0.0))
            head(nc.vector.memset(run[:, :, :, :], 0.0))
            head(nc.vector.memset(run[:, 1, STEP, SUMS:SROW], -BIG))
            dve.wait_ge(s_start, 16)
            dve.wait_ge(s_w, 32)

            def spread_scans(ch, h, first, count):
                for f in range(first, first + count):
                    last = scan(nc, at[:, h, :, :], at[:, h, 1:STEP + 1, :], g["keep"][:, ds(ch * STEP, STEP)],
                                f, QROW, QROW, ALU.mult, ALU.add)
                return last

            def sum_scans(h, head):
                factor = delta[:, h, 0, :, :].rearrange("p j h -> p (j h)")[:, ds(head, STEP, HEADS)]
                data = run[:, h, 1:STEP + 1, :]
                for f in range(head * HDIM, (head + 1) * HDIM):
                    scan(nc, run[:, h, :, :], data, factor, f, SROW, SROW, ALU.mult, ALU.add)
                return scan(nc, run[:, h, :, :], delta[:, h, 1, :, :], factor, FEAT + head, SROW, HEADS,
                            ALU.mult, ALU.add, df=head)

            head(nc.vector.tensor_copy(at[:, 0, 0, :], start[:, :]))
            dve.wait_ge(s_at[0], 16)
            head(spread_scans(0, 0, 0, QROW))

            def chunk(c, h, end):
                ch = 2 * c + h
                step = stepper(dve, s_dve, 5 + ch * STEPS)
                keep = g["keep"][:, ds(ch * STEP, STEP)]
                fall, grow = delta[:, h, 0, :, :], delta[:, h, 1, :, :]
                ea4 = bc(ea[:, ds(ch * STEP, STEP)], HEADS)
                q = at[:, h, 1:STEP + 1, 0:FEAT]
                flat = weight[:, h, :, :].rearrange("p k n -> p (k n)")
                more = not (end and h == 1)
                dve.wait_ge(s_rows[h], (c + 1) * 16 * STEP)
                nc.vector.tensor_tensor(rows[:, h, :, :], rows[:, h, :, :], at[:, h, 1:STEP + 1, FEAT:2 * FEAT],
                                        ALU.add).then_inc(s_kv, 1)
                step(nc.vector.tensor_copy(run[:, 1 - h, 0, 0:SUMS], run[:, h, STEP, 0:SUMS]))
                if more:
                    step(nc.vector.tensor_copy(at[:, 1 - h, 0, :], at[:, h, STEP, :]))
                step(nc.vector.tensor_scalar(cut[:, :], keep, BIG, -BIG, ALU.mult, ALU.add))
                dve.wait_ge(s_wt[h], (c + 1) * 16)
                for n in range(GROUPS + 1):
                    if n < GROUPS:
                        dve.wait_ge(s_turn, (ch + 2) * GROUPS + n + 1)
                        nc.vector.tensor_tensor(flat[:, n * 512:(n + 1) * 512], turned[:, n % 2, :],
                                                flat[:, n * 512:(n + 1) * 512], ALU.mult).then_inc(s_tp, 1)
                    if n < HEADS:
                        last = sum_scans(1 - h, n)
                        if n == HEADS - 1:
                            last.then_inc(s_scan, 1)
                    elif more:
                        if n == HEADS:
                            dve.wait_ge(s_at[1 - h], (c + 1 + h) * 16)
                        rest = -(-QROW // (GROUPS + 1 - HEADS))
                        first = (n - HEADS) * rest
                        last = spread_scans(ch + 1, 1 - h, first, min(rest, QROW - first))
                    if n >= 1:
                        i = n - 1
                        dve.wait_ge(s_mm, ch * GROUPS + i + 1)
                        q8 = at[:, h, 1 + 8 * i:9 + 8 * i, 0:FEAT]
                        nc.vector.tensor_tensor(q8, keys[:, i % 2, :].rearrange("p (j f) -> p j f", j=8), q8,
                                                ALU.mult).then_inc(s_k, 1)
                if more:
                    step(last)
                step(nc.vector.tensor_copy(run[:, h, 0, SUMS:SROW], run[:, 1 - h, STEP, SUMS:SROW]))
                dve.wait_ge(s_k, (ch + 1) * GROUPS + 2)
                step(nc.vector.reduce_sum(fall, q.rearrange("p j (h d) -> p j h d", d=HDIM), axis=AX.X))
                step(nc.vector.tensor_tensor(fall, fall, ea4, ALU.mult))
                nc.vector.tensor_tensor(fall, fall, at[:, h, 1:STEP + 1, 2 * FEAT:QROW], ALU.add).then_inc(s_alpha, 1)
                dve.wait_ge(s_alpha, ch + 1)
                dve.wait_ge(s_out[h], (c + 1) * 16)
                for k in range(HEADS):
                    last = scan(nc, run[:, h, :, :], fall, cut[:, :], SUMS + k, SROW, HEADS, ALU.add, ALU.max, df=k)
                step(last)
                peak, before = run[:, h, 1:STEP + 1, SUMS:SROW], run[:, h, 0:STEP, SUMS:SROW]
                step(nc.vector.tensor_tensor(grow, fall, peak, ALU.subtract))
                step(nc.vector.tensor_tensor(fall, before, peak, ALU.subtract))
                nc.vector.tensor_scalar(fall, fall, 0.0, None, ALU.min).then_inc(s_exp, 1)
                dve.wait_ge(s_expd, ch + 1)
                step(nc.vector.tensor_tensor(fall, fall, bc(keep, HEADS), ALU.mult))
                step(nc.vector.tensor_tensor(times[:, :, :], grow, ea4, ALU.mult))
                dve.wait_ge(s_v, (ch + 1) * GROUPS + 2)
                h4 = run[:, h, 1:STEP + 1, 0:FEAT].rearrange("p j (h d) -> p j h d", d=HDIM)
                step(nc.vector.tensor_tensor(h4, h4, bc(times[:, :, :], HDIM), ALU.mult))
                dve.sem_inc(s_pass, 1)
                assert step.count[0] == STEPS or not more, step.count

            every_chunk(dve, chunk)
            tail = stepper(dve, s_dve, 5 + CHUNKS * STEPS - 2)
            tail(nc.vector.tensor_copy(run[:, 1, 0, 0:SUMS], run[:, 0, STEP, 0:SUMS]))
            for head_ in range(HEADS):
                last = sum_scans(1, head_)
            last.then_inc(s_scan, 1)

        @block.scalar
        def _(act):
            act.sem_inc(s_v, 2)
            for h in range(2):
                act.dma_start(at[:, h, 1:STEP + 1, :], spread[:, h * STEP:(h + 1) * STEP, :]).then_inc(s_at[h], 16)

            def chunk(c, h, last):
                ch = 2 * c + h
                act.wait_ge(s_out[h], (c + 1) * 16)
                for i in range(GROUPS):
                    act.wait_ge(s_mm, ch * GROUPS + i + 1)
                    nc.scalar.activation(run[:, h, 1 + 8 * i:9 + 8 * i, 0:FEAT],
                                         values[:, i % 2, :].rearrange("p (j f) -> p j f", j=8),
                                         ACT.Copy).then_inc(s_v, 1)
                if not last:
                    act.wait_ge(s_alpha, ch + 1)
                    act.dma_start(at[:, h, 1:STEP + 1, :], spread[:, ds((ch + 2) * STEP, STEP), :]).then_inc(s_at[h], 16)
                act.wait_ge(s_exp, ch + 1)
                nc.scalar.activation(delta[:, h, :, :, :], delta[:, h, :, :, :], ACT.Exp).then_inc(s_expd, 1)

            every_chunk(act, chunk)

        @block.tensor
        def _(pe):
            pe.sem_inc(s_turn, 2 * GROUPS)
            pe.wait_ge(s_w, 32)
            with pe.Fori(0, CHUNKS // 2) as c:
                for h in range(2):
                    ch = 2 * c + h
                    pe.wait_ge(s_kv, ch + 1)
                    for n in range(GROUPS + 1):
                        if n < GROUPS:
                            pe.wait_ge(s_tp, ch * GROUPS + n + 1)
                            for k in range(4):
                                j = 2 * (4 * n + k)
                                last = nc.tensor.transpose(turned[:, n % 2, k * P:(k + 1) * P],
                                                           rows[:, h, j:j + 2, :].rearrange("p a f -> p (a f)"),
                                                           g["ident"][:, :])
                            last.then_inc(s_turn, 1)
                        if n >= 1:
                            pe.wait_ge(s_tp, ch * GROUPS + n + 2)
                            i = n - 1
                            pe.wait_ge(s_k, ch * GROUPS + i + 1)
                            pe.wait_ge(s_v, ch * GROUPS + i + 1)
                            for k in range(4):
                                for bank, part in ((keys, 0), (values, 1)):
                                    last = nc.tensor.matmul(bank[:, i % 2, k * P:(k + 1) * P], weight[:, h, 4 * i + k, :],
                                                            w_kv[:, part * P:(part + 1) * P], start=True, stop=True)
                            last.then_inc(s_mm, 1)


def result_phase(nc, io, g, dram, out):
    with ExitStack() as stack:
        m = Memory(nc, stack, "nodes4")
        x = m.sb("x", [P, BLKS, FEAT])
        acc = m.sb("acc", [P, BLKS, SROW])
        y = m.sb("y", [P, BLKS, FEAT])
        tmp = m.sb("tmp", [P, BLKS, FEAT])
        inv = m.sb("inv", [P, BLKS, HEADS])
        stat = m.sb("stat", [P, 2, BLKS])
        w, b, bv = m.sb("w", [P, P]), m.sb("b", [P, FEAT]), m.sb("bv", [P, FEAT])
        s_in, s_dve, s_var, s_std, s_x, s_out, s_y = (m.sem(n) for n in ("in", "dve", "var", "std", "x", "out", "y"))
        s_acc = [m.sem(f"acc_in{k}") for k in range(PARTS)]
        prod = NodeProduct(nc, m, g, "", y, w, FEAT,
                           lambda k, ps: nc.vector.tensor_tensor(tmp[:, 2 * k:2 * k + 2, :], ps, over_blocks(b, 2), ALU.add))
        block = stack.enter_context(nc.Block())

        @block.sync
        def _(sp):
            sp.dma_start(x[:, :, :], node_view(dram["x3"])).then_inc(s_in, 16)
            for tile, name in ((w, "w_proj"), (b, "b_proj"), (bv, "bv")):
                sp.dma_start(tile[:, :], io[name]).then_inc(s_in, 16)
            sp.wait_ge(s_x, PARTS)
            whole = NODES // BLKS
            sp.dma_start(out[0:whole * BLKS, :].rearrange("(p b) f -> p b f", b=BLKS), x[0:whole, :, :]).then_inc(s_out, 16)
            left = NODES - whole * BLKS
            sp.dma_start(out[whole * BLKS:NODES, :].rearrange("(p b) f -> p b f", p=1), x[whole:whole + 1, 0:left, :]
                         ).then_inc(s_out, 16)
            sp.wait_ge(s_out, 32)

        @block.gpsimd
        def _(pool):
            gather_nodes(pool, g, dram["run_softmax"], acc, s_acc)

        @block.vector
        def _(dve):
            step = stepper(dve, s_dve)
            heads = lambda t: t.rearrange("p b (h d) -> p b h d", d=HDIM)
            dve.wait_ge(s_in, 64)
            for part in range(PARTS + 1):
                if part < PARTS:
                    bl = blocks_of(part)
                    ip, yp, tp, num, den = inv[:, bl, :], y[:, bl, :], tmp[:, bl, :], acc[:, bl, 0:FEAT], acc[:, bl, FEAT:SUMS]
                    dve.wait_ge(s_acc[part], 16 * PBLK)
                    step(nc.vector.tensor_scalar(ip, den, 1e-16, None, ALU.add))
                    step(nc.vector.reciprocal(ip, ip))
                    step(nc.vector.tensor_tensor(ip, ip, bc(g["has"][:, bl], HEADS), ALU.mult))
                    step(nc.vector.tensor_tensor(heads(yp), heads(num), bc(ip, HDIM), ALU.mult))
                    step(nc.vector.tensor_tensor(ip, ip, den, ALU.mult))
                    step(nc.vector.tensor_copy(tp, over_blocks(bv, PBLK)))
                    step(nc.vector.tensor_tensor(heads(tp), heads(tp), bc(ip, HDIM), ALU.mult))
                    nc.vector.tensor_tensor(yp, yp, tp, ALU.add).then_inc(s_y, 1)
                if part >= 1:
                    prod.dve(dve, part - 1)
                    bl = blocks_of(part - 1)
                    xp = x[:, bl, :]
                    step(nc.vector.tensor_tensor(xp, xp, tmp[:, bl, :], ALU.add))
                    norm_dve(dve, nc, step, xp, acc[:, bl, 0:FEAT], stat[:, :, bl], s_var, s_std, part, s_x)

        @block.scalar
        def _(act):
            for part in range(PARTS):
                prod.act(act, part)
                norm_act(act, nc, g, stat[:, :, blocks_of(part)], s_var, s_std, part + 1)

        @block.tensor
        def _(pe):
            for part in range(PARTS):
                pe.wait_ge(s_y, part + 1)
                prod.pe(pe, part)



def program(nc, io, out, upto):
    dram = {}
    for name, shape in dict(table0=(NPAD, FEAT), table1=(NPAD, ATT), table2=(NPAD, FEAT), table3=(NPAD, FEAT),
                            quer3=(NPAD, QROW), x1=(NPAD, FEAT), x2=(NPAD, FEAT), x3=(NPAD, FEAT),
                            run_sum=(EPAD, FEAT), run_softmax=(EPAD, SROW),
                            at_dst1=(EPAD + NPAD, HEADS), at_dst3=(EPAD + NPAD, QROW),
                            weight3=(P, COLS // 2, P), count_src=(NPAD,), count_dst=(NPAD,)).items():
        dram[name] = nc.dram_tensor(name, shape, F32, kind="Internal").ap()
    with ExitStack() as stack:
        m = Memory(nc, stack, "g")
        g = dict(iota=m.sb("iota", [P, P, GRP], BF16), rownum=m.sb("rownum", [P, P]), nodenum=m.sb("nodenum", [P, BLKS]),
                 edge0=m.sb("edge0", [P, 1]), eps=m.sb("eps", [P, 1]), ones=m.sb("ones", [P, P]),
                 ident=m.sb("ident", [P, P]), below=m.sb("below", [P, P]),
                 keep=m.sb("keep", [P, COLS]), through=m.sb("through", [P, 1]),
                 fixrow=m.sb("fixrow", [P, 1], U32), dst0=m.sb("dst0", [P, 1], U32),
                 has=m.sb("has", [P, BLKS]), lastrow=m.sb("lastrow", [P, BLKS], U32),
                 firstrow=m.sb("firstrow", [P, BLKS], U32), root_in=m.sb("root_in", [P, BLKS]))
        setup_phase(nc, io, g, dram)
        sum_phase(nc, io, g, dram, "edges1", dram["table0"], first_extra)
        segments_phase(nc, io, g, dram)
        carry_phase(nc, g, dram, "carry1", False)
        first_nodes_phase(nc, io, g, dram)
        rest(nc, io, g, dram, out, upto)


def store_phase(nc, src, out):
    with ExitStack() as stack:
        m = Memory(nc, stack, "store")
        s = m.sem("out")
        block = stack.enter_context(nc.Block())

        @block.sync
        def _(sp):
            sp.dma_start(out, src[0:NODES, 0:FEAT]).then_inc(s, 16)
            sp.wait_ge(s, 16)


def rest(nc, io, g, dram, out, upto):
    attention_phase(nc, io, g, dram)
    carry_phase(nc, g, dram, "carry2", True)
    attention_nodes_phase(nc, io, g, dram)
    if upto == 2:
        return store_phase(nc, dram["x2"], out)
    sum_phase(nc, io, g, dram, "edges3", dram["x2"], network_extra)
    carry_phase(nc, g, dram, "carry3", False)
    batchnorm_phase(nc, io, g, dram)
    if upto == 3:
        return store_phase(nc, dram["x3"], out)
    transformer_phase(nc, io, g, dram)
    carry_phase(nc, g, dram, "carry4", True)
    result_phase(nc, io, g, dram, out)


def kernel(**inputs):
    import concourse.bacc as bacc
    from concourse.bass_utils import run_bass_kernel_spmd as run

    v = {k: np.asarray(a) for k, a in inputs.items()}

    def edges(a, cols=COLS, fill=0):
        flat = np.full((EPAD,) + a.shape[1:], fill, a.dtype)
        flat[:EDGES] = a
        wide = np.full((P, cols) + a.shape[1:], fill, a.dtype)
        wide[:, :COLS] = flat.reshape((P, COLS) + a.shape[1:])
        return wide

    def diagonal(a, n):
        k, w = a.shape
        d = np.zeros((n * k, n * w), a.dtype)
        for i in range(n):
            d[i * k:(i + 1) * k, i * w:(i + 1) * w] = a
        return d

    def rows(a):
        return np.ascontiguousarray(np.broadcast_to(a.reshape(1, -1), (P, a.size)))

    x = np.zeros((NPAD, FEAT), v["x"].dtype)
    x[:NODES] = v["x"]
    w_node = np.zeros((FEAT, ATT), np.float32)
    w_node[:, :FEAT] = v["L1_gnn_W_node"]
    attn = np.zeros((FEAT, 2 * HEADS), np.float32)
    for h in range(HEADS):
        attn[h * HDIM:(h + 1) * HDIM, h] = v["L1_gnn_attn_src"][h]
        attn[h * HDIM:(h + 1) * HDIM, HEADS + h] = v["L1_gnn_attn_dst"][h]
    w3 = np.zeros((FEAT, 3 * FEAT), np.float32)
    w3[:, :FEAT], w3[:, FEAT:2 * FEAT], w3[:, 2 * FEAT:] = v["L3_gnn_Wq"], v["L3_gnn_W_dst"], v["L3_gnn_W_src"]
    b3 = np.zeros((3 * FEAT,), np.float32)
    b3[:FEAT], b3[2 * FEAT:] = v["L3_gnn_bq"], v["L3_gnn_b_src"]
    e16 = edges(v["edge_attr_16"]).reshape(P, COLS // 8, 8, EDIM).transpose(2, 3, 1, 0).reshape(P, COLS // 8, P)
    e64 = edges(v["edge_attr_64"]).reshape(P, COLS // 2, 2, FEAT).transpose(2, 3, 1, 0).reshape(P, COLS // 2, P)
    arrays = dict(
        x=x, src=edges(v["src"], COLS + 2 * STEP, NPAD - 1), dst=edges(v["dst"], COLS, NPAD - 1),
        e16=e16, e64=e64, ea=edges(v["edge_weight1"][:, 0]),
        w_node=diagonal(w_node, 2), w_node_t=np.concatenate([v["L1_gnn_W_node"].T] * 2, axis=1), attn=attn,
        w_edge=diagonal(v["L1_gnn_W_edge"], 8), ln_gamma=rows(v["L1_gnn_ln_gamma"]), ln_beta=rows(v["L1_gnn_ln_beta"]),
        w2=diagonal(v["L2_gnn_W"], 2), b2=rows(v["L2_gnn_b"]), gamma2=rows(v["L2_gnn_gamma"]), beta2=rows(v["L2_gnn_beta"]),
        w3=diagonal(w3, 2), b3=rows(b3), bk=rows(v["L3_gnn_b_kv"][:FEAT]), bv=rows(v["L3_gnn_b_kv"][FEAT:]),
        fc1=diagonal(v["L3_gnn_W_fc1"], 2), fc2=diagonal(v["L3_gnn_W_fc2"], 2), fc3=diagonal(v["L3_gnn_W_fc3"], 2),
        bfc=np.stack([np.concatenate([v[f"L3_gnn_b_fc{i}"]] * 2) for i in (1, 2, 3)], axis=1),
        w_kv=np.concatenate([diagonal(v["L3_gnn_W_kv"][:, :FEAT], 2), diagonal(v["L3_gnn_W_kv"][:, FEAT:], 2)], axis=1), w_proj=diagonal(v["L3_gnn_W_proj"], 2), b_proj=rows(v["L3_gnn_b_proj"]),
    )
    arrays = {k: np.ascontiguousarray(a) for k, a in arrays.items()}
    nc = bacc.Bacc("TRN2", target_bir_lowering=False, num_devices=1)
    io = {k: nc.dram_tensor(f"in_{k}", a.shape, mybir.dt.from_np(a.dtype), kind="ExternalInput").ap()
          for k, a in arrays.items()}
    io["src"] = io["src"].bitcast(U32)
    out = nc.dram_tensor("out", (NODES, FEAT), F32, kind="ExternalOutput").ap()
    program(nc, io, out, 4)
    r = run(nc, [{f"in_{k}": a for k, a in arrays.items()}], core_ids=[0])
    return r.results[0]["out"]
```

```python
from contextlib import ExitStack

import numpy as np

import concourse.bass as bass
from concourse import mybir

F32 = mybir.dt.float32
BF16 = mybir.dt.bfloat16
I32 = mybir.dt.int32
U32 = mybir.dt.uint32
ALU = mybir.AluOpType
ACT = mybir.ActivationFunctionType
AX = mybir.AxisListType

P = 128
NODES, EDGES, FEAT, HEADS, EDIM = 12500, 212500, 64, 4, 16
HDIM = FEAT // HEADS
BLKS = -(-NODES // P)
NPAD = BLKS * P
STEP = 64
COLS = -(-EDGES // (P * 2 * STEP)) * 2 * STEP
EPAD = COLS * P
CHUNKS = COLS // STEP
PARTS = 7
PBLK = BLKS // PARTS
PPAIR = PBLK // 2
PAIRS = BLKS // 2
REAL = NODES - (P - 1) * BLKS
SROW = FEAT + 2 * HEADS
SUMS = FEAT + HEADS
QROW = 2 * FEAT + HEADS
GRP = 32
GPC = STEP // GRP
OWN = GRP * 11 // 16
HI = NPAD // P
BIG = 1.0e30
LN_EPS = 1e-5
ds = bass.ds


class Memory:

    def __init__(self, nc, stack, tag):
        self.nc, self.stack, self.tag, self.sems = nc, stack, tag, []
        stack.callback(self.clear)

    def clear(self):
        if self.sems:
            self.nc.clear_and_free_semaphores(self.sems)
            self.nc.all_engine_barrier(sem_only=True)

    def sb(self, name, shape, dtype=F32):
        return self.stack.enter_context(self.nc.sbuf_tensor(f"{self.tag}_{name}", shape, dtype))

    def ps(self, name, shape, dtype=F32):
        return self.stack.enter_context(self.nc.psum_tensor(f"{self.tag}_{name}", shape, dtype))

    def sem(self, name):
        self.sems.append(self.nc.alloc_semaphore(f"{self.tag}_{name}"))
        return self.sems[-1]


def stepper(eng, sem, base=0):
    count = [0]

    def step(ins):
        count[0] += 1
        ins.then_inc(sem, 1)
        eng.wait_ge(sem, base + count[0])

    step.count = count
    return step


def bc(ap, n):
    return ap.unsqueeze(len(ap.shape)).to_broadcast([*ap.shape, n])



def onehot_rows(dve, nc, ch, k, hist, made, used):
    s = k % 2
    dve.wait_ge(used, ch * GPC + k + 1)
    cols = ds(ch * STEP + k * GRP, GRP)
    nc.vector.tensor_tensor(hist["oh_hi"][:, s, :, :], hist["iota"][:, 0:HI, :],
                            hist["hi"][:, cols].unsqueeze(1).to_broadcast([P, HI, GRP]), ALU.is_equal)
    own = hist["own"]
    nc.vector.tensor_tensor(hist["oh_lo"][:, s, :, 0:own], hist["iota"][:, :, 0:own],
                            hist["lo"][:, ds(ch * STEP + k * GRP, own)].unsqueeze(1).to_broadcast([P, P, own]),
                            ALU.is_equal).then_inc(made, 1)


def sign_rows(act, nc, g, ch, k, hist, made, used):
    s = k % 2
    act.wait_ge(used, ch * GPC + k + 1)
    for u in range(hist["own"], GRP):
        last = nc.scalar.activation(hist["oh_lo"][:, s, :, u], g["rownum"][:, :], ACT.Sign,
                                    bias=hist["minus_lo"][:, ds(ch * STEP + k * GRP + u, 1)])
    last.then_inc(made, 1)


def onehot_products(pe, nc, ch, k, hist, made, used, made_signs=None):
    s = k % 2
    pe.wait_ge(made, ch * GPC + k + 1)
    for u in range(GRP):
        if u == hist["own"]:
            pe.wait_ge(made_signs, ch * GPC + k + 1)
        c0 = 0 if u < hist["own"] else P
        last = nc.tensor.matmul(hist["count"][0:HI, c0:c0 + P], hist["oh_hi"][:, s, :, u], hist["oh_lo"][:, s, :, u],
                                start=False, stop=False, skip_group_check=True)
    last.then_inc(used, 1)


def split_number(step, nc, number, part, hist):
    step(nc.vector.tensor_single_scalar(part[:, :], number, 7, ALU.logical_shift_right))
    step(nc.vector.tensor_copy(hist["hi"][:, :], part[:, :]))
    step(nc.vector.tensor_single_scalar(part[:, :], number, P - 1, ALU.bitwise_and))
    step(nc.vector.tensor_copy(hist["lo"][:, :], part[:, :]))



def setup_phase(nc, io, g, dram):
    with ExitStack() as stack:
        m = Memory(nc, stack, "setup")
        hist = dict(oh_hi=m.sb("oh_hi", [P, 2, HI, GRP], BF16), oh_lo=m.sb("oh_lo", [P, 2, P, GRP], BF16),
                    iota=g["iota"], hi=m.sb("hi", [P, COLS], BF16), lo=m.sb("lo", [P, COLS], BF16),
                    minus_lo=m.sb("minus_lo", [P, COLS]), count=m.ps("count", [P, 512]), own=OWN)
        src = m.sb("src", [P, COLS], U32)
        part = m.sb("part", [P, COLS], U32)
        number = m.sb("number", [P, 1])
        zero = m.sb("zero", [P, 2 * P], BF16)
        counts = m.sb("counts", [P, P])
        signs = m.sb("signs", [P, P + 1])
        deg = m.sb("deg", [P, BLKS])
        root = m.sb("root", [P, BLKS])
        x = m.sb("x", [P, BLKS, FEAT])
        s_src, s_x = m.sem("src_in"), m.sem("x_in")
        s_const, s_zero, s_dve = m.sem("constants"), m.sem("zeros"), m.sem("dve")
        s_made, s_used, s_open = m.sem("onehots_made"), m.sem("onehots_used"), m.sem("count_open")
        s_all, s_counts, s_deg_out, s_deg_in = m.sem("count_done"), m.sem("counts"), m.sem("deg_out"), m.sem("deg_in")
        s_signs, s_low = m.sem("signs_made"), m.sem("low_parts")
        s_max, s_root, s_table, s_store = m.sem("deg_max"), m.sem("root"), m.sem("table"), m.sem("stored")
        block = stack.enter_context(nc.Block())

        @block.sync
        def _(sp):
            sp.dma_start(src[:, :], io["src"][:, 0:COLS]).then_inc(s_src, 16)
            sp.dma_start(x[:, :, :], io["x"].rearrange("(p b) f -> p b f", p=P)).then_inc(s_x, 16)
            sp.wait_ge(s_counts, 1)
            sp.dma_start(dram["count_src"].rearrange("(h l) -> h l", l=P), counts[0:HI, :]).then_inc(s_deg_out, 16)
            sp.wait_ge(s_deg_out, 16)
            sp.dma_start(deg[:, :], dram["count_src"].rearrange("(p b) -> p b", p=P)).then_inc(s_deg_in, 16)
            for part in range(PARTS):
                sp.wait_ge(s_table, part + 1)
                sp.dma_start(node_view(dram["table0"])[:, blocks_of(part), :], x[:, blocks_of(part), :]).then_inc(s_store, 16)
            sp.wait_ge(s_store, 16 * PARTS)

        @block.gpsimd
        def _(pool):
            pool.iota(g["iota"][:, :, :], [[1, P], [0, GRP]], base=0, channel_multiplier=0,
                      allow_small_or_imprecise_dtypes=True).then_inc(s_const, 1)
            pool.iota(g["rownum"][:, :], [[1, P]], base=0, channel_multiplier=0,
                      allow_small_or_imprecise_dtypes=True).then_inc(s_const, 1)
            pool.iota(g["nodenum"][:, :], [[1, BLKS]], base=0, channel_multiplier=BLKS,
                      allow_small_or_imprecise_dtypes=True).then_inc(s_const, 1)
            pool.iota(g["edge0"][:, :], [[1, 1]], base=-1, channel_multiplier=COLS,
                      allow_small_or_imprecise_dtypes=True).then_inc(s_const, 1)
            pool.iota(number[:, :], [[1, 1]], base=0, channel_multiplier=1,
                      allow_small_or_imprecise_dtypes=True).then_inc(s_const, 1)

        @block.vector
        def _(dve):
            step = stepper(dve, s_dve)
            dve.sem_inc(s_used, 2)
            nc.vector.memset(zero[:, :], 0.0).then_inc(s_zero, 1)
            nc.vector.memset(g["eps"][:, :], LN_EPS)
            step(nc.vector.memset(g["ones"][:, :], 1.0))
            dve.wait_ge(s_const, 5)
            step(nc.vector.tensor_scalar(g["ident"][:, :], g["rownum"][:, :], number[:, :], None, ALU.is_equal))
            step(nc.vector.tensor_scalar(g["below"][:, :], g["rownum"][:, :], number[:, :], None, ALU.is_gt))
            dve.wait_ge(s_src, 16)
            split_number(step, nc, src[:, :], part, hist)
            nc.vector.tensor_scalar(hist["minus_lo"][:, :], hist["lo"][:, :], -1.0, 0.5, ALU.mult, ALU.add).then_inc(s_low, 1)
            with dve.Fori(0, CHUNKS) as ch:
                for k in range(GPC):
                    onehot_rows(dve, nc, ch, k, hist, s_made, s_used)
            dve.wait_ge(s_all, 1)
            step(nc.vector.tensor_copy(signs[0:HI, 1:P + 1], hist["count"][0:HI, P:2 * P]))
            step(nc.vector.tensor_scalar(signs[0:HI, 0:1], signs[0:HI, P:P + 1], -1.0, None, ALU.mult))
            step(nc.vector.tensor_tensor(counts[0:HI, :], signs[0:HI, 1:P + 1], signs[0:HI, 0:P], ALU.subtract))
            nc.vector.scalar_tensor_tensor(out=counts[0:HI, :], in0=counts[0:HI, :], scalar=0.5,
                                           in1=hist["count"][0:HI, 0:P], op0=ALU.mult, op1=ALU.add).then_inc(s_counts, 1)
            dve.wait_ge(s_deg_in, 16)
            nc.vector.tensor_scalar(deg[:, :], deg[:, :], 1.0, None, ALU.max).then_inc(s_max, 1)
            dve.wait_ge(s_root, 1)
            step(nc.vector.reciprocal(root[:, :], root[:, :]))
            dve.wait_ge(s_x, 16)
            for seventh in range(PARTS):
                bl = blocks_of(seventh)
                nc.vector.tensor_tensor(x[:, bl, :], x[:, bl, :], bc(root[:, bl], FEAT), ALU.mult).then_inc(s_table, 1)

        @block.scalar
        def _(act):
            act.wait_ge(s_const, 5)
            act.wait_ge(s_low, 1)
            with act.Fori(0, CHUNKS) as ch:
                for k in range(GPC):
                    sign_rows(act, nc, g, ch, k, hist, s_signs, s_used)
            act.wait_ge(s_max, 1)
            nc.scalar.activation(root[:, :], deg[:, :], ACT.Sqrt).then_inc(s_root, 1)

        @block.tensor
        def _(pe):
            pe.wait_ge(s_zero, 1)
            nc.tensor.matmul(hist["count"][0:HI, 0:2 * P], zero[:, 0:HI], zero[:, :], start=True, stop=False,
                             skip_group_check=True)
            with pe.Fori(0, CHUNKS) as ch:
                for k in range(GPC):
                    onehot_products(pe, nc, ch, k, hist, s_made, s_used, s_signs)
            nc.tensor.matmul(hist["count"][0:HI, 0:2 * P], zero[:, 0:HI], zero[:, :], start=False, stop=True,
                             skip_group_check=True).then_inc(s_all, 1)



def gather_chunk(pool, nc, slot, table, idx, rows, width, *sems):
    for u in range(STEP):
        pool.indirect_dma_start(out=rows[:, slot, u, 0:width], out_offset=None, in_=table,
                                in_offset=bass.IndirectOffsetOnAxis(ap=idx[:, slot, u:u + 1], axis=0)
                                ).then_inc(sems[u * len(sems) // STEP], 16)


def sum_phase(nc, io, g, dram, tag, table, extra):
    with ExitStack() as stack:
        m = Memory(nc, stack, tag)
        idx = m.sb("idx", [P, 2, STEP], U32)
        rows = m.sb("rows", [P, 2, STEP, FEAT])
        run = m.sb("run", [P, 2, STEP + 1, FEAT])
        s_idx = [m.sem(f"idx{h}") for h in range(2)]
        s_rows = [m.sem(f"rows{h}") for h in range(2)]
        s_out = [m.sem(f"out{h}") for h in range(2)]
        s_scan, s_carry, s_pass = m.sem("scanned"), m.sem("carried"), m.sem("passed")
        work = extra(nc, m, io, g, dram)
        block = stack.enter_context(nc.Block())
        store = dram["run_sum"].rearrange("(p j) f -> p j f", p=P)
        SC = FEAT // 8

        @block.sync
        def _(sp):
            for h in range(2):
                sp.sem_inc(s_out[h], 16)
                sp.dma_start(idx[:, h, :], io["src"][:, h * STEP:(h + 1) * STEP]).then_inc(s_idx[h], 16)
            with sp.Fori(0, CHUNKS // 2) as c:
                for h in range(2):
                    ch = 2 * c + h
                    sp.wait_ge(s_scan, (ch + 3) * SC)
                    sp.dma_start(store[:, ds(ch * STEP, STEP), :], run[:, h, 1:STEP + 1, :]).then_inc(s_out[h], 16)
                    sp.dma_start(idx[:, h, :], io["src"][:, ds((ch + 2) * STEP, STEP)]).then_inc(s_idx[h], 16)
            for h in range(2):
                sp.wait_ge(s_out[h], 16 + 16 * (CHUNKS // 2))
                sp.wait_ge(s_idx[h], 16 + 16 * (CHUNKS // 2))

        @block.gpsimd
        def _(pool):
            with pool.Fori(0, CHUNKS // 2) as c:
                for h in range(2):
                    pool.wait_ge(s_idx[h], (c + 1) * 16)
                    pool.sem_inc(s_pass, 1)
                    pool.wait_ge(s_scan, (2 * c + h + 1) * SC)
                    pool.sem_inc(s_pass, 1)
                    gather_chunk(pool, nc, h, table, idx, rows, FEAT, s_rows[h])

        @block.vector
        def _(dve):
            dve.sem_inc(s_scan, 2 * SC)
            nc.vector.memset(run[:, 1, STEP, :], 0.0).then_inc(s_carry, 1)
            work["dve_first"](dve)
            with dve.Fori(0, CHUNKS // 2) as c:
                for h in range(2):
                    ch = 2 * c + h
                    work["dve"](dve, ch)
                    dve.wait_ge(s_out[h], (c + 1) * 16)
                    dve.wait_ge(s_scan, (ch + 2) * SC)
                    dve.wait_ge(s_carry, ch + 1)
                    nc.vector.tensor_copy(run[:, h, 0, :], run[:, 1 - h, STEP, :]).then_inc(s_carry, 1)
                    dve.wait_ge(s_carry, ch + 2)
                    dve.wait_ge(s_rows[h], (c + 1) * 16 * STEP)
                    dve.sem_inc(s_pass, 1)
                    with dve.Fori(0, SC) as k:
                        for u in range(8):
                            f = k * 8 + u
                            last = scan(nc, run[:, h, :, :], rows[:, h, :, :], g["keep"][:, ds(ch * STEP, STEP)],
                                        f, FEAT, FEAT, ALU.mult, ALU.add)
                        last.then_inc(s_scan, 1)
            work["dve_last"](dve)

        @block.scalar
        def _(act):
            work["act"](act)

        @block.tensor
        def _(pe):
            work["pe"](pe)


def scan(nc, run, data, keep, f, rw, dw, op0, op1, df=None):
    flat = run.rearrange("p j f -> p (j f)")
    dflat = data.rearrange("p j f -> p (j f)")
    df = f if df is None else df
    return nc.vector.tensor_tensor_scan(out=flat[:, ds(f + rw, STEP, rw)], data0=keep,
                                        data1=dflat[:, ds(df, STEP, dw)], initial=flat[:, ds(f, 1)],
                                        op0=op0, op1=op1)


def first_extra(nc, m, io, g, dram):
    hist = dict(oh_hi=m.sb("oh_hi", [P, 2, HI, GRP], BF16), oh_lo=m.sb("oh_lo", [P, 2, P, GRP], BF16),
                iota=g["iota"], hi=m.sb("hi", [P, COLS], BF16), lo=m.sb("lo", [P, COLS], BF16), count=m.ps("count", [P, 512]),
                own=GRP)
    dst = m.sb("dst", [P, COLS], I32)
    before = m.sb("before", [P, 1], I32)
    beforef = m.sb("beforef", [P, 1])
    dstf = m.sb("dstf", [P, COLS])
    first = m.sb("first", [P, COLS])
    part = m.sb("part", [P, COLS], I32)
    zero = m.sb("zero", [P, P], BF16)
    zeros = m.sb("zeros", [P, STEP, QROW])
    counts = m.sb("counts", [P, P])
    s_dst, s_dve, s_zero, s_zeros = m.sem("dst_in"), m.sem("dve"), m.sem("zero"), m.sem("zeroed")
    s_made, s_used, s_all, s_counts = m.sem("onehots_made"), m.sem("onehots_used"), m.sem("count_done"), m.sem("counts")
    s_store = m.sem("counts_out")

    def dve_first(dve):
        step = stepper(dve, s_dve)
        dve.sem_inc(s_used, 2)
        nc.vector.memset(zero[:, :], 0.0).then_inc(s_zero, 1)
        nc.vector.memset(zeros[:, :, :], 0.0).then_inc(s_zero, 1)
        nc.vector.memset(before[:, :], -1).then_inc(s_zero, 1)
        dve.wait_ge(s_dst, 32)
        step(nc.vector.tensor_copy(dstf[:, :], dst[:, :]))
        step(nc.vector.tensor_copy(beforef[:, :], before[:, :]))
        step(nc.vector.tensor_tensor(g["keep"][:, 1:COLS], dstf[:, 1:COLS], dstf[:, 0:COLS - 1], ALU.is_equal))
        step(nc.vector.tensor_tensor(g["keep"][:, 0:1], dstf[:, 0:1], beforef[:, :], ALU.is_equal))
        step(nc.vector.tensor_scalar(first[:, :], dstf[:, :], dstf[:, 0:1], None, ALU.is_equal))
        step(nc.vector.reduce_sum(beforef[:, :], first[:, :], axis=AX.X))
        step(nc.vector.tensor_scalar(g["through"][:, :], beforef[:, :], float(COLS), None, ALU.is_equal))
        step(nc.vector.tensor_tensor(g["through"][:, :], g["through"][:, :], g["keep"][:, 0:1], ALU.mult))
        step(nc.vector.tensor_tensor(beforef[:, :], beforef[:, :], g["edge0"][:, :], ALU.add))
        step(nc.vector.tensor_copy(g["fixrow"][:, :], beforef[:, :]))
        step(nc.vector.tensor_copy(g["dst0"][:, :], dstf[:, 0:1]))
        split_number(step, nc, dst[:, :], part, hist)

    def dve_chunk(dve, ch):
        for k in range(GPC):
            onehot_rows(dve, nc, ch, k, hist, s_made, s_used)

    def dve_last(dve):
        dve.wait_ge(s_all, 1)
        nc.vector.tensor_copy(counts[0:HI, :], hist["count"][0:HI, 0:P]).then_inc(s_counts, 1)

    def act(act):
        act.dma_start(dst[:, :], io["dst"]).then_inc(s_dst, 16)
        act.wait_ge(s_zero, 3)
        act.dma_start(before[1:P, :], io["dst"][0:P - 1, COLS - 1:COLS],
                      allow_slow_non_contiguous=True).then_inc(s_dst, 16)
        zero_row = zeros[:, :, :].rearrange("p j f -> p (j f)").unsqueeze(1)
        act.dma_start(dram["at_dst1"][0:EPAD, :].rearrange("(p c j) f -> p c (j f)", p=P, j=STEP),
                      zero_row[:, :, 0:STEP * HEADS].to_broadcast([P, CHUNKS, STEP * HEADS])
                      ).then_inc(s_zeros, 16)
        with act.Fori(0, CHUNKS) as ch:
            act.wait_ge(s_used, (ch + 1) * GPC + 2)
            act.dma_start(dram["at_dst3"][0:EPAD, :].rearrange("(p j) f -> p j f", p=P)[:, ds(ch * STEP, STEP), :],
                          zeros[:, :, :]).then_inc(s_zeros, 16)
        act.wait_ge(s_counts, 1)
        act.dma_start(dram["count_dst"].rearrange("(h l) -> h l", l=P), counts[0:HI, :]).then_inc(s_store, 16)
        act.wait_ge(s_store, 16)
        act.wait_ge(s_zeros, 16 * (CHUNKS + 1))

    def pe(pe):
        pe.wait_ge(s_zero, 1)
        nc.tensor.matmul(hist["count"][0:HI, 0:P], zero[:, 0:HI], zero[:, :], start=True, stop=False,
                         skip_group_check=True)
        with pe.Fori(0, CHUNKS) as ch:
            for k in range(GPC):
                onehot_products(pe, nc, ch, k, hist, s_made, s_used)
        nc.tensor.matmul(hist["count"][0:HI, 0:P], zero[:, 0:HI], zero[:, :], start=False, stop=True,
                         skip_group_check=True).then_inc(s_all, 1)

    return dict(dve_first=dve_first, dve=dve_chunk, dve_last=dve_last, act=act, pe=pe)



def segments_phase(nc, io, g, dram):
    with ExitStack() as stack:
        m = Memory(nc, stack, "segments")
        deg = m.sb("deg", [P, BLKS])
        upto = m.sb("upto", [P, BLKS])
        total = m.ps("total", [P, 512])
        one = m.sb("one", [P, BLKS])
        t = m.sb("t", [P, BLKS])
        s_deg, s_dve, s_pe, s_act = m.sem("deg_in"), m.sem("dve"), m.sem("pe"), m.sem("act")
        block = stack.enter_context(nc.Block())

        @block.sync
        def _(sp):
            sp.dma_start(deg[:, :], dram["count_dst"].rearrange("(p b) -> p b", p=P)).then_inc(s_deg, 16)

        @block.gpsimd
        def _(pool):
            pass

        @block.vector
        def _(dve):
            step = stepper(dve, s_dve)
            step(nc.vector.memset(one[:, :], 1.0))
            dve.wait_ge(s_deg, 16)
            step(nc.vector.tensor_tensor_scan(out=upto[:, :], data0=one[:, :], data1=deg[:, :], initial=0.0,
                                              op0=ALU.mult, op1=ALU.add))
            dve.wait_ge(s_pe, 1)
            step(nc.vector.tensor_tensor(upto[:, :], upto[:, :], total[:, 0:1].to_broadcast([P, BLKS]), ALU.add))
            step(nc.vector.tensor_scalar(t[:, :], upto[:, :], -1.0, 0.0, ALU.add, ALU.max))
            step(nc.vector.tensor_copy(g["lastrow"][:, :], t[:, :]))
            step(nc.vector.tensor_scalar(g["has"][:, :], deg[:, :], 1.0, None, ALU.min))
            step(nc.vector.tensor_tensor(upto[:, :], upto[:, :], deg[:, :], ALU.subtract))
            step(nc.vector.tensor_tensor(upto[:, :], upto[:, :], g["has"][:, :], ALU.mult))
            step(nc.vector.tensor_scalar(t[:, :], g["nodenum"][:, :], float(EPAD), None, ALU.add))
            step(nc.vector.tensor_scalar(one[:, :], g["has"][:, :], -1.0, 1.0, ALU.mult, ALU.add))
            step(nc.vector.tensor_tensor(t[:, :], t[:, :], one[:, :], ALU.mult))
            step(nc.vector.tensor_tensor(t[:, :], t[:, :], upto[:, :], ALU.add))
            step(nc.vector.tensor_copy(g["firstrow"][:, :], t[:, :]))
            step(nc.vector.tensor_scalar(deg[:, :], deg[:, :], 1.0, None, ALU.max))
            dve.wait_ge(s_act, 1)
            step(nc.vector.reciprocal(g["root_in"][:, :], g["root_in"][:, :]))
            step(nc.vector.tensor_tensor(g["root_in"][:, :], g["root_in"][:, :], g["has"][:, :], ALU.mult))

        @block.scalar
        def _(act):
            act.wait_ge(s_dve, 14)
            nc.scalar.activation(g["root_in"][:, :], deg[:, :], ACT.Sqrt).then_inc(s_act, 1)

        @block.tensor
        def _(pe):
            pe.wait_ge(s_dve, 2)
            nc.tensor.matmul(total[:, 0:1], g["below"][:, :], upto[:, BLKS - 1:BLKS],
                             start=True, stop=True).then_inc(s_pe, 1)



def carry_phase(nc, g, dram, tag, softmax):
    table = dram["run_softmax" if softmax else "run_sum"]
    width = SROW if softmax else FEAT
    sums = SUMS if softmax else FEAT
    with ExitStack() as stack:
        m = Memory(nc, stack, tag)
        end = m.sb("end", [P, width])
        row = m.sb("row", [P, width])
        both = m.sb("both", [P, 3, sums])
        flip = m.sb("flip", [sums, 3, P])
        state = m.sb("state", [sums, P + 1])
        peak = m.sb("peak", [sums, P + 1])
        fac = m.sb("fac", [sums, 2, P])
        back = m.sb("back", [P, 2, sums])
        rpk = m.sb("rpk", [P, sums])
        efac = m.sb("efac", [P, 2, sums])
        ps = m.ps("ps", [P, 512])
        s_end, s_row, s_dve, s_pe, s_act, s_fixed = (m.sem("end_in"), m.sem("row_in"), m.sem("dve"), m.sem("pe"),
                                                     m.sem("act"), m.sem("fixed"))
        s_turned, s_ready, s_exp, s_mend = m.sem("turned"), m.sem("ready"), m.sem("exp"), m.sem("mend")
        block = stack.enter_context(nc.Block())
        np_ = 3 if softmax else 2
        planes = [0, 1, 2] if softmax else [0, 2]

        def widen(step, out, maxima):
            step(nc.vector.tensor_copy(out[:, 0:FEAT].rearrange("p (h d) -> p h d", d=HDIM), bc(maxima, HDIM)))
            step(nc.vector.tensor_copy(out[:, FEAT:SUMS], maxima))

        @block.sync
        def _(sp):
            sp.dma_start(end[:, :], table.rearrange("(p j) f -> p j f", p=P)[:, COLS - 1, :]).then_inc(s_end, 16)

        @block.gpsimd
        def _(pool):
            pool.indirect_dma_start(out=row[:, :], out_offset=None, in_=table[:, :],
                                    in_offset=bass.IndirectOffsetOnAxis(ap=g["fixrow"][:, :], axis=0)
                                    ).then_inc(s_row, 16)
            pool.wait_ge(s_mend, 1)
            pool.indirect_dma_start(out=table[:, :], out_offset=bass.IndirectOffsetOnAxis(ap=g["fixrow"][:, :], axis=0),
                                    in_=row[:, :], in_offset=None).then_inc(s_fixed, 16)
            pool.wait_ge(s_fixed, 16)

        @block.vector
        def _(dve):
            step = stepper(dve, s_dve)
            step(nc.vector.memset(state[:, :], 0.0))
            step(nc.vector.memset(peak[:, :], 0.0))
            step(nc.vector.tensor_copy(both[:, 2, :], g["through"][:, :].to_broadcast([P, sums])))
            dve.wait_ge(s_end, 16)
            step(nc.vector.tensor_copy(both[:, 0, :], end[:, 0:sums]))
            if softmax:
                widen(step, both[:, 1, :], end[:, SUMS:SROW])
            nc.vector.tensor_copy(rpk[:, 0:1], both[:, 0, 0:1]).then_inc(s_ready, 1)
            dve.wait_ge(s_turned, 1)
            step(nc.vector.tensor_copy(flip[:, 0:np_, :], ps[0:sums, 0:np_ * P].rearrange("f (n p) -> f n p", n=np_)))
            through = flip[:, np_ - 1, :]
            if softmax:
                step(nc.vector.tensor_scalar(fac[:, 0, :], through, BIG, -BIG, ALU.mult, ALU.add))
                step(nc.vector.tensor_tensor_scan(out=peak[:, 1:P + 1], data0=fac[:, 0, :], data1=flip[:, 1, :],
                                                  initial=0.0, op0=ALU.add, op1=ALU.max))
                step(nc.vector.tensor_tensor(fac[:, 0, :], peak[:, 0:P], peak[:, 1:P + 1], ALU.subtract))
                step(nc.vector.tensor_scalar(fac[:, 0, :], fac[:, 0, :], 0.0, None, ALU.min))
                step(nc.vector.tensor_tensor(fac[:, 1, :], flip[:, 1, :], peak[:, 1:P + 1], ALU.subtract))
                nc.vector.tensor_scalar(fac[:, 1, :], fac[:, 1, :], 0.0, None, ALU.min).then_inc(s_exp, 1)
                dve.wait_ge(s_act, 1)
                step(nc.vector.tensor_tensor(fac[:, 0, :], fac[:, 0, :], through, ALU.mult))
                step(nc.vector.tensor_tensor(fac[:, 1, :], fac[:, 1, :], flip[:, 0, :], ALU.mult))
                step(nc.vector.tensor_tensor_scan(out=state[:, 1:P + 1], data0=fac[:, 0, :], data1=fac[:, 1, :],
                                                  initial=0.0, op0=ALU.mult, op1=ALU.add))
            else:
                step(nc.vector.tensor_tensor_scan(out=state[:, 1:P + 1], data0=through, data1=flip[:, 0, :],
                                                  initial=0.0, op0=ALU.mult, op1=ALU.add))
            nc.vector.tensor_copy(rpk[:, 0:1], both[:, 0, 0:1]).then_inc(s_ready, 1)
            dve.wait_ge(s_turned, 2)
            dve.wait_ge(s_row, 16)
            if softmax:
                step(nc.vector.tensor_copy(back[:, :, :], ps[:, 0:2 * sums].rearrange("p (n f) -> p n f", n=2)))
                widen(step, rpk, row[:, SUMS:SROW])
                step(nc.vector.tensor_scalar(end[:, 0:1], g["keep"][:, 0:1], BIG, -BIG, ALU.mult, ALU.add))
                step(nc.vector.tensor_scalar(back[:, 1, :], back[:, 1, :], end[:, 0:1], None, ALU.add))
                step(nc.vector.tensor_tensor(efac[:, 1, :], back[:, 1, :], rpk[:, :], ALU.max))
                step(nc.vector.tensor_tensor(efac[:, 0, :], rpk[:, :], efac[:, 1, :], ALU.subtract))
                nc.vector.tensor_tensor(efac[:, 1, :], back[:, 1, :], efac[:, 1, :], ALU.subtract).then_inc(s_exp, 1)
                dve.wait_ge(s_act, 2)
                step(nc.vector.tensor_tensor(row[:, 0:sums], row[:, 0:sums], efac[:, 0, :], ALU.mult))
                step(nc.vector.tensor_tensor(back[:, 0, :], back[:, 0, :], efac[:, 1, :], ALU.mult))
                nc.vector.tensor_tensor(row[:, 0:sums], row[:, 0:sums], back[:, 0, :], ALU.add).then_inc(s_mend, 1)
            else:
                nc.vector.scalar_tensor_tensor(out=row[:, :], in0=ps[:, 0:FEAT], scalar=g["keep"][:, 0:1],
                                               in1=row[:, :], op0=ALU.mult, op1=ALU.add).then_inc(s_mend, 1)

        @block.scalar
        def _(act):
            if softmax:
                act.wait_ge(s_exp, 1)
                nc.scalar.activation(fac[:, :, :], fac[:, :, :], ACT.Exp).then_inc(s_act, 1)
                act.wait_ge(s_exp, 2)
                nc.scalar.activation(efac[:, :, :], efac[:, :, :], ACT.Exp).then_inc(s_act, 1)

        @block.tensor
        def _(pe):
            pe.wait_ge(s_ready, 1)
            for n, plane in enumerate(planes):
                last = nc.tensor.transpose(ps[0:sums, n * P:(n + 1) * P], both[:, plane, :], g["ident"][:, :])
            last.then_inc(s_turned, 1)
            pe.wait_ge(s_ready, 2)
            for n, what in enumerate([state, peak] if softmax else [state]):
                last = nc.tensor.transpose(ps[:, n * sums:(n + 1) * sums], what[:, 0:P], g["ident"][0:sums, 0:sums])
            last.then_inc(s_turned, 1)



def blocks_of(part):
    return slice(part * PBLK, (part + 1) * PBLK)


def gather_nodes(pool, g, table, acc, sems):
    for b in range(BLKS):
        pool.indirect_dma_start(out=acc[:, b, :], out_offset=None, in_=table[:, :],
                                in_offset=bass.IndirectOffsetOnAxis(ap=g["lastrow"][:, b:b + 1], axis=0)
                                ).then_inc(sems[b // PBLK], 16)


def scatter_nodes(pool, g, table, rows, ready, sem):
    for b in range(BLKS):
        if b % PBLK == 0:
            pool.wait_ge(ready, b // PBLK + 1)
        pool.indirect_dma_start(out=table[:, :], out_offset=bass.IndirectOffsetOnAxis(ap=g["firstrow"][:, b:b + 1], axis=0),
                                in_=rows[:, b, :], in_offset=None).then_inc(sem, 16)


def halves(part):
    return [slice(part * PBLK, part * PBLK + PPAIR), slice(part * PBLK + PPAIR, (part + 1) * PBLK)]


class Norm:

    def __init__(self, nc, m, g, name, x, sq, stat):
        self.nc, self.g, self.x, self.sq, self.stat = nc, g, x, sq, stat
        self.s_diff, self.s_sq, self.s_var, self.s_std = (m.sem(name + n) for n in ("diff", "sq", "var", "std"))

    def dve(self, dve, step, part, ready=None):
        v = self.nc.vector
        for bl in halves(part):
            x, mean = self.x[:, bl, :], self.stat[:, 0, bl]
            step(v.reduce_sum(mean, x, axis=AX.X))
            step(v.tensor_scalar(mean, mean, 1.0 / FEAT, None, ALU.mult))
            v.tensor_tensor(x, x, bc(mean, FEAT), ALU.subtract).then_inc(self.s_diff, 1)
        for n, bl in enumerate(halves(part)):
            dve.wait_ge(self.s_sq, 2 * part + n + 1)
            v.reduce_sum(self.stat[:, 1, bl], self.sq[:, bl, 0:FEAT], axis=AX.X).then_inc(self.s_var, 1)
        for n, bl in enumerate(halves(part)):
            x, var = self.x[:, bl, :], self.stat[:, 1, bl]
            dve.wait_ge(self.s_std, 2 * part + n + 1)
            step(v.reciprocal(var, var))
            last = v.tensor_tensor(x, x, bc(var, FEAT), ALU.mult)
            if ready is None or n == 0:
                step(last)
            else:
                last.then_inc(ready, 1)

    def act(self, act, part):
        for n, bl in enumerate(halves(part)):
            act.wait_ge(self.s_diff, 2 * part + n + 1)
            self.nc.scalar.activation(self.sq[:, bl, 0:FEAT], self.x[:, bl, :], ACT.Square).then_inc(self.s_sq, 1)
        for n, bl in enumerate(halves(part)):
            act.wait_ge(self.s_var, 2 * part + n + 1)
            self.nc.scalar.activation(self.stat[:, 1, bl], self.stat[:, 1, bl], ACT.Sqrt, scale=1.0 / FEAT,
                                      bias=self.g["eps"][:, :]).then_inc(self.s_std, 1)


class NodeProduct:

    def __init__(self, nc, m, g, name, x, w, width, finish, banks=None):
        self.nc, self.g, self.x, self.w, self.width, self.finish = nc, g, x, w, width, finish
        self.turned, self.out, self.xt = banks or (m.ps("turned", [P, 2, 512]), m.ps("out", [P, 4, 512]),
                                                   m.sb("xt", [P, 2, 4, P]))
        self.s_turn, self.s_xt, self.s_mm, self.s_done = (m.sem(name + n) for n in ("turn", "xt", "mm", "done"))
        self.groups = [(part * PPAIR + k, min(4, PPAIR - k)) for part in range(PARTS) for k in (0, 4)]

    def pe(self, pe, part):
        for n in (2 * part, 2 * part + 1):
            if n >= 2:
                pe.wait_ge(self.s_xt, n - 1)
            k0, count = self.groups[n]
            for k in range(count):
                last = self.nc.tensor.transpose(self.turned[:, n % 2, k * P:(k + 1) * P],
                                                self.x[:, 2 * (k0 + k):2 * (k0 + k) + 2, :].rearrange("p b f -> p (b f)"),
                                                self.g["ident"][:, :])
            last.then_inc(self.s_turn, 1)
        for n in (2 * part, 2 * part + 1):
            pe.wait_ge(self.s_xt, n + 1)
            k0, count = self.groups[n]
            for k in range(count):
                pair = k0 + k
                if pair >= 4:
                    pe.wait_ge(self.s_done, pair - 3)
                self.nc.tensor.matmul(self.out[:, pair % 4, 0:2 * self.width], self.xt[:, n % 2, k, :],
                                      self.w[:, :], start=True, stop=True).then_inc(self.s_mm, 1)

    def act(self, act, part):
        for n in (2 * part, 2 * part + 1):
            k0, count = self.groups[n]
            act.wait_ge(self.s_turn, n + 1)
            if n >= 2:
                act.wait_ge(self.s_mm, self.groups[n - 1][0])
            self.nc.scalar.activation(self.xt[:, n % 2, 0:count, :],
                                      self.turned[:, n % 2, 0:count * P].rearrange("p (k n) -> p k n", k=count),
                                      ACT.Copy).then_inc(self.s_xt, 1)

    def dve(self, dve, part):
        for pair in range(part * PPAIR, (part + 1) * PPAIR):
            dve.wait_ge(self.s_mm, pair + 1)
            self.finish(pair, self.out[:, pair % 4, 0:2 * self.width].rearrange("p (b f) -> p b f", b=2)
                        ).then_inc(self.s_done, 1)
        dve.wait_ge(self.s_done, (part + 1) * PPAIR)


def node_view(ap):
    return ap.rearrange("(p b) f -> p b f", p=P)



ATT = FEAT + 2 * HEADS


def first_nodes_phase(nc, io, g, dram):
    with ExitStack() as stack:
        m = Memory(nc, stack, "nodes1")
        x = m.sb("x", [P, BLKS, FEAT])
        acc = m.sb("acc", [P, BLKS, FEAT])
        stat = m.sb("stat", [P, 2, BLKS])
        tab = m.sb("tab", [P, BLKS, ATT])
        at = m.sb("at", [P, BLKS, HEADS])
        w = m.sb("w", [P, 2 * ATT])
        wt = m.sb("wt", [FEAT, P])
        attn = m.sb("attn", [FEAT, 2 * HEADS])
        small = m.ps("small", [P, 512])
        s_w, s_x, s_dve = m.sem("w_in"), m.sem("x_in"), m.sem("dve")
        norm = Norm(nc, m, g, "", x, acc, stat)
        s_acc = [m.sem(f"acc_in{k}") for k in range(PARTS)]
        s_small, s_ready, s_at, s_out, s_spread = (m.sem("small"), m.sem("ready"), m.sem("at"), m.sem("out"),
                                                   m.sem("spread"))
        prod = NodeProduct(nc, m, g, "", x, w, ATT,
                           lambda k, ps: nc.vector.tensor_copy(tab[:, 2 * k:2 * k + 2, :], ps))
        block = stack.enter_context(nc.Block())

        @block.sync
        def _(sp):
            sp.dma_start(w[:, :], io["w_node"]).then_inc(s_w, 16)
            sp.dma_start(wt[:, :], io["w_node_t"]).then_inc(s_w, 16)
            sp.dma_start(attn[:, :], io["attn"]).then_inc(s_w, 16)
            sp.dma_start(x[:, :, :], node_view(io["x"])).then_inc(s_x, 16)
            for part in range(PARTS):
                sp.wait_ge(s_at, part + 1)
                for name, tile in (("x1", x), ("table1", tab)):
                    sp.dma_start(node_view(dram[name])[:, blocks_of(part), :], tile[:, blocks_of(part), :]).then_inc(s_out, 16)
            sp.wait_ge(s_out, 32 * PARTS)

        @block.gpsimd
        def _(pool):
            gather_nodes(pool, g, dram["run_sum"], acc, s_acc)
            scatter_nodes(pool, g, dram["at_dst1"], at, s_at, s_spread)
            pool.wait_ge(s_spread, 16 * BLKS)

        @block.vector
        def _(dve):
            step = stepper(dve, s_dve)
            dve.wait_ge(s_w, 48)
            dve.wait_ge(s_small, 1)
            step(nc.vector.tensor_copy(w[0:FEAT, FEAT:ATT], small[0:FEAT, 0:2 * HEADS]))
            step(nc.vector.tensor_copy(w[FEAT:P, ATT + FEAT:2 * ATT], small[FEAT:P, 0:2 * HEADS]))
            dve.wait_ge(s_x, 16)
            for part in range(PARTS + 1):
                if part < PARTS:
                    bl = blocks_of(part)
                    xp, ap = x[:, bl, :], acc[:, bl, :]
                    dve.wait_ge(s_acc[part], 16 * PBLK)
                    step(nc.vector.tensor_tensor(ap, ap, bc(g["root_in"][:, bl], FEAT), ALU.mult))
                    step(nc.vector.tensor_tensor(xp, xp, ap, ALU.add))
                    norm.dve(dve, step, part, s_ready)
                if part >= 1:
                    prod.dve(dve, part - 1)
                    bl = blocks_of(part - 1)
                    nc.vector.tensor_copy(at[:, bl, :], tab[:, bl, FEAT + HEADS:ATT]).then_inc(s_at, 1)

        @block.scalar
        def _(act):
            for part in range(PARTS):
                norm.act(act, part)
                prod.act(act, part)

        @block.tensor
        def _(pe):
            pe.wait_ge(s_w, 48)
            nc.tensor.matmul(small[:, 0:2 * HEADS], wt[:, :], attn[:, :], start=True, stop=True).then_inc(s_small, 1)
            for part in range(PARTS):
                pe.wait_ge(s_ready, part + 1)
                prod.pe(pe, part)



def every_chunk(eng, body):
    with eng.Fori(0, CHUNKS // 2 - 1) as c:
        for h in range(2):
            body(c, h, False)
    for h in range(2):
        body(CHUNKS // 2 - 1, h, True)


def softmax_scans(dve, nc, run, fall, grow, data, s_scan):
    for head in range(HEADS):
        factor = fall.rearrange("p j h -> p (j h)")[:, ds(head, STEP, HEADS)]
        with dve.Fori(0, 2) as k:
            for u in range(HDIM // 2):
                scan(nc, run, data, factor, head * HDIM + k * (HDIM // 2) + u, SROW, data.shape[2],
                     ALU.mult, ALU.add)
        last = scan(nc, run, grow, factor, FEAT + head, SROW, HEADS, ALU.mult, ALU.add, df=head)
    last.then_inc(s_scan, 1)


def attention_phase(nc, io, g, dram):
    with ExitStack() as stack:
        m = Memory(nc, stack, "edges2")
        idx = m.sb("idx", [P, 2, STEP], U32)
        rows = m.sb("rows", [P, 2, STEP, ATT])
        run = m.sb("run", [P, 2, STEP + 1, SROW])
        at = m.sb("at", [P, 2, STEP + 1, HEADS])
        start = m.sb("start", [P, ATT])
        attr = m.sb("attr", [P, 2, STEP // 8, P])
        w_edge = m.sb("w_edge", [P, 8 * HEADS])
        delta = m.sb("delta", [P, 2, STEP, HEADS])
        score = m.ps("score", [P, 2, 512])
        s_idx, s_rows, s_out, s_attr, s_at = ([m.sem(f"{n}{h}") for h in range(2)]
                                              for n in ("idx", "rows", "out", "attr", "at"))
        s_start, s_w, s_scan, s_dve, s_pass = m.sem("start"), m.sem("w"), m.sem("scanned"), m.sem("dve"), m.sem("passed")
        s_score, s_read, s_exp, s_expd = m.sem("score"), m.sem("score_read"), m.sem("to_exp"), m.sem("exp_done")
        block = stack.enter_context(nc.Block())
        store = dram["run_softmax"].rearrange("(p j) f -> p j f", p=P)
        spread = dram["at_dst1"][0:EPAD, :].rearrange("(p j) f -> p j f", p=P)
        STEPS = 11

        @block.sync
        def _(sp):
            sp.dma_start(w_edge[:, :], io["w_edge"]).then_inc(s_w, 16)
            for h in range(2):
                sp.sem_inc(s_out[h], 16)
                sp.dma_start(idx[:, h, :], io["src"][:, h * STEP:(h + 1) * STEP]).then_inc(s_idx[h], 16)
                sp.dma_start(attr[:, h, :, :], io["e16"][:, h * 8:(h + 1) * 8, :]).then_inc(s_attr[h], 16)

            def chunk(c, h, last):
                ch = 2 * c + h
                sp.wait_ge(s_scan, ch + 3)
                sp.dma_start(store[:, ds(ch * STEP, STEP), :], run[:, h, 1:STEP + 1, :]).then_inc(s_out[h], 16)
                if not last:
                    sp.dma_start(idx[:, h, :], io["src"][:, ds((ch + 2) * STEP, STEP)]).then_inc(s_idx[h], 16)
                    sp.dma_start(attr[:, h, :, :], io["e16"][:, ds((ch + 2) * 8, 8), :]).then_inc(s_attr[h], 16)

            every_chunk(sp, chunk)
            for h in range(2):
                sp.wait_ge(s_out[h], 16 + 16 * (CHUNKS // 2))

        @block.gpsimd
        def _(pool):
            pool.indirect_dma_start(out=start[:, :], out_offset=None, in_=dram["table1"],
                                    in_offset=bass.IndirectOffsetOnAxis(ap=g["dst0"][:, :], axis=0)
                                    ).then_inc(s_start, 16)
            with pool.Fori(0, CHUNKS // 2) as c:
                for h in range(2):
                    pool.wait_ge(s_idx[h], (c + 1) * 16)
                    pool.sem_inc(s_pass, 1)
                    pool.wait_ge(s_scan, 2 * c + h + 1)
                    pool.sem_inc(s_pass, 1)
                    gather_chunk(pool, nc, h, dram["table1"], idx, rows, ATT, s_rows[h])

        @block.vector
        def _(dve):
            dve.sem_inc(s_scan, 2)
            dve.sem_inc(s_read, 2)
            head = stepper(dve, s_dve)
            head(nc.vector.memset(run[:, 1, STEP, :], 0.0))
            dve.wait_ge(s_start, 16)
            head(nc.vector.tensor_copy(at[:, 1, STEP, :], start[:, FEAT + HEADS:ATT]))

            def chunk(c, h):
                ch = 2 * c + h
                step = stepper(dve, s_dve, 2 + ch * STEPS)
                keep = g["keep"][:, ds(ch * STEP, STEP)]
                fall, grow = delta[:, 0, :, :], delta[:, 1, :, :]
                dve.wait_ge(s_out[h], (c + 1) * 16)
                dve.wait_ge(s_scan, ch + 2)
                step(nc.vector.tensor_copy(run[:, h, 0, :], run[:, 1 - h, STEP, :]))
                step(nc.vector.tensor_copy(at[:, h, 0, :], at[:, 1 - h, STEP, :]))
                dve.wait_ge(s_at[h], (c + 1) * 16)
                for k in range(HEADS):
                    last = scan(nc, at[:, h, :, :], at[:, h, 1:STEP + 1, :], keep, k, HEADS, HEADS, ALU.mult, ALU.add)
                step(last)
                dve.wait_ge(s_rows[h], (c + 1) * 16 * STEP)
                step(nc.vector.tensor_tensor(fall, rows[:, h, :, FEAT:FEAT + HEADS], at[:, h, 1:STEP + 1, :], ALU.add))
                dve.wait_ge(s_score, ch + 1)
                nc.vector.tensor_tensor(fall, score[:, h, 0:STEP * HEADS].rearrange("p (j h) -> p j h", h=HEADS),
                                        fall, ALU.add).then_inc(s_read, 1)
                dve.wait_ge(s_read, ch + 3)
                step(nc.vector.scalar_tensor_tensor(out=grow, in0=fall, scalar=0.2, in1=fall, op0=ALU.mult, op1=ALU.max))
                step(nc.vector.tensor_scalar(fall, fall, 0.0, None, ALU.max))
                for k in range(HEADS):
                    last = scan(nc, run[:, h, :, :], fall, keep, SUMS + k, SROW, HEADS, ALU.mult, ALU.max, df=k)
                step(last)
                step(nc.vector.tensor_tensor(fall, run[:, h, 0:STEP, SUMS:SROW], run[:, h, 1:STEP + 1, SUMS:SROW],
                                             ALU.subtract))
                step(nc.vector.tensor_scalar(fall, fall, 0.0, None, ALU.min))
                nc.vector.tensor_tensor(grow, grow, run[:, h, 1:STEP + 1, SUMS:SROW], ALU.subtract).then_inc(s_exp, 1)
                dve.wait_ge(s_expd, ch + 1)
                step(nc.vector.tensor_tensor(fall, fall, bc(keep, HEADS), ALU.mult))
                h4 = rows[:, h, :, 0:FEAT].rearrange("p j (h d) -> p j h d", d=HDIM)
                step(nc.vector.tensor_tensor(h4, h4, bc(grow, HDIM), ALU.mult))
                assert step.count[0] == STEPS
                dve.sem_inc(s_pass, 1)
                softmax_scans(dve, nc, run[:, h, :, :], fall, grow, rows[:, h, :, :], s_scan)

            with dve.Fori(0, CHUNKS // 2) as c:
                for h in range(2):
                    chunk(c, h)

        @block.scalar
        def _(act):
            act.dma_start(at[:, 0, 1:STEP + 1, :], spread[:, 0:STEP, :]).then_inc(s_at[0], 16)

            def chunk(c, h, last):
                ch = 2 * c + h
                act.wait_ge(s_exp, ch + 1)
                nc.scalar.activation(delta[:, :, :, :], delta[:, :, :, :], ACT.Exp).then_inc(s_expd, 1)
                if not (last and h == 1):
                    act.dma_start(at[:, 1 - h, 1:STEP + 1, :], spread[:, ds((ch + 1) * STEP, STEP), :]
                                  ).then_inc(s_at[1 - h], 16)

            every_chunk(act, chunk)

        @block.tensor
        def _(pe):
            pe.wait_ge(s_w, 16)
            with pe.Fori(0, CHUNKS // 2) as c:
                for h in range(2):
                    pe.wait_ge(s_attr[h], (c + 1) * 16)
                    pe.wait_ge(s_read, 2 * c + h + 1)
                    for k in range(8):
                        last = nc.tensor.matmul(score[:, h, k * 8 * HEADS:(k + 1) * 8 * HEADS], attr[:, h, k, :],
                                                w_edge[:, :], start=True, stop=True)
                    last.then_inc(s_score, 1)


def attention_nodes_phase(nc, io, g, dram):
    with ExitStack() as stack:
        m = Memory(nc, stack, "nodes2")
        x = m.sb("x", [P, BLKS, FEAT])
        acc = m.sb("acc", [P, BLKS, SROW])
        y = m.sb("y", [P, BLKS, FEAT])
        hn = m.sb("h", [P, BLKS, ATT])
        inv = m.sb("inv", [P, BLKS, HEADS])
        stat = m.sb("stat", [P, 2, BLKS])
        gamma, beta = m.sb("gamma", [P, FEAT]), m.sb("beta", [P, FEAT])
        s_in, s_dve, s_x, s_out = (m.sem(n) for n in ("in", "dve", "x", "out"))
        s_acc = [m.sem(f"acc_in{k}") for k in range(PARTS)]
        inner, outer = Norm(nc, m, g, "i", y, acc, stat), Norm(nc, m, g, "o", x, acc, stat)
        block = stack.enter_context(nc.Block())

        @block.sync
        def _(sp):
            sp.dma_start(x[:, :, :], node_view(dram["x1"])).then_inc(s_in, 16)
            sp.dma_start(hn[:, :, :], node_view(dram["table1"])).then_inc(s_in, 16)
            sp.dma_start(gamma[:, :], io["ln_gamma"]).then_inc(s_in, 16)
            sp.dma_start(beta[:, :], io["ln_beta"]).then_inc(s_in, 16)
            for part in range(PARTS):
                sp.wait_ge(s_x, part + 1)
                sp.dma_start(node_view(dram["x2"])[:, blocks_of(part), :], x[:, blocks_of(part), :]).then_inc(s_out, 16)
            sp.wait_ge(s_out, 16 * PARTS)

        @block.gpsimd
        def _(pool):
            gather_nodes(pool, g, dram["run_softmax"], acc, s_acc)

        @block.vector
        def _(dve):
            step = stepper(dve, s_dve)
            dve.wait_ge(s_in, 64)
            step(nc.vector.tensor_tensor(x[:, :, :], x[:, :, :], over_blocks(beta), ALU.add))
            for part in range(PARTS):
                bl = blocks_of(part)
                xp, yp, ap, ip = x[:, bl, :], y[:, bl, :], acc[:, bl, :], inv[:, bl, :]
                dve.wait_ge(s_acc[part], 16 * PBLK)
                step(nc.vector.tensor_scalar(ip, ap[:, :, FEAT:SUMS], 1e-8, None, ALU.add))
                step(nc.vector.reciprocal(ip, ip))
                step(nc.vector.tensor_tensor(ip, ip, bc(g["has"][:, bl], HEADS), ALU.mult))
                step(nc.vector.tensor_tensor(yp.rearrange("p b (h d) -> p b h d", d=HDIM),
                                             ap[:, :, 0:FEAT].rearrange("p b (h d) -> p b h d", d=HDIM),
                                             bc(ip, HDIM), ALU.mult))
                step(nc.vector.tensor_tensor(yp, yp, hn[:, bl, 0:FEAT], ALU.add))
                inner.dve(dve, step, part)
                step(nc.vector.tensor_tensor(yp, yp, over_blocks(gamma, PBLK), ALU.mult))
                step(nc.vector.tensor_tensor(xp, xp, yp, ALU.add))
                outer.dve(dve, step, part, s_x)

        @block.scalar
        def _(act):
            for part in range(PARTS):
                inner.act(act, part)
                outer.act(act, part)


def over_blocks(v, blocks=BLKS):
    return v[:, :].unsqueeze(1).to_broadcast([P, blocks, FEAT])



def network_extra(nc, m, io, g, dram):
    CP = STEP // 2
    SUBS = CP // 4
    attr = m.sb("attr", [P, 2, CP, P])
    out = m.sb("weight", [P, 2, CP, P])
    hid = [m.sb(f"hid{i}", [P, 2, 512]) for i in range(2)]
    w = [m.sb(f"fc{i}", [P, P]) for i in range(3)]
    bias = m.sb("bias", [P, 3])
    pre = [m.ps(f"pre{i}", [P, 2, 512]) for i in range(3)]
    s_w = m.sem("w")
    s_attr, s_out = ([m.sem(f"{n}{h}") for h in range(2)] for n in ("attr_in", "weight_out"))
    s_mm = [m.sem(f"mm{i}") for i in range(3)]
    s_act = [m.sem(f"act{i}") for i in range(3)]

    def act(act):
        for i in range(3):
            act.dma_start(w[i][:, :], io[f"fc{i + 1}"]).then_inc(s_w, 16)
        act.dma_start(bias[:, :], io["bfc"]).then_inc(s_w, 16)
        for h in range(2):
            act.dma_start(attr[:, h, :, :], io["e64"][:, h * CP:(h + 1) * CP, :]).then_inc(s_attr[h], 16)
            act.sem_inc(s_out[h], 16)
        for i in range(3):
            act.sem_inc(s_act[i], 2)
        act.wait_ge(s_w, 64)

        def chunk(c, h, last):
            ch = 2 * c + h
            flat = out[:, h, :, :].rearrange("p k n -> p (k n)")
            for q in range(SUBS + 2):
                if q < SUBS:
                    act.wait_ge(s_mm[0], ch * SUBS + q + 1)
                    act.wait_ge(s_mm[1], ch * SUBS + q + 1)
                    nc.scalar.activation(hid[0][:, q % 2, :], pre[0][:, q % 2, :], ACT.Silu, bias=bias[:, 0:1]
                                         ).then_inc(s_act[0], 1)
                if 1 <= q <= SUBS:
                    r = q - 1
                    act.wait_ge(s_mm[1], ch * SUBS + r + 3)
                    act.wait_ge(s_mm[2], ch * SUBS + r + 1)
                    nc.scalar.activation(hid[1][:, r % 2, :], pre[1][:, r % 2, :], ACT.Silu, bias=bias[:, 1:2]
                                         ).then_inc(s_act[1], 1)
                if q >= 2:
                    r = q - 2
                    if r == 0:
                        act.wait_ge(s_out[h], 16 * (c + 1))
                    act.wait_ge(s_mm[2], ch * SUBS + r + 3)
                    nc.scalar.activation(flat[:, r * 512:(r + 1) * 512], pre[2][:, r % 2, :], ACT.Identity,
                                         bias=bias[:, 2:3]).then_inc(s_act[2], 1)
            act.wait_ge(s_act[2], (ch + 1) * SUBS + 2)
            act.dma_start(dram["weight3"][:, ds(ch * CP, CP), :], out[:, h, :, :]).then_inc(s_out[h], 16)
            if not last:
                act.dma_start(attr[:, h, :, :], io["e64"][:, ds((ch + 2) * CP, CP), :]).then_inc(s_attr[h], 16)

        every_chunk(act, chunk)
        for h in range(2):
            act.wait_ge(s_out[h], 16 + 16 * (CHUNKS // 2))

    def pe(pe):
        for i in (1, 2):
            pe.sem_inc(s_mm[i], 2)
        pe.wait_ge(s_w, 64)
        with pe.Fori(0, CHUNKS // 2) as c:
            for h in range(2):
                ch = 2 * c + h
                pe.wait_ge(s_attr[h], (c + 1) * 16)
                flat = attr[:, h, :, :].rearrange("p k n -> p (k n)")
                for q in range(SUBS + 2):
                    if q < SUBS:
                        pe.wait_ge(s_act[0], ch * SUBS + q + 1)
                        nc.tensor.matmul(pre[0][:, q % 2, :], w[0][:, :], flat[:, q * 512:(q + 1) * 512],
                                         start=True, stop=True).then_inc(s_mm[0], 1)
                    if 1 <= q <= SUBS:
                        r = q - 1
                        pe.wait_ge(s_act[0], ch * SUBS + r + 3)
                        pe.wait_ge(s_act[1], ch * SUBS + r + 1)
                        nc.tensor.matmul(pre[1][:, r % 2, :], w[1][:, :], hid[0][:, r % 2, :],
                                         start=True, stop=True).then_inc(s_mm[1], 1)
                    if q >= 2:
                        r = q - 2
                        pe.wait_ge(s_act[1], ch * SUBS + r + 3)
                        pe.wait_ge(s_act[2], ch * SUBS + r + 1)
                        nc.tensor.matmul(pre[2][:, r % 2, :], w[2][:, :], hid[1][:, r % 2, :],
                                         start=True, stop=True).then_inc(s_mm[2], 1)

    return dict(dve_first=lambda dve: None, dve=lambda dve, ch: None, dve_last=lambda dve: None, act=act, pe=pe)



QALL = QROW + FEAT


def batchnorm_phase(nc, io, g, dram):
    with ExitStack() as stack:
        m = Memory(nc, stack, "nodes3")
        x = m.sb("x", [P, BLKS, FEAT])
        acc = m.sb("acc", [P, BLKS, FEAT])
        y = m.sb("y", [P, BLKS, FEAT])
        tab = m.sb("tab", [P, BLKS, QALL])
        stat = m.sb("stat", [P, 2, BLKS])
        w, b = m.sb("w", [P, P]), m.sb("b", [P, FEAT])
        w3, b3, bk = m.sb("w3", [P, 6 * FEAT]), m.sb("b3", [P, 3 * FEAT]), m.sb("bk", [P, FEAT])
        gamma, beta, mean, std, shift = (m.sb(n, [P, FEAT]) for n in ("gamma", "beta", "mean", "std", "shift"))
        real = m.sb("real", [P, P])
        total = m.ps("total", [P, 2, 512])
        s_in, s_dve, s_x, s_out = (m.sem(n) for n in ("in", "dve", "x", "out"))
        s_sum, s_first, s_y, s_tot, s_shift, s_mean, s_square, s_bstd, s_tab, s_spread = (
            m.sem(n) for n in ("sum", "first", "y", "total", "shift", "mean", "square", "bstd", "tab", "spread"))
        norm = Norm(nc, m, g, "n", x, y, stat)
        s_acc = [m.sem(f"acc_in{k}") for k in range(PARTS)]
        prod = NodeProduct(nc, m, g, "y", acc, w, FEAT,
                           lambda k, ps: nc.vector.tensor_tensor(y[:, 2 * k:2 * k + 2, :], ps, over_blocks(b, 2), ALU.add))

        def finish(k, ps):
            bias = b3[:, :].unsqueeze(1).to_broadcast([P, 2, 3 * FEAT])
            nc.vector.tensor_tensor(tab[:, 2 * k:2 * k + 2, 0:2 * FEAT], ps[:, :, 0:2 * FEAT], bias[:, :, 0:2 * FEAT], ALU.add)
            return nc.vector.tensor_tensor(tab[:, 2 * k:2 * k + 2, QROW:QALL], ps[:, :, 2 * FEAT:], bias[:, :, 2 * FEAT:], ALU.add)

        prod3 = NodeProduct(nc, m, g, "q", x, w3, 3 * FEAT, finish, (prod.turned, prod.out, prod.xt))
        starts = sorted(set(range(0, REAL, PPAIR)) | set(range(REAL, BLKS, PPAIR)) | {REAL})
        runs = list(zip(starts, starts[1:] + [BLKS]))
        block = stack.enter_context(nc.Block())

        def total_of(what, part, half):
            for b0, b1 in runs:
                if (b1 - 1) // PBLK == part:
                    last = nc.tensor.matmul(total[:, half, 0:(b1 - b0) * FEAT], g["ones"][:, :] if b0 < REAL else real[:, :],
                                            what[:, b0:b1, :].rearrange("p b f -> p (b f)"),
                                            start=b0 == 0, stop=b1 == BLKS, skip_group_check=True)
            return last

        def by_feature(half):
            return total[:, half, 0:PPAIR * FEAT].rearrange("p (b f) -> p f b", f=FEAT)

        @block.sync
        def _(sp):
            sp.dma_start(x[:, :, :], node_view(dram["x2"])).then_inc(s_in, 16)
            for tile, name in ((w, "w2"), (b, "b2"), (gamma, "gamma2"), (beta, "beta2"), (w3, "w3"), (b3, "b3"), (bk, "bk")):
                sp.dma_start(tile[:, :], io[name]).then_inc(s_in, 16)
            for part in range(PARTS):
                bl = blocks_of(part)
                sp.wait_ge(s_tab, part + 1)
                for name, rows in (("x3", x[:, bl, :]), ("quer3", tab[:, bl, 0:QROW]), ("table3", tab[:, bl, QROW:QALL])):
                    sp.dma_start(node_view(dram[name])[:, bl, :], rows).then_inc(s_out, 16)
            sp.wait_ge(s_out, 48 * PARTS)

        @block.gpsimd
        def _(pool):
            gather_nodes(pool, g, dram["run_sum"], acc, s_acc)
            scatter_nodes(pool, g, dram["at_dst3"], tab[:, :, 0:QROW], s_tab, s_spread)
            pool.wait_ge(s_spread, 16 * BLKS)

        @block.vector
        def _(dve):
            step = stepper(dve, s_dve)
            step(nc.vector.tensor_scalar(real[:, :], g["ident"][:, P - 1:P].to_broadcast([P, P]), -1.0, 1.0, ALU.mult, ALU.add))
            dve.wait_ge(s_in, 128)
            for part in range(PARTS + 1):
                if part < PARTS:
                    bl = blocks_of(part)
                    dve.wait_ge(s_acc[part], 16 * PBLK)
                    step(nc.vector.tensor_tensor(acc[:, bl, :], acc[:, bl, :], bc(g["has"][:, bl], FEAT), ALU.mult))
                    nc.vector.tensor_tensor(acc[:, bl, :], acc[:, bl, :], x[:, bl, :], ALU.add).then_inc(s_sum, 1)
                if part >= 1:
                    prod.dve(dve, part - 1)
                if part == 1:
                    dve.sem_inc(s_first, 1)
                    dve.wait_ge(s_shift, 1)
                    step(nc.vector.reduce_sum(shift[:, :], by_feature(1), axis=AX.X))
                    step(nc.vector.tensor_scalar(shift[:, :], shift[:, :], 1.0 / (PPAIR * P), None, ALU.mult))
                    step(nc.vector.tensor_tensor(b[:, :], b[:, :], shift[:, :], ALU.subtract))
                    step(nc.vector.tensor_tensor(y[:, 0:PBLK, :], y[:, 0:PBLK, :], over_blocks(shift, PBLK), ALU.subtract))
                if part >= 1:
                    dve.sem_inc(s_y, 1)
            dve.wait_ge(s_tot, 1)
            step(nc.vector.reduce_sum(mean[:, :], by_feature(0), axis=AX.X))
            step(nc.vector.tensor_scalar(mean[:, :], mean[:, :], 1.0 / NODES, None, ALU.mult))
            step(nc.vector.tensor_tensor(shift[:, :], mean[:, :], mean[:, :], ALU.mult))
            dve.wait_ge(s_tot, 2)
            step(nc.vector.reduce_sum(std[:, :], by_feature(1), axis=AX.X))
            step(nc.vector.scalar_tensor_tensor(out=std[:, :], in0=std[:, :], scalar=1.0 / NODES, in1=shift[:, :],
                                                op0=ALU.mult, op1=ALU.subtract))
            nc.vector.tensor_scalar(std[:, :], std[:, :], 0.0, None, ALU.max).then_inc(s_mean, 1)
            dve.wait_ge(s_bstd, 1)
            step(nc.vector.reciprocal(std[:, :], std[:, :]))
            step(nc.vector.tensor_tensor(std[:, :], std[:, :], gamma[:, :], ALU.mult))
            step(nc.vector.tensor_tensor(mean[:, :], mean[:, :], std[:, :], ALU.mult))
            step(nc.vector.tensor_tensor(beta[:, :], beta[:, :], mean[:, :], ALU.subtract))
            for part in range(PARTS + 1):
                if part < PARTS:
                    bl = blocks_of(part)
                    xp, yp = x[:, bl, :], y[:, bl, :]
                    step(nc.vector.tensor_tensor(yp, yp, over_blocks(std, PBLK), ALU.mult))
                    step(nc.vector.tensor_tensor(yp, yp, over_blocks(beta, PBLK), ALU.add))
                    step(nc.vector.scalar_tensor_tensor(out=xp, in0=yp, scalar=0.0, in1=xp, op0=ALU.max, op1=ALU.add))
                    norm.dve(dve, step, part, s_x)
                if part >= 1:
                    prod3.dve(dve, part - 1)
                    bl = blocks_of(part - 1)
                    q, tmp = tab[:, bl, 0:FEAT], acc[:, bl, :]
                    step(nc.vector.tensor_scalar(q, q, float(HDIM) ** -0.5, None, ALU.mult))
                    step(nc.vector.tensor_tensor(tmp, q, over_blocks(bk, PBLK), ALU.mult))
                    nc.vector.reduce_sum(tab[:, bl, 2 * FEAT:QROW], tmp.rearrange("p b (h d) -> p b h d", d=HDIM),
                                         axis=AX.X).then_inc(s_tab, 1)

        @block.scalar
        def _(act):
            for part in range(PARTS + 1):
                if part < PARTS:
                    prod.act(act, part)
                if part >= 1:
                    bl = blocks_of(part - 1)
                    act.wait_ge(s_y, part)
                    nc.scalar.activation(acc[:, bl, :], y[:, bl, :], ACT.Square).then_inc(s_square, 1)
            act.wait_ge(s_mean, 1)
            nc.scalar.activation(std[:, :], std[:, :], ACT.Sqrt, bias=g["eps"][:, :]).then_inc(s_bstd, 1)
            for part in range(PARTS):
                norm.act(act, part)
                prod3.act(act, part)

        @block.tensor
        def _(pe):
            for part in range(PARTS + 1):
                if part < PARTS:
                    pe.wait_ge(s_sum, part + 1)
                    prod.pe(pe, part)
                if part == 0:
                    pe.wait_ge(s_first, 1)
                    nc.tensor.matmul(total[:, 1, 0:PPAIR * FEAT], g["ones"][:, :],
                                     y[:, 0:PPAIR, :].rearrange("p b f -> p (b f)"),
                                     start=True, stop=True, skip_group_check=True).then_inc(s_shift, 1)
                else:
                    pe.wait_ge(s_y, part)
                    tot = total_of(y, part - 1, 0)
                    pe.wait_ge(s_square, part)
                    squares = total_of(acc, part - 1, 1)
            tot.then_inc(s_tot, 1)
            squares.then_inc(s_tot, 1)
            for part in range(PARTS):
                pe.wait_ge(s_x, part + 1)
                prod3.pe(pe, part)



def transformer_phase(nc, io, g, dram):
    CP = STEP // 2
    GROUPS = CP // 4
    PIECES = 4
    PCOLS = STEP // PIECES
    with ExitStack() as stack:
        m = Memory(nc, stack, "edges4")
        idx = m.sb("idx", [P, 2, STEP], U32)
        rows = m.sb("rows", [P, 2, STEP, FEAT])
        run = m.sb("run", [P, 2, STEP + 1, SROW])
        at = m.sb("at", [P, 2, STEP + 1, QROW])
        start = m.sb("start", [P, QROW])
        weight = m.sb("weight", [P, 2, CP, P])
        ea = m.sb("ea", [P, COLS])
        w_kv = m.sb("w_kv", [P, 4 * FEAT])
        cut = m.sb("cut", [P, STEP])
        delta = m.sb("delta", [P, 2, 2, STEP, HEADS])
        times = m.sb("times", [P, STEP, HEADS])
        turned = m.ps("turned", [P, 2, 512])
        keys = m.ps("keys", [P, 2, 512])
        values = m.ps("values", [P, 2, 512])
        s_idx, s_out, s_at, s_wt = ([m.sem(f"{n}{h}") for h in range(2)] for n in ("idx", "out", "at", "weight"))
        s_rows = [[m.sem(f"rows{h}{n}") for n in range(PIECES)] for h in range(2)]
        (s_w, s_start, s_scan, s_dve, s_pass, s_near, s_turn, s_tp, s_mm, s_k, s_v, s_alpha, s_exp, s_expd) = (
            m.sem(n) for n in ("w", "start", "scanned", "dve", "passed", "near", "turned", "times", "mm", "k_read",
                               "v_read", "alpha", "to_exp", "exp_done"))
        block = stack.enter_context(nc.Block())
        store = dram["run_softmax"].rearrange("(p j) f -> p j f", p=P)
        spread = dram["at_dst3"][0:EPAD, :].rearrange("(p j) f -> p j f", p=P)
        STEPS = 13
        SPREAD = 25

        @block.sync
        def _(sp):
            def load_idx(ch, h):
                sp.dma_start(idx[:, h, :], io["src"][:, ds(ch * STEP, STEP)]).then_inc(s_idx[h], 16)

            def load_weight(ch, h):
                sp.dma_start(weight[:, h, :, :], dram["weight3"][:, ds(ch * CP, CP), :]).then_inc(s_wt[h], 16)

            for h in range(2):
                sp.sem_inc(s_out[h], 16)
                load_idx(h, h)
            sp.dma_start(ea[:, :], io["ea"]).then_inc(s_w, 16)
            sp.dma_start(w_kv[:, :], io["w_kv"]).then_inc(s_w, 16)
            for h in range(2):
                load_weight(h, h)

            def chunk(c, h, last):
                ch = 2 * c + h
                if not last:
                    sp.wait_ge(s_turn, (ch + 3) * GROUPS)
                    load_idx(ch + 2, h)
                    sp.wait_ge(s_mm, (ch + 1) * GROUPS)
                    load_weight(ch + 2, h)
                sp.wait_ge(s_scan, ch + 2)
                sp.dma_start(store[:, ds(ch * STEP, STEP), :], run[:, h, 1:STEP + 1, :]).then_inc(s_out[h], 16)

            every_chunk(sp, chunk)
            for h in range(2):
                sp.wait_ge(s_out[h], 16 + 16 * (CHUNKS // 2))

        @block.gpsimd
        def _(pool):
            pool.indirect_dma_start(out=start[:, :], out_offset=None, in_=dram["quer3"],
                                    in_offset=bass.IndirectOffsetOnAxis(ap=g["dst0"][:, :], axis=0)
                                    ).then_inc(s_start, 16)
            with pool.Fori(0, CHUNKS // 2) as c:
                for h in range(2):
                    pool.wait_ge(s_idx[h], (c + 1) * 16)
                    pool.sem_inc(s_pass, 1)
                    pool.wait_ge(s_turn, (2 * c + h + 1) * GROUPS)
                    pool.sem_inc(s_pass, 1)
                    gather_chunk(pool, nc, h, dram["table3"], idx, rows, FEAT, *s_rows[h])

        @block.vector
        def _(dve):
            dve.sem_inc(s_k, 2)
            dve.sem_inc(s_tp, 2)
            head = stepper(dve, s_dve)
            head(nc.vector.memset(delta[:, :, :, :, :], 0.0))
            head(nc.vector.memset(run[:, :, :, :], 0.0))
            head(nc.vector.memset(run[:, 1, STEP, SUMS:SROW], -BIG))
            dve.wait_ge(s_start, 16)
            dve.wait_ge(s_w, 32)

            def spread_scans(ch, h, first, count):
                order = [*range(FEAT, 2 * FEAT), *range(FEAT), *range(2 * FEAT, QROW)]
                for n in range(first, first + count):
                    last = scan(nc, at[:, h, :, :], at[:, h, 1:STEP + 1, :], g["keep"][:, ds(ch * STEP, STEP)],
                                order[n], QROW, QROW, ALU.mult, ALU.add)
                    if n == FEAT - 1:
                        last.then_inc(s_near, 1)
                return last

            def sum_scans(h, head):
                factor = delta[:, h, 0, :, :].rearrange("p j h -> p (j h)")[:, ds(head, STEP, HEADS)]
                data = run[:, h, 1:STEP + 1, :]
                for f in range(head * HDIM, (head + 1) * HDIM):
                    scan(nc, run[:, h, :, :], data, factor, f, SROW, SROW, ALU.mult, ALU.add)
                return scan(nc, run[:, h, :, :], delta[:, h, 1, :, :], factor, FEAT + head, SROW, HEADS,
                            ALU.mult, ALU.add, df=head)

            head(nc.vector.tensor_copy(at[:, 0, 0, :], start[:, :]))
            dve.wait_ge(s_at[0], 16)
            head(spread_scans(0, 0, 0, QROW))

            def chunk(c, h, end):
                ch = 2 * c + h
                step = stepper(dve, s_dve, 5 + ch * STEPS)
                keep = g["keep"][:, ds(ch * STEP, STEP)]
                fall, grow = delta[:, h, 0, :, :], delta[:, h, 1, :, :]
                ea4 = bc(ea[:, ds(ch * STEP, STEP)], HEADS)
                q = at[:, h, 1:STEP + 1, 0:FEAT]
                flat = weight[:, h, :, :].rearrange("p k n -> p (k n)")
                more = not (end and h == 1)
                step(nc.vector.tensor_copy(run[:, 1 - h, 0, 0:SUMS], run[:, h, STEP, 0:SUMS]))
                if more:
                    step(nc.vector.tensor_copy(at[:, 1 - h, 0, :], at[:, h, STEP, :]))
                step(nc.vector.tensor_scalar(cut[:, :], keep, BIG, -BIG, ALU.mult, ALU.add))
                dve.wait_ge(s_wt[h], (c + 1) * 16)
                for n in range(GROUPS + 1):
                    if n < GROUPS:
                        dve.wait_ge(s_turn, (ch + 2) * GROUPS + n + 1)
                        nc.vector.tensor_tensor(flat[:, n * 512:(n + 1) * 512], turned[:, n % 2, :],
                                                flat[:, n * 512:(n + 1) * 512], ALU.mult).then_inc(s_tp, 1)
                    if n < HEADS:
                        last = sum_scans(1 - h, n)
                        if n == HEADS - 1:
                            last.then_inc(s_scan, 1)
                    elif more:
                        if n == HEADS:
                            dve.wait_ge(s_at[1 - h], (c + 1 + h) * 16)
                        spread_scans(ch + 1, 1 - h, (n - HEADS) * SPREAD, SPREAD)
                    if n >= 1:
                        i = n - 1
                        dve.wait_ge(s_mm, ch * GROUPS + i + 1)
                        q8 = at[:, h, 1 + 8 * i:9 + 8 * i, 0:FEAT]
                        nc.vector.tensor_tensor(q8, keys[:, i % 2, :].rearrange("p (j f) -> p j f", j=8), q8,
                                                ALU.mult).then_inc(s_k, 1)
                step(nc.vector.tensor_copy(run[:, h, 0, SUMS:SROW], run[:, 1 - h, STEP, SUMS:SROW]))
                dve.wait_ge(s_k, (ch + 1) * GROUPS + 2)
                step(nc.vector.reduce_sum(fall, q.rearrange("p j (h d) -> p j h d", d=HDIM), axis=AX.X))
                step(nc.vector.tensor_tensor(fall, fall, ea4, ALU.mult))
                nc.vector.tensor_tensor(fall, fall, at[:, h, 1:STEP + 1, 2 * FEAT:QROW], ALU.add).then_inc(s_alpha, 1)
                dve.wait_ge(s_alpha, ch + 1)
                dve.wait_ge(s_out[h], (c + 1) * 16)
                for k in range(HEADS):
                    last = scan(nc, run[:, h, :, :], fall, cut[:, :], SUMS + k, SROW, HEADS, ALU.add, ALU.max, df=k)
                step(last)
                peak, before = run[:, h, 1:STEP + 1, SUMS:SROW], run[:, h, 0:STEP, SUMS:SROW]
                step(nc.vector.tensor_tensor(grow, fall, peak, ALU.subtract))
                step(nc.vector.tensor_tensor(fall, before, peak, ALU.subtract))
                nc.vector.tensor_scalar(fall, fall, 0.0, None, ALU.min).then_inc(s_exp, 1)
                if more:
                    done = (GROUPS + 1 - HEADS) * SPREAD
                    step(spread_scans(ch + 1, 1 - h, done, QROW - done))
                dve.wait_ge(s_expd, ch + 1)
                step(nc.vector.tensor_tensor(fall, fall, bc(keep, HEADS), ALU.mult))
                step(nc.vector.tensor_tensor(times[:, :, :], grow, ea4, ALU.mult))
                dve.wait_ge(s_v, (ch + 1) * GROUPS + 2)
                h4 = run[:, h, 1:STEP + 1, 0:FEAT].rearrange("p j (h d) -> p j h d", d=HDIM)
                step(nc.vector.tensor_tensor(h4, h4, bc(times[:, :, :], HDIM), ALU.mult))
                dve.sem_inc(s_pass, 1)
                assert step.count[0] == STEPS or not more, step.count

            every_chunk(dve, chunk)
            tail = stepper(dve, s_dve, 5 + CHUNKS * STEPS - 2)
            tail(nc.vector.tensor_copy(run[:, 1, 0, 0:SUMS], run[:, 0, STEP, 0:SUMS]))
            for head_ in range(HEADS):
                last = sum_scans(1, head_)
            last.then_inc(s_scan, 1)

        @block.scalar
        def _(act):
            act.sem_inc(s_v, 2)
            for h in range(2):
                act.dma_start(at[:, h, 1:STEP + 1, :], spread[:, h * STEP:(h + 1) * STEP, :]).then_inc(s_at[h], 16)

            def chunk(c, h, last):
                ch = 2 * c + h
                act.wait_ge(s_out[h], (c + 1) * 16)
                for i in range(GROUPS):
                    act.wait_ge(s_mm, ch * GROUPS + i + 1)
                    nc.scalar.activation(run[:, h, 1 + 8 * i:9 + 8 * i, 0:FEAT],
                                         values[:, i % 2, :].rearrange("p (j f) -> p j f", j=8),
                                         ACT.Copy).then_inc(s_v, 1)
                if not last:
                    act.wait_ge(s_alpha, ch + 1)
                    act.dma_start(at[:, h, 1:STEP + 1, :], spread[:, ds((ch + 2) * STEP, STEP), :]).then_inc(s_at[h], 16)
                act.wait_ge(s_exp, ch + 1)
                nc.scalar.activation(delta[:, h, :, :, :], delta[:, h, :, :, :], ACT.Exp).then_inc(s_expd, 1)

            every_chunk(act, chunk)

        @block.tensor
        def _(pe):
            pe.sem_inc(s_turn, 2 * GROUPS)
            pe.wait_ge(s_w, 32)
            with pe.Fori(0, CHUNKS // 2) as c:
                for h in range(2):
                    ch = 2 * c + h
                    for n in range(GROUPS + 1):
                        if n < GROUPS:
                            if n % (GROUPS // PIECES) == 0:
                                pe.wait_ge(s_rows[h][n * PIECES // GROUPS], (c + 1) * 16 * PCOLS)
                            if n == 0:
                                pe.wait_ge(s_near, ch + 1)
                            pe.wait_ge(s_tp, ch * GROUPS + n + 1)
                            for k in range(4):
                                j = 2 * (4 * n + k)
                                out = turned[:, n % 2, k * P:(k + 1) * P]
                                nc.tensor.matmul(out, rows[:, h, j:j + 2, :].rearrange("p a f -> p (a f)"), g["ident"][:, :],
                                                 start=True, stop=False, skip_group_check=True)
                                for a in range(2):
                                    last = nc.tensor.matmul(out[a * FEAT:(a + 1) * FEAT, :], at[:, h, 1 + j + a, FEAT:2 * FEAT],
                                                            g["ident"][:, :], start=False, stop=a == 1,
                                                            skip_group_check=True)
                            last.then_inc(s_turn, 1)
                        if n >= 1:
                            pe.wait_ge(s_tp, ch * GROUPS + n + 2)
                            i = n - 1
                            pe.wait_ge(s_k, ch * GROUPS + i + 1)
                            pe.wait_ge(s_v, ch * GROUPS + i + 1)
                            for k in range(4):
                                for bank, part in ((keys, 0), (values, 1)):
                                    last = nc.tensor.matmul(bank[:, i % 2, k * P:(k + 1) * P], weight[:, h, 4 * i + k, :],
                                                            w_kv[:, part * P:(part + 1) * P], start=True, stop=True)
                            last.then_inc(s_mm, 1)


def result_phase(nc, io, g, dram, out):
    with ExitStack() as stack:
        m = Memory(nc, stack, "nodes4")
        x = m.sb("x", [P, BLKS, FEAT])
        acc = m.sb("acc", [P, BLKS, SROW])
        y = m.sb("y", [P, BLKS, FEAT])
        tmp = m.sb("tmp", [P, BLKS, FEAT])
        inv = m.sb("inv", [P, BLKS, HEADS])
        stat = m.sb("stat", [P, 2, BLKS])
        w, b, bv = m.sb("w", [P, P]), m.sb("b", [P, FEAT]), m.sb("bv", [P, FEAT])
        s_in, s_dve, s_x, s_out, s_y = (m.sem(n) for n in ("in", "dve", "x", "out", "y"))
        norm = Norm(nc, m, g, "n", x, acc, stat)
        s_acc = [m.sem(f"acc_in{k}") for k in range(PARTS)]
        prod = NodeProduct(nc, m, g, "", y, w, FEAT,
                           lambda k, ps: nc.vector.tensor_tensor(tmp[:, 2 * k:2 * k + 2, :], ps, over_blocks(b, 2), ALU.add))
        block = stack.enter_context(nc.Block())

        @block.sync
        def _(sp):
            sp.dma_start(x[:, :, :], node_view(dram["x3"])).then_inc(s_in, 16)
            for tile, name in ((w, "w_proj"), (b, "b_proj"), (bv, "bv")):
                sp.dma_start(tile[:, :], io[name]).then_inc(s_in, 16)
            whole = NODES // BLKS
            count = 0
            for part in range(PARTS):
                bl = blocks_of(part)
                sp.wait_ge(s_x, part + 1)
                sp.dma_start(out[0:whole * BLKS, :].rearrange("(p b) f -> p b f", b=BLKS)[:, bl, :], x[0:whole, bl, :]
                             ).then_inc(s_out, 16)
                count += 1
                b0, b1 = bl.start, min(bl.stop, REAL)
                if b0 < b1:
                    sp.dma_start(out[whole * BLKS + b0:whole * BLKS + b1, :].rearrange("(p b) f -> p b f", p=1),
                                 x[whole:whole + 1, b0:b1, :]).then_inc(s_out, 16)
                    count += 1
            sp.wait_ge(s_out, 16 * count)

        @block.gpsimd
        def _(pool):
            gather_nodes(pool, g, dram["run_softmax"], acc, s_acc)

        @block.vector
        def _(dve):
            step = stepper(dve, s_dve)
            heads = lambda t: t.rearrange("p b (h d) -> p b h d", d=HDIM)
            dve.wait_ge(s_in, 64)
            for part in range(PARTS + 1):
                if part < PARTS:
                    bl = blocks_of(part)
                    ip, yp, tp, num, den = inv[:, bl, :], y[:, bl, :], tmp[:, bl, :], acc[:, bl, 0:FEAT], acc[:, bl, FEAT:SUMS]
                    dve.wait_ge(s_acc[part], 16 * PBLK)
                    step(nc.vector.tensor_scalar(ip, den, 1e-16, None, ALU.add))
                    step(nc.vector.reciprocal(ip, ip))
                    step(nc.vector.tensor_tensor(ip, ip, bc(g["has"][:, bl], HEADS), ALU.mult))
                    step(nc.vector.tensor_tensor(heads(yp), heads(num), bc(ip, HDIM), ALU.mult))
                    step(nc.vector.tensor_tensor(ip, ip, den, ALU.mult))
                    step(nc.vector.tensor_copy(tp, over_blocks(bv, PBLK)))
                    step(nc.vector.tensor_tensor(heads(tp), heads(tp), bc(ip, HDIM), ALU.mult))
                    nc.vector.tensor_tensor(yp, yp, tp, ALU.add).then_inc(s_y, 1)
                if part >= 1:
                    prod.dve(dve, part - 1)
                    bl = blocks_of(part - 1)
                    xp = x[:, bl, :]
                    step(nc.vector.tensor_tensor(xp, xp, tmp[:, bl, :], ALU.add))
                    norm.dve(dve, step, part - 1, s_x)

        @block.scalar
        def _(act):
            for part in range(PARTS):
                prod.act(act, part)
                norm.act(act, part)

        @block.tensor
        def _(pe):
            for part in range(PARTS):
                pe.wait_ge(s_y, part + 1)
                prod.pe(pe, part)



def program(nc, io, out):
    dram = {}
    for name, shape in dict(table0=(NPAD, FEAT), table1=(NPAD, ATT), table3=(NPAD, FEAT),
                            quer3=(NPAD, QROW), x1=(NPAD, FEAT), x2=(NPAD, FEAT), x3=(NPAD, FEAT),
                            run_sum=(EPAD, FEAT), run_softmax=(EPAD, SROW),
                            at_dst1=(EPAD + NPAD, HEADS), at_dst3=(EPAD + NPAD, QROW),
                            weight3=(P, COLS // 2, P), count_src=(NPAD,), count_dst=(NPAD,)).items():
        dram[name] = nc.dram_tensor(name, shape, F32, kind="Internal").ap()
    with ExitStack() as stack:
        m = Memory(nc, stack, "g")
        g = dict(iota=m.sb("iota", [P, P, GRP], BF16), rownum=m.sb("rownum", [P, P]), nodenum=m.sb("nodenum", [P, BLKS]),
                 edge0=m.sb("edge0", [P, 1]), eps=m.sb("eps", [P, 1]), ones=m.sb("ones", [P, P]),
                 ident=m.sb("ident", [P, P]), below=m.sb("below", [P, P]),
                 keep=m.sb("keep", [P, COLS]), through=m.sb("through", [P, 1]),
                 fixrow=m.sb("fixrow", [P, 1], U32), dst0=m.sb("dst0", [P, 1], U32),
                 has=m.sb("has", [P, BLKS]), lastrow=m.sb("lastrow", [P, BLKS], U32),
                 firstrow=m.sb("firstrow", [P, BLKS], U32), root_in=m.sb("root_in", [P, BLKS]))
        setup_phase(nc, io, g, dram)
        sum_phase(nc, io, g, dram, "edges1", dram["table0"], first_extra)
        segments_phase(nc, io, g, dram)
        carry_phase(nc, g, dram, "carry1", False)
        first_nodes_phase(nc, io, g, dram)
        attention_phase(nc, io, g, dram)
        carry_phase(nc, g, dram, "carry2", True)
        attention_nodes_phase(nc, io, g, dram)
        sum_phase(nc, io, g, dram, "edges3", dram["x2"], network_extra)
        carry_phase(nc, g, dram, "carry3", False)
        batchnorm_phase(nc, io, g, dram)
        transformer_phase(nc, io, g, dram)
        carry_phase(nc, g, dram, "carry4", True)
        result_phase(nc, io, g, dram, out)


def kernel(**inputs):
    import concourse.bacc as bacc
    from concourse.bass_utils import run_bass_kernel_spmd as run

    v = {k: np.asarray(a) for k, a in inputs.items()}

    def edges(a, cols=COLS, fill=0):
        flat = np.full((EPAD,) + a.shape[1:], fill, a.dtype)
        flat[:EDGES] = a
        wide = np.full((P, cols) + a.shape[1:], fill, a.dtype)
        wide[:, :COLS] = flat.reshape((P, COLS) + a.shape[1:])
        return wide

    def diagonal(a, n):
        k, w = a.shape
        d = np.zeros((n * k, n * w), a.dtype)
        for i in range(n):
            d[i * k:(i + 1) * k, i * w:(i + 1) * w] = a
        return d

    def rows(a):
        return np.ascontiguousarray(np.broadcast_to(a.reshape(1, -1), (P, a.size)))

    x = np.zeros((NPAD, FEAT), v["x"].dtype)
    x[:NODES] = v["x"]
    w_node = np.zeros((FEAT, ATT), np.float32)
    w_node[:, :FEAT] = v["L1_gnn_W_node"]
    attn = np.zeros((FEAT, 2 * HEADS), np.float32)
    for h in range(HEADS):
        attn[h * HDIM:(h + 1) * HDIM, h] = v["L1_gnn_attn_src"][h]
        attn[h * HDIM:(h + 1) * HDIM, HEADS + h] = v["L1_gnn_attn_dst"][h]
    w3 = np.zeros((FEAT, 3 * FEAT), np.float32)
    w3[:, :FEAT], w3[:, FEAT:2 * FEAT], w3[:, 2 * FEAT:] = v["L3_gnn_Wq"], v["L3_gnn_W_dst"], v["L3_gnn_W_src"]
    b3 = np.zeros((3 * FEAT,), np.float32)
    b3[:FEAT], b3[2 * FEAT:] = v["L3_gnn_bq"], v["L3_gnn_b_src"]
    e16 = edges(v["edge_attr_16"]).reshape(P, COLS // 8, 8, EDIM).transpose(2, 3, 1, 0).reshape(P, COLS // 8, P)
    e64 = edges(v["edge_attr_64"]).reshape(P, COLS // 2, 2, FEAT).transpose(2, 3, 1, 0).reshape(P, COLS // 2, P)
    arrays = dict(
        x=x, src=edges(v["src"], COLS + 2 * STEP, NPAD - 1), dst=edges(v["dst"], COLS, NPAD - 1),
        e16=e16, e64=e64, ea=edges(v["edge_weight1"][:, 0]),
        w_node=diagonal(w_node, 2), w_node_t=np.concatenate([v["L1_gnn_W_node"].T] * 2, axis=1), attn=attn,
        w_edge=diagonal(v["L1_gnn_W_edge"], 8), ln_gamma=rows(v["L1_gnn_ln_gamma"]), ln_beta=rows(v["L1_gnn_ln_beta"]),
        w2=diagonal(v["L2_gnn_W"], 2), b2=rows(v["L2_gnn_b"]), gamma2=rows(v["L2_gnn_gamma"]), beta2=rows(v["L2_gnn_beta"]),
        w3=diagonal(w3, 2), b3=rows(b3), bk=rows(v["L3_gnn_b_kv"][:FEAT]), bv=rows(v["L3_gnn_b_kv"][FEAT:]),
        fc1=diagonal(v["L3_gnn_W_fc1"], 2), fc2=diagonal(v["L3_gnn_W_fc2"], 2), fc3=diagonal(v["L3_gnn_W_fc3"], 2),
        bfc=np.stack([np.concatenate([v[f"L3_gnn_b_fc{i}"]] * 2) for i in (1, 2, 3)], axis=1),
        w_kv=np.concatenate([diagonal(v["L3_gnn_W_kv"][:, :FEAT], 2), diagonal(v["L3_gnn_W_kv"][:, FEAT:], 2)], axis=1),
        w_proj=diagonal(v["L3_gnn_W_proj"], 2), b_proj=rows(v["L3_gnn_b_proj"]),
    )
    arrays = {k: np.ascontiguousarray(a) for k, a in arrays.items()}
    nc = bacc.Bacc("TRN2", target_bir_lowering=False, num_devices=1)
    io = {k: nc.dram_tensor(f"in_{k}", a.shape, mybir.dt.from_np(a.dtype), kind="ExternalInput").ap()
          for k, a in arrays.items()}
    io["src"] = io["src"].bitcast(U32)
    out = nc.dram_tensor("out", (NODES, FEAT), F32, kind="ExternalOutput").ap()
    program(nc, io, out)
    r = run(nc, [{f"in_{k}": a for k, a in arrays.items()}], core_ids=[0])
    return r.results[0]["out"]
```
